# Optimizing a Trainium2 kernel written in Bass

```python
import numpy as np
import jax
import jax.numpy as jnp

def _softmax(x, axis=-1):
    return jax.nn.softmax(x, axis=axis)

def _gelu(x):
    return jax.nn.gelu(x, approximate=True)

def _silu(x):
    return jax.nn.silu(x)

def _sigmoid(x):
    return jax.nn.sigmoid(x)

def _layernorm(x, axis=-1, eps=1e-05):
    m = jnp.mean(x, axis=axis, keepdims=True)
    v = jnp.var(x, axis=axis, keepdims=True)
    return (x - m) / jnp.sqrt(v + eps)

def _scatter_add(tgt, idx, src, axis=0):
    return tgt.at[idx].add(src)

def _segment_sum(src, seg, n):
    return jax.ops.segment_sum(src, seg, n)
kernel_name = 'mk_macaron_d1_jaxref_r8_1b28fb'

def setup_inputs(seed: int=0):
    np.random.seed(seed)
    _w = jnp.asarray

    def _L0_attn_setup():
        import jax, jax.numpy as jnp
        import numpy as np
        from jax import lax
        D_MODEL = 128
        D_STATE = 128
        D_CONV = 4
        EXPAND = 2
        HEADDIM = 64
        D_INNER = EXPAND * D_MODEL
        NHEADS = D_INNER // HEADDIM
        CONV_DIM = D_INNER + 2 * D_STATE
        D_IN_PROJ = 2 * D_INNER + 2 * D_STATE + NHEADS
        B_SZ, L_SEQ = (4, 256)
        EPS = 1e-05

        def _mamba_block(x, in_proj_w, conv_w, conv_b, dt_bias, A_log, D, norm_w, out_proj_w, ln_w, ln_b):
            b, l, _ = x.shape
            zxbcdt = jnp.einsum('bld,ed->ble', x, in_proj_w)
            z = zxbcdt[..., :D_INNER]
            xBC = zxbcdt[..., D_INNER:D_INNER + CONV_DIM]
            dt = jax.nn.softplus(zxbcdt[..., D_INNER + CONV_DIM:] + dt_bias)
            xBC_t = xBC.transpose(0, 2, 1)
            conv = lax.conv_general_dilated(xBC_t, conv_w[:, None, :], (1,), [(D_CONV - 1, 0)], feature_group_count=CONV_DIM, dimension_numbers=('NCW', 'OIW', 'NCW'))
            xBC = jax.nn.silu(conv + conv_b[:, None]).transpose(0, 2, 1)
            x_ssm = xBC[..., :D_INNER].reshape(b, l, NHEADS, HEADDIM)
            Bm = xBC[..., D_INNER:D_INNER + D_STATE]
            Cm = xBC[..., D_INNER + D_STATE:]
            A = -jnp.exp(A_log)
            dA = jnp.exp(dt * A)

            def step(h, inp):
                dA_t, x_t, B_t, C_t, dt_t = inp
                dBx = dt_t[:, :, None, None] * x_t[..., None] * B_t[:, None, None, :]
                h = h * dA_t[:, :, None, None] + dBx
                y = jnp.einsum('bhpn,bn->bhp', h, C_t)
                return (h, y)
            h0 = jnp.zeros((b, NHEADS, HEADDIM, D_STATE), dtype=x.dtype)
            inputs = (dA.transpose(1, 0, 2), x_ssm.transpose(1, 0, 2, 3), Bm.transpose(1, 0, 2), Cm.transpose(1, 0, 2), dt.transpose(1, 0, 2))
            _, ys = lax.scan(step, h0, inputs)
            y = ys.transpose(1, 0, 2, 3) + D[None, None, :, None] * x_ssm
            y = y.reshape(b, l, D_INNER)
            y = y * jax.nn.silu(z)
            y = y * lax.rsqrt(jnp.mean(y * y, axis=-1, keepdims=True) + EPS) * norm_w
            y = jnp.einsum('bld,ed->ble', y, out_proj_w) + x
            mu = jnp.mean(y, axis=-1, keepdims=True)
            var = jnp.mean((y - mu) ** 2, axis=-1, keepdims=True)
            return (y - mu) * lax.rsqrt(var + EPS) * ln_w + ln_b
        key = jax.random.key(seed)
        ks = jax.random.split(key, 10)
        x = jax.random.normal(ks[0], (B_SZ, L_SEQ, D_MODEL), dtype=jnp.float32)
        in_proj_w = jax.random.normal(ks[1], (D_IN_PROJ, D_MODEL), dtype=jnp.float32) * 0.02
        conv_w = jax.random.normal(ks[2], (CONV_DIM, D_CONV), dtype=jnp.float32) * 0.2
        conv_b = jax.random.normal(ks[3], (CONV_DIM,), dtype=jnp.float32) * 0.02
        dt_bias = jax.random.normal(ks[4], (NHEADS,), dtype=jnp.float32) * 0.5
        A_log = jnp.log(jax.random.uniform(ks[5], (NHEADS,), minval=1.0, maxval=16.0, dtype=jnp.float32))
        D = 1.0 + 0.1 * jax.random.normal(ks[6], (NHEADS,), dtype=jnp.float32)
        norm_w = jnp.ones((D_INNER,), dtype=jnp.float32)
        out_proj_w = jax.random.normal(ks[7], (D_MODEL, D_INNER), dtype=jnp.float32) * 0.02
        ln_w = jnp.ones((D_MODEL,), dtype=jnp.float32)
        ln_b = jnp.zeros((D_MODEL,), dtype=jnp.float32)
        return {'x': x, 'in_proj_w': in_proj_w, 'conv_w': conv_w, 'conv_b': conv_b, 'dt_bias': dt_bias, 'A_log': A_log, 'D': D, 'norm_w': norm_w, 'out_proj_w': out_proj_w, 'ln_w': ln_w, 'ln_b': ln_b}
    _L0_attn_in = _L0_attn_setup()

    def _L0_ffn_setup():
        import jax, jax.numpy as jnp
        import numpy as np
        TOP_K = 2

        def _moe(x, Wr, br, W1, b1, W2, b2):
            B, S, D = x.shape
            E = Wr.shape[1]
            xt = x.reshape(-1, D)
            logits = xt @ Wr + br
            top_vals, top_idx = jax.lax.top_k(logits, TOP_K)
            mask = jnp.zeros_like(logits, dtype=bool).at[jnp.arange(xt.shape[0])[:, None], top_idx].set(True)
            sparse_logits = jnp.where(mask, logits, -jnp.inf)
            gate = jax.nn.softmax(sparse_logits, axis=-1)
            h = jax.nn.relu(jnp.einsum('td,edh->teh', xt, W1) + b1)
            y = jnp.einsum('teh,ehd->ted', h, W2) + b2
            out = jnp.einsum('ted,te->td', y, gate)
            return out.reshape(B, S, D)
        key = jax.random.key(seed)
        ks = jax.random.split(key, 5)
        B, S, D, E, H = (2, 256, 128, 8, 512)
        scale = 1.0 / np.sqrt(D)
        return {'x': jax.random.normal(ks[0], (B, S, D), dtype=jnp.float32), 'Wr': jax.random.normal(ks[1], (D, E), dtype=jnp.float32) * scale, 'br': jnp.zeros((E,), dtype=jnp.float32), 'W1': jax.random.normal(ks[2], (E, D, H), dtype=jnp.float32) * scale, 'b1': jnp.zeros((E, H), dtype=jnp.float32), 'W2': jax.random.normal(ks[3], (E, H, D), dtype=jnp.float32) * (1.0 / np.sqrt(H)), 'b2': jnp.zeros((E, D), dtype=jnp.float32)}
    _L0_ffn_in = _L0_ffn_setup()
    _d = {'L0_attn_x': _L0_attn_in['x'], 'L0_attn_in_proj_w': _L0_attn_in['in_proj_w'], 'L0_attn_conv_w': _L0_attn_in['conv_w'], 'L0_attn_conv_b': _L0_attn_in['conv_b'], 'L0_attn_dt_bias': _L0_attn_in['dt_bias'], 'L0_attn_A_log': _L0_attn_in['A_log'], 'L0_attn_D': _L0_attn_in['D'], 'L0_attn_norm_w': _L0_attn_in['norm_w'], 'L0_attn_out_proj_w': _L0_attn_in['out_proj_w'], 'L0_attn_ln_w': _L0_attn_in['ln_w'], 'L0_attn_ln_b': _L0_attn_in['ln_b'], 'L0_ffn_Wr': _L0_ffn_in['Wr'], 'L0_ffn_br': _L0_ffn_in['br'], 'L0_ffn_W1': _L0_ffn_in['W1'], 'L0_ffn_b1': _L0_ffn_in['b1'], 'L0_ffn_W2': _L0_ffn_in['W2'], 'L0_ffn_b2': _L0_ffn_in['b2']}
    _x0 = _d['L0_attn_x']
    _d['L0_attn_x'] = jax.random.normal(jax.random.fold_in(jax.random.key(seed), 1), (4, 512, 128), dtype=_x0.dtype)
    del _x0
    return _d

def reference(L0_attn_x, L0_attn_in_proj_w, L0_attn_conv_w, L0_attn_conv_b, L0_attn_dt_bias, L0_attn_A_log, L0_attn_D, L0_attn_norm_w, L0_attn_out_proj_w, L0_attn_ln_w, L0_attn_ln_b, L0_ffn_Wr, L0_ffn_br, L0_ffn_W1, L0_ffn_b1, L0_ffn_W2, L0_ffn_b2):

    def _L0_attn_ref(x, in_proj_w, conv_w, conv_b, dt_bias, A_log, D, norm_w, out_proj_w, ln_w, ln_b):
        import jax, jax.numpy as jnp
        import numpy as np
        from jax import lax
        D_MODEL = 128
        D_STATE = 128
        D_CONV = 4
        EXPAND = 2
        HEADDIM = 64
        D_INNER = EXPAND * D_MODEL
        NHEADS = D_INNER // HEADDIM
        CONV_DIM = D_INNER + 2 * D_STATE
        D_IN_PROJ = 2 * D_INNER + 2 * D_STATE + NHEADS
        B_SZ, L_SEQ = (4, 256)
        EPS = 1e-05

        def _mamba_block(x, in_proj_w, conv_w, conv_b, dt_bias, A_log, D, norm_w, out_proj_w, ln_w, ln_b):
            b, l, _ = x.shape
            zxbcdt = jnp.einsum('bld,ed->ble', x, in_proj_w)
            z = zxbcdt[..., :D_INNER]
            xBC = zxbcdt[..., D_INNER:D_INNER + CONV_DIM]
            dt = jax.nn.softplus(zxbcdt[..., D_INNER + CONV_DIM:] + dt_bias)
            xBC_t = xBC.transpose(0, 2, 1)
            conv = lax.conv_general_dilated(xBC_t, conv_w[:, None, :], (1,), [(D_CONV - 1, 0)], feature_group_count=CONV_DIM, dimension_numbers=('NCW', 'OIW', 'NCW'))
            xBC = jax.nn.silu(conv + conv_b[:, None]).transpose(0, 2, 1)
            x_ssm = xBC[..., :D_INNER].reshape(b, l, NHEADS, HEADDIM)
            Bm = xBC[..., D_INNER:D_INNER + D_STATE]
            Cm = xBC[..., D_INNER + D_STATE:]
            A = -jnp.exp(A_log)
            dA = jnp.exp(dt * A)

            def step(h, inp):
                dA_t, x_t, B_t, C_t, dt_t = inp
                dBx = dt_t[:, :, None, None] * x_t[..., None] * B_t[:, None, None, :]
                h = h * dA_t[:, :, None, None] + dBx
                y = jnp.einsum('bhpn,bn->bhp', h, C_t)
                return (h, y)
            h0 = jnp.zeros((b, NHEADS, HEADDIM, D_STATE), dtype=x.dtype)
            inputs = (dA.transpose(1, 0, 2), x_ssm.transpose(1, 0, 2, 3), Bm.transpose(1, 0, 2), Cm.transpose(1, 0, 2), dt.transpose(1, 0, 2))
            _, ys = lax.scan(step, h0, inputs)
            y = ys.transpose(1, 0, 2, 3) + D[None, None, :, None] * x_ssm
            y = y.reshape(b, l, D_INNER)
            y = y * jax.nn.silu(z)
            y = y * lax.rsqrt(jnp.mean(y * y, axis=-1, keepdims=True) + EPS) * norm_w
            y = jnp.einsum('bld,ed->ble', y, out_proj_w) + x
            mu = jnp.mean(y, axis=-1, keepdims=True)
            var = jnp.mean((y - mu) ** 2, axis=-1, keepdims=True)
            return (y - mu) * lax.rsqrt(var + EPS) * ln_w + ln_b
        return _mamba_block(x, in_proj_w, conv_w, conv_b, dt_bias, A_log, D, norm_w, out_proj_w, ln_w, ln_b)

    def _L0_ffn_ref(x, Wr, br, W1, b1, W2, b2):
        import jax, jax.numpy as jnp
        import numpy as np
        TOP_K = 2

        def _moe(x, Wr, br, W1, b1, W2, b2):
            B, S, D = x.shape
            E = Wr.shape[1]
            xt = x.reshape(-1, D)
            logits = xt @ Wr + br
            top_vals, top_idx = jax.lax.top_k(logits, TOP_K)
            mask = jnp.zeros_like(logits, dtype=bool).at[jnp.arange(xt.shape[0])[:, None], top_idx].set(True)
            sparse_logits = jnp.where(mask, logits, -jnp.inf)
            gate = jax.nn.softmax(sparse_logits, axis=-1)
            h = jax.nn.relu(jnp.einsum('td,edh->teh', xt, W1) + b1)
            y = jnp.einsum('teh,ehd->ted', h, W2) + b2
            out = jnp.einsum('ted,te->td', y, gate)
            return out.reshape(B, S, D)
        return _moe(x, Wr, br, W1, b1, W2, b2)
    x = L0_attn_x
    x = x + 0.5 * _L0_ffn_ref(_layernorm(x, axis=-1), L0_ffn_Wr, L0_ffn_br, L0_ffn_W1, L0_ffn_b1, L0_ffn_W2, L0_ffn_b2)
    x = x + _L0_attn_ref(_layernorm(x, axis=-1), L0_attn_in_proj_w, L0_attn_conv_w, L0_attn_conv_b, L0_attn_dt_bias, L0_attn_A_log, L0_attn_D, L0_attn_norm_w, L0_attn_out_proj_w, L0_attn_ln_w, L0_attn_ln_b)
    x = x + 0.5 * _L0_ffn_ref(_layernorm(x, axis=-1), L0_ffn_Wr, L0_ffn_br, L0_ffn_W1, L0_ffn_b1, L0_ffn_W2, L0_ffn_b2)
    return x

_drawn_inputs = setup_inputs


def setup_inputs(seed=0):
    import zlib

    import numpy as np

    out = dict(_drawn_inputs(seed))
    spreads = {'L0_attn_norm_w': (1.0, 0.2),
     'L0_attn_ln_w': (1.0, 0.2),
     'L0_attn_ln_b': (0.0, 0.1),
     'L0_ffn_br': (0.0, 0.1),
     'L0_ffn_b1': (0.0, 0.1),
     'L0_ffn_b2': (0.0, 0.1)}
    factors = {'L0_attn_dt_bias': 8.0, 'L0_attn_A_log': 8.0, 'L0_attn_D': 4.097}
    for name, (base, spread) in spreads.items():
        noise = np.random.default_rng([zlib.crc32(name.encode()), seed]).standard_normal(out[name].shape)
        drawn = base * np.exp(spread * noise) if base else spread * noise
        out[name] = jnp.asarray(drawn.astype(out[name].dtype))
    for name, factor in factors.items():
        out[name] = (out[name] * factor).astype(out[name].dtype)
    return out
```

```python
import concourse.bass as bass
from concourse import mybir
from contextlib import ExitStack

F32 = mybir.dt.float32
BF16 = mybir.dt.bfloat16
I32 = mybir.dt.int32
U32 = mybir.dt.uint32
ALU = mybir.AluOpType
ACT = mybir.ActivationFunctionType
AX = mybir.AxisListType
ds = bass.ds

P = 128
BATCH, SEQ, D = 4, 512, 128
TOK = BATCH * SEQ
NT = TOK // P
NC = SEQ // P
NE, HID, KTOP = 8, 512, 2
HC = HID // P
NG = KTOP * NT
SLOT_TILES = NG + NE - 1
ST = SLOT_TILES + 1
W1W = HID + HC
INNER, STATE, HEADS, HD, TAPS = 256, 128, 4, 64, 4
CONV = INNER + 2 * STATE
IC = INNER // P
VECS = NE * HC + CONV // P + IC
PAIRS = (SLOT_TILES - 3) // 2
EPS = 1e-5
LEAST_DECAY = -100.0
RSQRT_SEED = float(0x5F3759DF)
Z0, DT0, X0 = 0, INNER, INNER + HEADS
WCOLS = 2 * INNER + 2 * STATE + HEADS


class Steps:

    def __init__(self, engine, sem):
        self.engine, self.sem, self.base, self.n, self.fixed = engine, sem, 0, 0, 0

    def done(self, instruction):
        instruction.then_inc(self.sem, 1)
        self.n += 1

    def settle(self):
        self.engine.wait_ge(self.sem, self.base + self.n)

    def link(self, instruction):
        self.done(instruction)
        self.settle()

    def enter(self, i, per):
        self.fixed = self.base + self.n
        self.base, self.n, self.per = self.fixed + i * per, 0, per

    def leave(self, count):
        assert self.n == self.per, (self.n, self.per)
        self.base, self.n = self.fixed + count * self.per, 0


BLOCKS = (2, 3, 0, 1, 4, 5)


def early(pair):
    return isinstance(pair, int) and pair == 0


def after_tile(pair, u):
    return (pair, 1) if u == 0 else (pair + 1, 0)


def row(tensor, t):
    return tensor[:, ds(t, 1), :].rearrange("p a c -> p (a c)")


def macaron_block(nc, x, in_proj_w, conv_w, conv_b, dt_bias, A_log, D_skip, norm_w, out_proj_w,
                  ln_w, ln_b, Wr, br, W1, b1, W2, b2, out):
    ctx = ExitStack()
    with ctx:
        def sb(name, shape, dt=F32):
            return ctx.enter_context(nc.sbuf_tensor(name, shape, dt))

        def sem(name):
            return ctx.enter_context(nc.semaphore(name))

        X = sb("X", [P, NT, D])
        XN = sb("XN", [P, NT, D])
        XNT = sb("XNT", [P, TOK])
        W1S = sb("W1S", [P, NE, W1W])
        W2S = sb("W2S", [P, NE, HC, D])
        B2S = sb("B2S", [P, NE, D])
        vec_rows = sb("vec_rows", [VECS, P])
        WrS = sb("WrS", [P, NE])
        BrS = sb("BrS", [P, NE])
        in_rows = sb("in_rows", [P, 6, D])
        in_rows_dt = sb("in_rows_dt", [HEADS, D])
        WT = sb("WT", [P, WCOLS])
        out_rows = sb("out_rows", [P, INNER])
        WoT = sb("WoT", [P, IC, D])
        cw = sb("cw", [P, TAPS, TAPS])
        cb = sb("cb", [P, TAPS])
        cwh = sb("cwh", [P, TAPS, TAPS])
        cbh = sb("cbh", [P, TAPS])
        dtb = sb("dtb", [P, HEADS])
        alog = sb("alog", [P, HEADS])
        expA = sb("expA", [P, HEADS])
        Dch = sb("Dch", [P, IC])
        nw = sb("nw", [P, IC])
        diagD = sb("diagD", [P, IC, P])
        lnw = sb("lnw", [P, D])
        lnb = sb("lnb", [P, D])
        ident = sb("ident", [P, P])
        ones = sb("ones", [P, P])
        upto = sb("upto", [P, P])
        after = sb("after", [P, P])
        before_bf = sb("before_bf", [P, P], BF16)
        ones_bf = sb("ones_bf", [P, P], BF16)
        iota_e = sb("iota_e", [P, NE])
        iota_t = sb("iota_t", [P, NT])
        iota_st = sb("iota_st", [P, ST])
        iota_p = sb("iota_p", [P, 1])
        iota_row = sb("iota_row", [P, P], BF16)
        slot_id = sb("slot_id", [P, ST])
        group_val = sb("group_val", [P, NG])
        stats = sb("stats", [P, NT, 6])
        mv = sb("mv", [P, NT, 2])
        rs = sb("rs", [P, NT])
        rt = sb("rt", [P, NT])
        rv = sb("rv", [P, NT])
        lg = sb("lg", [P, NT, NE])
        top = sb("top", [P, NT, 8])
        topi = sb("topi", [P, NT, 8], U32)
        topf = sb("topf", [P, NT, KTOP])
        gate = sb("gate", [P, KTOP, NT])
        gd = sb("gd", [P, NT])
        ge = sb("ge", [P, NT])
        gr = sb("gr", [P, NT])
        pick = sb("pick", [P, KTOP, NT, NE])
        picks_bf = sb("picks_bf", [P, NT * NE], BF16)
        cnt = sb("cnt", [P, NE, NT])
        run = sb("run", [P, NE, NT])
        excl = sb("excl", [P, NE, NT])
        n_e = sb("n_e", [P, NE])
        cmp16 = sb("cmp16", [P, NE, NT])
        tiles_e = sb("tiles_e", [P, NE])
        end_e = sb("end_e", [P, NE])
        adj = sb("adj", [P, NE])
        base = sb("base", [P, NE, NT])
        slot_all = sb("slot_all", [P, NT, NE])
        slot_pick = sb("slot_pick", [P, KTOP, NT, NE])
        slot = sb("slot", [P, NG])
        slot_i = sb("slot_i", [P, NG], I32)
        a_i = sb("a_i", [P, NG], I32)
        b_i = sb("b_i", [P, NG], I32)
        a_f = sb("a_f", [P, NG])
        b_f = sb("b_f", [P, NG])
        val_p = sb("val_p", [P, NG])
        val_g = sb("val_g", [P, NG])
        onehot_a = sb("onehot_a", [P, NG, ST], BF16)
        rhs_ids = sb("rhs_ids", [P, NG, 2, ST], BF16)
        onehot_b = sb("onehot_b", [P, NG, P], BF16)
        ids_f = sb("ids_f", [P, ST])
        rows_out = sb("rows_out", [P, ST], I32)
        rows_in = sb("rows_in", [P, ST], I32)
        te_cmp = sb("te_cmp", [P, ST, NE])
        te_f = sb("te_f", [P, ST])
        te_i = sb("te_i", [P, ST], I32)
        gidx = [sb(f"gidx{u}", [P, 1], I32) for u in range(2)]
        sidx = [sb(f"sidx{u}", [P, 1], I32) for u in range(2)]
        XG = [sb(f"XG{u}", [P, D]) for u in range(2)]
        XT = [sb(f"XT{u}", [P, P]) for u in range(2)]
        W1B = [sb(f"W1B{u}", [P, W1W]) for u in range(2)]
        H = [sb(f"H{u}", [P, HC, P]) for u in range(2)]
        YS = [sb(f"YS{u}", [P, D]) for u in range(2)]
        Y1 = sb("Y1", [P, NT, D])
        Y2 = sb("Y2", [P, NT, D])
        dtr = sb("dtr", [P, NT, HEADS])
        sp = [sb(f"sp{k}", [P, NT, HEADS]) for k in range(5)]
        dt = sb("dt", [P, NT, HEADS])
        la = sb("la", [P, NT, HEADS])
        decay = sb("decay", [P, 3, NT, HEADS])
        dtd = sb("dtd", [P, NT, HEADS])
        acc = [sb(f"acc{k}", [P, SEQ]) for k in range(2)]
        th = [sb(f"th{k}", [P, SEQ]) for k in range(2)]
        conv = [sb(f"conv{k}", [P, SEQ]) for k in range(TAPS)]
        gz = sb("gz", [P, IC, SEQ])
        xdt = [sb(f"xdt{u}", [P, INNER]) for u in range(2)]
        xend = [sb(f"xend{u}", [P, INNER]) for u in range(2)]
        btok = [sb(f"btok{u}", [P, STATE]) for u in range(2)]
        gm = [sb(f"gm{u}", [P, P]) for u in range(2)]
        seg_rhs = [sb(f"seg_rhs{u}", [P, HEADS, P]) for u in range(2)]
        eseg = [sb(f"eseg{u}", [P, HEADS, P]) for u in range(2)]
        mix = [sb(f"mix{u}", [P, HEADS, P]) for u in range(2)]
        S = sb("S", [P, INNER])
        yi = sb("yi", [P, INNER])
        yt = [sb(f"yt{u}", [P, INNER]) for u in range(2)]
        y2T = sb("y2T", [P, NC, IC, P])
        sq = [sb(f"sq{u}", [P, IC, P]) for u in range(2)]
        res = sb("res", [P, NC, D])
        fin = sb("fin", [P, NC, D])

        PS = [ctx.enter_context(nc.psum_tensor(f"PS{i}", [P, 512], F32)) for i in range(8)]

        xn_dram = nc.dram_tensor("xn_rows", [TOK, D], F32, kind="Internal").ap()
        y_dram = nc.dram_tensor("y_rows", [KTOP * TOK + ST * P, D], F32, kind="Internal").ap()

        s_x = [sem(f"s_x{g}") for g in range(BATCH)]
        s_w = sem("s_w")
        s_const = sem("s_const")
        s_prep = sem("s_prep")
        s_w1s = sem("s_w1s")
        s_pool = sem("s_pool")
        s_turn = sem("s_turn")
        s_stats = sem("s_stats")
        s_dve = sem("s_dve")
        s_act = sem("s_act")
        s_xn = sem("s_xn")
        s_xnd = sem("s_xnd")
        s_lnT = sem("s_lnT")
        s_xnt = sem("s_xnt")
        s_small = sem("s_small")
        s_gd = sem("s_gd")
        s_ge = sem("s_ge")
        s_picks = sem("s_picks")
        s_cnt = sem("s_cnt")
        s_ob = sem("s_ob")
        s_bf = sem("s_bf")
        s_ids = sem("s_ids")
        s_idp = sem("s_idp")
        s_te = sem("s_te")
        s_gidx = sem("s_gidx")
        s_sidx = sem("s_sidx")
        s_gath = [sem(f"s_gath{u}") for u in range(2)]
        s_sc = [sem(f"s_sc{u}") for u in range(2)]
        s_xt = sem("s_xt")
        s_xtc = sem("s_xtc")
        s_w1 = sem("s_w1")
        s_upa = sem("s_upa")
        s_upb = sem("s_upb")
        s_ra = sem("s_ra")
        s_rb = sem("s_rb")
        s_y = sem("s_y")
        s_yc = sem("s_yc")
        s_yl = [sem(f"s_yl{g}") for g in range(BATCH)]
        s_comb = sem("s_comb")
        s_out = sem("s_out")
        s_sp = sem("s_sp")
        s_spe = sem("s_spe")
        s_la = sem("s_la")
        s_dec = sem("s_dec")
        s_dece = sem("s_dece")
        s_proj = sem("s_proj")
        s_tap = sem("s_tap")
        s_cv = sem("s_cv")
        s_th = sem("s_th")
        s_act_ch = sem("s_act_ch")
        s_segr = sem("s_segr")
        s_tr = sem("s_tr")
        s_trb = sem("s_trb")
        s_seg = sem("s_seg")
        s_bt = sem("s_bt")
        s_es = sem("s_es")
        s_xd = sem("s_xd")
        s_xe = sem("s_xe")
        s_gmm = sem("s_gmm")
        s_mix = sem("s_mix")
        s_yp = sem("s_yp")
        s_u = sem("s_u")
        s_S = sem("s_S")
        s_yt = sem("s_yt")
        s_yT = sem("s_yT")
        s_y2 = sem("s_y2")
        s_sq = sem("s_sq")
        s_o = sem("s_o")
        s_res = sem("s_res")
        block = ctx.enter_context(nc.Block())

        xf = x.rearrange("b s d -> (b s) d").rearrange("(t p) d -> p t d", p=P)
        of = out.rearrange("b s d -> (b s) d").rearrange("(t p) d -> p t d", p=P)
        N_CONST = 11
        N_WEIGHTS = 20

        @block.sync
        def _(sp_):
            for g in range(BATCH):
                sp_.dma_start(X[:, g * NC:(g + 1) * NC, :], xf[:, g * NC:(g + 1) * NC, :]).then_inc(s_x[g], 16)
            n = 0
            for dst, src in (
                (WrS[:], Wr), (BrS[:], br.partition_broadcast(P)),
                (vec_rows[0:NE * HC, :], b1.rearrange("e (c p) -> (e c) p", p=P)),
                (W1S[:, :, 0:HID], W1.rearrange("e d h -> d e h")),
                (W2S[:].rearrange("p e c d -> p (e c) d"), W2.rearrange("e (c p) d -> p (e c) d", p=P)),
                (B2S[:], b2.partition_broadcast(P)),
                (in_rows[:, 0:2, :], in_proj_w[0:INNER, :].rearrange("(c p) d -> p c d", p=P)),
                (in_rows[:, 2:6, :], in_proj_w[INNER:INNER + CONV, :].rearrange("(c p) d -> p c d", p=P)),
                (in_rows_dt[:], in_proj_w[INNER + CONV:INNER + CONV + HEADS, :]),
                (out_rows[:], out_proj_w),
                (cw[:], conv_w.rearrange("(c p) k -> p c k", p=P)),
                (vec_rows[NE * HC:NE * HC + TAPS, :], conv_b.rearrange("(c p) -> c p", p=P)),
                (vec_rows[NE * HC + TAPS:VECS, :], norm_w.rearrange("(c p) -> c p", p=P)),
                (dtb[:], dt_bias.partition_broadcast(P)), (alog[:], A_log.partition_broadcast(P)),
                (lnw[:], ln_w.partition_broadcast(P)), (lnb[:], ln_b.partition_broadcast(P)),
            ):
                sp_.dma_start(dst, src).then_inc(s_w, 16)
                n += 1
            for c in range(IC):
                sp_.dma_start(Dch[0:HD, c:c + 1], D_skip[2 * c:2 * c + 1].partition_broadcast(HD)).then_inc(s_w, 16)
                sp_.dma_start(Dch[HD:P, c:c + 1], D_skip[2 * c + 1:2 * c + 2].partition_broadcast(HD)).then_inc(s_w, 16)
                n += 2
            assert n == N_WEIGHTS + 1
            xn_v = xn_dram.rearrange("(t p) d -> p t d", p=P)
            y_v = y_dram[0:KTOP * TOK, :].rearrange("(k t p) d -> k p t d", p=P, k=KTOP)
            for layer in range(2):
                for g in range(BATCH):
                    sp_.wait_ge(s_xn, 2 * NT * layer + NC * (g + 1))
                    sp_.dma_start(xn_v[:, g * NC:(g + 1) * NC, :], XN[:, g * NC:(g + 1) * NC, :]).then_inc(s_xnd, 16)
                sp_.wait_ge(s_sc[0], 16 * (PAIRS + 2) * (layer + 1))
                sp_.wait_ge(s_sc[1], 16 * (PAIRS + 1) * (layer + 1))
                for g in range(BATCH):
                    for k, Y in enumerate((Y1, Y2)):
                        sp_.dma_start(Y[:, g * NC:(g + 1) * NC, :], y_v[k, :, g * NC:(g + 1) * NC, :]).then_inc(s_yl[g], 16)
            for g in range(BATCH):
                sp_.wait_ge(s_comb, BATCH + g + 1)
                sp_.dma_start(of[:, g * NC:(g + 1) * NC, :], X[:, g * NC:(g + 1) * NC, :]).then_inc(s_out, 16)
            sp_.wait_ge(s_out, 16 * BATCH)

        WEIGHTS = 16 * (N_WEIGHTS + 1)

        @block.gpsimd
        def _(pool):
            g = nc.gpsimd
            st = Steps(pool, s_pool)
            st.done(g.memset(ident[:], 0.0))
            st.done(g.memset(ones[:], 1.0))
            st.done(g.memset(upto[:], 1.0))
            st.done(g.memset(after[:], 1.0))
            st.done(g.memset(before_bf[:], 1.0))
            st.done(g.memset(ones_bf[:], 1.0))
            st.settle()
            g.affine_select(out=ident[:], in_=ident[:], compare_op=ALU.not_equal, fill=1.0, base=0,
                            pattern=[[-1, P]], channel_multiplier=1).then_inc(s_const, 1)
            g.affine_select(out=upto[:], in_=upto[:], compare_op=ALU.is_ge, fill=0.0, base=0,
                            pattern=[[1, P]], channel_multiplier=-1).then_inc(s_const, 1)
            g.affine_select(out=after[:], in_=after[:], compare_op=ALU.is_gt, fill=0.0, base=0,
                            pattern=[[-1, P]], channel_multiplier=1).then_inc(s_const, 1)
            g.affine_select(out=before_bf[:], in_=before_bf[:], compare_op=ALU.is_gt, fill=0.0, base=0,
                            pattern=[[1, P]], channel_multiplier=-1).then_inc(s_const, 1)
            small = dict(allow_small_or_imprecise_dtypes=True)
            g.iota(iota_e[:], pattern=[[1, NE]], base=0, channel_multiplier=0, **small).then_inc(s_const, 1)
            g.iota(iota_t[:], pattern=[[P, NT]], base=0, channel_multiplier=0, **small).then_inc(s_const, 1)
            g.iota(iota_st[:], pattern=[[1, ST]], base=0, channel_multiplier=0, **small).then_inc(s_const, 1)
            g.iota(iota_p[:], pattern=[[0, 1]], base=0, channel_multiplier=1, **small).then_inc(s_const, 1)
            g.iota(iota_row[:], pattern=[[1, P]], base=0, channel_multiplier=0, **small).then_inc(s_const, 1)
            g.iota(slot_id[:], pattern=[[P, ST]], base=0, channel_multiplier=1, **small).then_inc(s_const, 1)
            g.iota(group_val[:], pattern=[[1, NG]], base=-NG, channel_multiplier=0, **small).then_inc(s_const, 1)

            def experts(layer):
                pool.wait_ge(s_bf, layer + 1)
                for q in range(NG):
                    g.tensor_scalar(onehot_b[:, q, :], iota_row[:], b_f[:, q:q + 1], None,
                                    ALU.is_equal).then_inc(s_ob, 1)

                pool.wait_ge(s_xnd, 16 * BATCH * (layer + 1))

                def gather(pair, u):
                    j = pair * 2 + u
                    pool.wait_ge(s_gidx, layer * ST + j + 1)
                    if not early(pair):
                        pool.wait_ge(s_xt, layer * SLOT_TILES + j - 1)
                    pool.sem_inc(s_turn, 1)
                    g.indirect_dma_start(out=XG[u][:], out_offset=None, in_=xn_dram,
                                         in_offset=bass.IndirectOffsetOnAxis(ap=gidx[u][:, 0:1], axis=0)
                                         ).then_inc(s_gath[u], 16)

                def scatter(pair, u):
                    j = pair * 2 + u
                    pool.wait_ge(s_sidx, layer * SLOT_TILES + j + 1)
                    pool.wait_ge(s_yc, layer * SLOT_TILES + j + 1)
                    pool.sem_inc(s_turn, 1)
                    g.indirect_dma_start(out=y_dram, out_offset=bass.IndirectOffsetOnAxis(ap=sidx[u][:, 0:1], axis=0),
                                         in_=YS[u][:], in_offset=None).then_inc(s_sc[u], 16)

                gather(0, 0)
                gather(0, 1)
                for u in range(2):
                    gather(1, u)
                    scatter(0, u)
                with pool.Fori(1, PAIRS + 1) as pair:
                    for u in range(2):
                        gather(pair + 1, u)
                        scatter(pair, u)
                scatter(PAIRS + 1, 0)

            experts(0)
            pool.wait_ge(s_la, 1)

            def batch(b):
                for c in range(NC):
                    if not (isinstance(b, int) and c < 2):
                        pool.wait_ge(s_seg, b * NC + (c - 1))
                    g.tensor_tensor(seg_rhs[c % 2][:], upto[:].unsqueeze(1).broadcast_to([P, HEADS, P]),
                                    row(la, b * NC + c).unsqueeze(2).broadcast_to([P, HEADS, P]),
                                    ALU.mult).then_inc(s_segr, 1)

            batch(0)
            with pool.Fori(1, BATCH) as b:
                batch(b)
            experts(1)

        @block.tensor
        def _(pe):
            mm = nc.tensor.matmul

            def norm_project(n, rhs, width):
                def small(g):
                    pe.wait_ge(s_xnt, BATCH * n + g + 1)
                    for t in range(g * NC, (g + 1) * NC):
                        last = mm(PS[2][:, t * width:(t + 1) * width], XNT[:, t * P:(t + 1) * P], rhs,
                                  start=True, stop=True)
                    return last

                for g in range(BATCH):
                    pe.wait_ge(s_xn, NT * n + (g + 1) * NC)
                    if g >= 2:
                        pe.wait_ge(s_xnt, BATCH * n + g - 1)
                    for c in range(NC):
                        last = nc.tensor.transpose(PS[g % 2][:, c * P:(c + 1) * P], XN[:, g * NC + c, :], ident[:])
                    last.then_inc(s_lnT, 1)
                    if g:
                        small(g - 1)
                small(BATCH - 1).then_inc(s_small, 1)

            def weights():
                pe.wait_ge(s_w, WEIGHTS)
                for c in range(4):
                    nc.tensor.transpose(PS[6][:, c * P:(c + 1) * P], in_rows[:, c, :], ident[:])
                for c in range(2):
                    nc.tensor.transpose(PS[7][:, c * P:(c + 1) * P], in_rows[:, 4 + c, :], ident[:])
                nc.tensor.transpose(PS[7][:, 256:256 + HEADS], in_rows_dt[:], ident[0:HEADS, 0:HEADS])
                nc.tensor.transpose(PS[7][:, 260:260 + VECS], vec_rows[:], ident[0:VECS, 0:VECS])
                for c in range(IC):
                    last = nc.tensor.transpose(PS[5][:, c * P:(c + 1) * P], out_rows[:, c * P:(c + 1) * P], ident[:])
                last.then_inc(s_prep, 1)

            def experts(layer):
                pe.wait_ge(s_picks, layer + 1)
                mm(PS[3][:, 0:NT * NE], before_bf[:], picks_bf[:], start=True, stop=True)
                mm(PS[4][:, 0:NT * NE], ones_bf[:], picks_bf[:], start=True, stop=True).then_inc(s_cnt, 1)
                pe.wait_ge(s_w1s, 1)
                pe.wait_ge(s_ids, layer + 1)
                for q in range(NG):
                    pe.wait_ge(s_ob, NG * layer + q + 1)
                    last = mm(PS[5][:, 0:2 * ST], onehot_b[:, q, :], rhs_ids[:, q, :, :].rearrange("p a b -> p (a b)"),
                              start=(q == 0), stop=(q == NG - 1))
                last.then_inc(s_idp, 1)
                pe.wait_ge(s_te, layer + 1)
                B0 = layer * SLOT_TILES

                def turn(pair, u):
                    j = pair * 2 + u
                    pe.wait_ge(s_gath[u], layer * 16 * (ST // 2) + (pair + 1) * 16)
                    if not early(pair):
                        pe.wait_ge(s_xtc, B0 + j - 1)
                    nc.tensor.transpose(PS[u][:, 0:P], XG[u][:], ident[:]).then_inc(s_xt, 1)

                def step(pair, u, last_one=False):
                    j = pair * 2 + u
                    e = pe.value_load(te_i[0:1, ds(j, 1)], min_val=0, max_val=NE - 1)
                    pe.wait_ge(s_xtc, B0 + j + 1)
                    pe.wait_ge(s_w1, B0 + j + 1)
                    for half, (free, ready) in enumerate(((s_ra, s_upa), (s_rb, s_upb))):
                        bank = PS[2 + 2 * half + u]
                        if not early(pair):
                            pe.wait_ge(free, B0 + j - 1)
                        for c in range(2):
                            h = 2 * half + c
                            last = mm(bank[:, c * P:(c + 1) * P], W1B[u][:, h * P:(h + 1) * P], XT[u][:],
                                      start=True, stop=True)
                        last.then_inc(ready, 1)
                    if not last_one:
                        turn(*after_tile(pair, u))
                    pe.wait_ge(s_ra, B0 + j + 1)
                    if not early(pair):
                        pe.wait_ge(s_yc, B0 + j - 1)
                    for c in range(HC):
                        if c == 2:
                            pe.wait_ge(s_rb, B0 + j + 1)
                        last = mm(PS[6 + u][:, 0:D], H[u][:, c, :],
                                  W2S[:, ds(e, 1), c, :].rearrange("p a d -> p (a d)"),
                                  start=(c == 0), stop=(c == HC - 1))
                    last.then_inc(s_y, 1)

                turn(0, 0)
                step(0, 0)
                step(0, 1)
                with pe.Fori(1, PAIRS + 1) as pair:
                    for u in range(2):
                        step(pair, u)
                step(PAIRS + 1, 0, True)

            def mixer():
                pe.wait_ge(s_la, 1)
                flat = la[:].rearrange("p t h -> p (t h)")
                for k, m in enumerate((upto, after, ones)):
                    last = mm(PS[3][:, k * NT * HEADS:(k + 1) * NT * HEADS], m[:], flat, start=True, stop=True)
                last.then_inc(s_dec, 1)
                pe.wait_ge(s_dece, 1)

                def batch(b):
                    first = isinstance(b, int)

                    def s1(c):
                        q = b * NC + c
                        tile = slice(c * P, (c + 1) * P)
                        if not (first and c == 0):
                            pe.wait_ge(s_gmm, q)
                        for i in range(IC):
                            nc.tensor.transpose(PS[2][:, i * P:(i + 1) * P], conv[i][:, tile], ident[:])
                        mm(PS[2][:, 2 * P:3 * P], conv[2][:, tile], conv[3][:, tile], start=True,
                           stop=True).then_inc(s_tr, 1)
                        if c < NC - 1:
                            if not (first and c == 0):
                                pe.wait_ge(s_bt, b * (NC - 1) + c)
                            nc.tensor.transpose(PS[3][:, 0:P], conv[2][:, tile], ident[:]).then_inc(s_trb, 1)
                        pe.wait_ge(s_segr, q + 1)
                        if not (first and c == 0):
                            pe.wait_ge(s_es, q)
                        mm(PS[5][:], after[:], seg_rhs[c % 2][:].rearrange("p h t -> p (h t)"), start=True,
                           stop=True).then_inc(s_seg, 1)

                    def s2(c):
                        q = b * NC + c
                        tile = slice(c * P, (c + 1) * P)
                        u = c % 2
                        if not (first and c == 0):
                            pe.wait_ge(s_yt, q)
                        for i in range(IC):
                            mm(PS[6][:, i * P:(i + 1) * P], conv[i][:, tile], diagD[:, i, :], start=(i == 0),
                               stop=False, skip_group_check=True)
                        pe.wait_ge(s_mix, q + 1)
                        pe.wait_ge(s_xd, q + 1)
                        for h in range(HEADS):
                            last = mm(PS[6][:, h * HD:(h + 1) * HD], mix[u][:, h, :], xdt[u][:, h * HD:(h + 1) * HD],
                                      start=False, stop=True, skip_group_check=True)
                        if c:
                            pe.wait_ge(s_S, b * (NC - 1) + c)
                            last = mm(PS[6][:, INNER:2 * INNER], conv[3][:, tile], S[:], start=True, stop=True,
                                      skip_group_check=True)
                        last.then_inc(s_yp, 1)
                        if c < NC - 1:
                            pe.wait_ge(s_bt, b * (NC - 1) + c + 1)
                            pe.wait_ge(s_xe, b * (NC - 1) + c + 1)
                            if not (first and c == 0):
                                pe.wait_ge(s_S, b * (NC - 1) + c)
                            mm(PS[7][:, 0:INNER], btok[u][:], xend[u][:], start=True, stop=True).then_inc(s_u, 1)

                    def s3(c):
                        q = b * NC + c
                        pe.wait_ge(s_yt, q + 1)
                        if not (first and c == 0):
                            pe.wait_ge(s_y2, q)
                        for i in range(IC):
                            last = nc.tensor.transpose(PS[4][:, i * P:(i + 1) * P], yt[c % 2][:, i * P:(i + 1) * P], ident[:])
                        last.then_inc(s_yT, 1)

                    def s4(c):
                        q = b * NC + c
                        if c == 0:
                            pe.wait_ge(s_cv, (b + 1) * 6)
                        pe.wait_ge(s_y2, q + 1)
                        for i in range(IC):
                            mm(PS[0][:, c * P:(c + 1) * P], y2T[:, c, i, :], WoT[:, i, :], start=(i == 0), stop=(i == IC - 1))
                        pe.wait_ge(s_sq, q + 1)
                        for i in range(IC):
                            last = mm(PS[1][:, c:c + 1], sq[c % 2][:, i, :], ones[:, 0:1], start=(i == 0), stop=(i == IC - 1))
                        last.then_inc(s_o, 1)

                    for m, k in enumerate(BLOCKS):
                        if m < 2:
                            if not first:
                                pe.wait_ge(s_res, b)
                        else:
                            pe.wait_ge(s_cv, b * 6 + (m - 1))
                        w0 = X0 + k * P if k < TAPS else Z0 + (k - TAPS) * P
                        mm(PS[m % 2][:], WT[:, w0:w0 + P], XNT[:, ds(b * SEQ, SEQ)], start=True,
                           stop=True).then_inc(s_proj, 1)
                    pe.wait_ge(s_act_ch, (b + 1) * TAPS)
                    s1(0)
                    for c in range(NC):
                        if c + 1 < NC:
                            s1(c + 1)
                        s2(c)
                        if c:
                            s3(c - 1)
                        if c > 1:
                            s4(c - 2)
                    s3(NC - 1)
                    s4(NC - 2)
                    s4(NC - 1)

                batch(0)
                with pe.Fori(1, BATCH) as b:
                    batch(b)

            pe.wait_ge(s_const, N_CONST)
            pe.wait_ge(s_w, WEIGHTS)
            norm_project(0, WrS[:], NE)
            weights()
            experts(0)
            norm_project(1, WT[:, DT0:DT0 + HEADS], HEADS)
            mixer()
            norm_project(2, WrS[:], NE)
            experts(1)

        @block.scalar
        def _(act):
            A = nc.scalar.activation
            st = Steps(act, s_act)

            def norm_project(n):
                for g in range(BATCH):
                    act.wait_ge(s_lnT, BATCH * n + g + 1)
                    A(XNT[:, g * SEQ:(g + 1) * SEQ], PS[g % 2][:], ACT.Copy).then_inc(s_xnt, 1)

            def weights():
                act.wait_ge(s_prep, 1)
                act.wait_ge(s_w, WEIGHTS)
                st.done(A(WT[:, Z0:Z0 + INNER], PS[6][:, 0:INNER], ACT.Copy))
                st.done(A(WT[:, X0:X0 + INNER], PS[6][:, INNER:2 * INNER], ACT.Copy))
                st.done(A(WT[:, X0 + INNER:X0 + CONV], PS[7][:, 0:2 * P], ACT.Copy))
                st.done(A(WT[:, DT0:DT0 + HEADS], PS[7][:, 256:256 + HEADS], ACT.Copy))
                st.done(A(W1S[:, :, HID:W1W], PS[7][:, 260:260 + NE * HC].rearrange("p (e c) -> p e c", e=NE), ACT.Copy))
                st.done(A(cb[:], PS[7][:, 260 + NE * HC:260 + NE * HC + TAPS], ACT.Copy))
                st.done(A(nw[:], PS[7][:, 260 + NE * HC + TAPS:260 + VECS], ACT.Copy))
                st.done(A(expA[:], alog[:], ACT.Exp))
                st.settle()
                st.done(A(WoT[:, 0, :], PS[5][:, 0:P], ACT.Copy, scale=nw[:, 0:1]))
                st.settle()
                A(WoT[:, 1, :], PS[5][:, P:2 * P], ACT.Copy, scale=nw[:, 1:2]).then_inc(s_w1s, 1)

            def experts(layer):
                act.wait_ge(s_gd, layer + 1)
                A(ge[:], gd[:], ACT.Exp).then_inc(s_ge, 1)
                act.wait_ge(s_te, layer + 1)
                act.wait_ge(s_w1s, 1)
                B0 = layer * SLOT_TILES

                def weights_of(pair, u):
                    j = pair * 2 + u
                    e = act.value_load(te_i[0:1, ds(j, 1)], min_val=0, max_val=NE - 1)
                    if not early(pair):
                        act.wait_ge(s_upb, B0 + j - 1)
                        act.wait_ge(s_ra, B0 + j - 1)
                        act.wait_ge(s_rb, B0 + j - 1)
                    A(W1B[u][:], W1S[:, ds(e, 1), :].rearrange("p a h -> p (a h)"), ACT.Copy).then_inc(s_w1, 1)

                def step(pair, u, last_one=False):
                    j = pair * 2 + u
                    if not last_one:
                        weights_of(*after_tile(pair, u))
                    act.wait_ge(s_upb, B0 + j + 1)
                    act.wait_ge(s_w1, B0 + j + 1)
                    if not early(pair):
                        act.wait_ge(s_y, B0 + j - 1)
                    for c in (2, 3):
                        last = A(H[u][:, c, :], PS[4 + u][:, (c - 2) * P:(c - 1) * P], ACT.Relu,
                                 bias=W1B[u][:, HID + c:HID + c + 1])
                    last.then_inc(s_rb, 1)

                weights_of(0, 0)
                step(0, 0)
                step(0, 1)
                with act.Fori(1, PAIRS + 1) as pair:
                    for u in range(2):
                        step(pair, u)
                step(PAIRS + 1, 0, True)

            def mixer():
                act.wait_ge(s_sp, 1)
                A(sp[1][:], sp[0][:], ACT.Exp, scale=-1.0).then_inc(s_spe, 1)
                act.wait_ge(s_dec, 1)
                A(decay[:].rearrange("p k t h -> p (k t h)"), PS[3][:, 0:3 * NT * HEADS], ACT.Exp).then_inc(s_dece, 1)

                def batch(b):
                    first = isinstance(b, int)

                    def tanh(m):
                        if m < 2:
                            if not first:
                                act.wait_ge(s_cv, b * 6 + (m - 1))
                        else:
                            act.wait_ge(s_act_ch, b * TAPS + (m - 1))
                        if m < TAPS:
                            act.wait_ge(s_cv, b * 6 + (m + 1))
                            A(th[m % 2][:], acc[m % 2][:], ACT.Tanh).then_inc(s_th, 1)
                        else:
                            act.wait_ge(s_proj, b * 6 + (m + 1))
                            A(th[m % 2][:], PS[m % 2][:], ACT.Tanh, scale=0.5).then_inc(s_th, 1)

                    for m, k in enumerate(BLOCKS[0:TAPS]):
                        act.wait_ge(s_proj, b * 6 + (m + 1))
                        if not (first and m < 2):
                            act.wait_ge(s_act_ch, b * TAPS + (m - 1))
                        A(acc[m % 2][:], PS[m % 2][:], ACT.Identity, bias=cbh[:, k:k + 1],
                          scale=cwh[:, k, TAPS - 1:TAPS]).then_inc(s_tap, 1)
                        if m:
                            tanh(m - 1)
                    tanh(TAPS - 1)
                    tanh(TAPS)
                    tanh(TAPS + 1)

                    def chunk(c):
                        q = b * NC + c
                        u = c % 2
                        if c < NC - 1:
                            act.wait_ge(s_trb, b * (NC - 1) + (c + 1))
                            if c >= 2:
                                act.wait_ge(s_u, b * (NC - 1) + (c - 1))
                            elif not first:
                                act.wait_ge(s_u, b * (NC - 1))
                            A(btok[u][:], PS[3][:, 0:P], ACT.Copy).then_inc(s_bt, 1)
                        act.wait_ge(s_seg, q + 1)
                        if not (first and c < 2):
                            act.wait_ge(s_mix, q - 1)
                        A(eseg[u][:].rearrange("p h t -> p (h t)"), PS[5][:], ACT.Exp).then_inc(s_es, 1)

                    def squares(c):
                        q = b * NC + c
                        act.wait_ge(s_y2, q + 1)
                        if not (first and c < 2):
                            act.wait_ge(s_o, q - 1)
                        A(sq[c % 2][:], y2T[:, c, :, :], ACT.Square).then_inc(s_sq, 1)

                    chunk(0)
                    chunk(1)
                    for c in range(NC):
                        if c + 2 < NC:
                            chunk(c + 2)
                        squares(c)

                batch(0)
                with act.Fori(1, BATCH) as b:
                    batch(b)

            norm_project(0)
            weights()
            experts(0)
            norm_project(1)
            mixer()
            norm_project(2)
            experts(1)

        @block.vector
        def _(dve):
            v = nc.vector
            st = Steps(dve, s_dve)

            def rsqrt(r, val, tmp):
                st.link(v.tensor_scalar(r.bitcast(I32), val.bitcast(I32), -0.5, RSQRT_SEED, ALU.mult, ALU.add))
                for _ in range(3):
                    st.link(v.tensor_tensor(tmp, r, r, ALU.mult))
                    st.link(v.scalar_tensor_tensor(out=tmp, in0=tmp, scalar=-0.5, in1=val, op0=ALU.mult, op1=ALU.mult))
                    st.link(v.scalar_tensor_tensor(out=r, in0=tmp, scalar=1.5, in1=r, op0=ALU.add, op1=ALU.mult))

            def norm(n):
                for t in range(NT):
                    if n == 0 and t % NC == 0:
                        dve.wait_ge(s_x[t // NC], 16)
                    st.done(v.bn_stats(stats[:, t, :], X[:, t, :]))
                st.settle()
                for t in range(NT):
                    st.done(v.bn_aggr(mv[:, t, :], stats[:, t, :]))
                st.settle()
                st.link(v.tensor_scalar(rv[:], mv[:, :, 1], EPS, None, ALU.add))
                rsqrt(rs[:], rv[:], rt[:])
                if n == 1:
                    dve.wait_ge(s_xnd, 16 * BATCH)
                for t in range(NT):
                    v.tensor_scalar(XN[:, t, :], X[:, t, :], mv[:, t, 0:1], rs[:, t:t + 1],
                                    ALU.subtract, ALU.mult).then_inc(s_xn, 1)

            def parameters():
                dve.wait_ge(s_w, WEIGHTS)
                dve.wait_ge(s_w1s, 1)
                st.done(v.tensor_scalar(cwh[:].rearrange("p c k -> p (c k)"), cw[:].rearrange("p c k -> p (c k)"), 0.5, None, ALU.mult))
                st.done(v.tensor_scalar(cbh[:], cb[:], 0.5, None, ALU.mult))
                for c in range(IC):
                    st.done(v.tensor_scalar(diagD[:, c, :], ident[:], Dch[:, c:c + 1], None, ALU.mult))
                st.settle()

            def route(layer):
                dve.wait_ge(s_small, 2 * layer + 1)
                st.link(v.tensor_tensor(lg[:], PS[2][:, 0:NT * NE].rearrange("p (t e) -> p t e", e=NE),
                                        BrS[:].unsqueeze(1).broadcast_to([P, NT, NE]), ALU.add))
                for t in range(NT):
                    st.done(v.max(top[:, t, :], lg[:, t, :]))
                st.settle()
                for t in range(NT):
                    st.done(v.max_index(topi[:, t, :], top[:, t, :], lg[:, t, :]))
                v.tensor_tensor(gd[:], top[:, :, 1], top[:, :, 0], ALU.subtract).then_inc(s_gd, 1)
                st.settle()
                st.link(v.tensor_copy(topf[:], topi[:, :, 0:KTOP]))
                for k in range(KTOP):
                    st.done(v.tensor_tensor(pick[:, k, :, :], iota_e[:].unsqueeze(1).broadcast_to([P, NT, NE]),
                                            topf[:, :, k:k + 1].broadcast_to([P, NT, NE]), ALU.is_equal))
                st.settle()
                v.tensor_tensor(picks_bf[:].rearrange("p (t e) -> p t e", e=NE), pick[:, 0, :, :], pick[:, 1, :, :],
                                ALU.add).then_inc(s_picks, 1)
                dve.wait_ge(s_ge, layer + 1)
                st.link(v.tensor_scalar(gr[:], ge[:], 2.0, 2.0, ALU.mult, ALU.add))
                st.link(v.reciprocal(gate[:, 0, :], gr[:]))
                st.done(v.tensor_tensor(gate[:, 1, :], gate[:, 0, :], ge[:], ALU.mult))
                dve.wait_ge(s_cnt, layer + 1)
                st.link(v.tensor_copy(cnt[:], PS[4][:, 0:NT * NE].rearrange("p (t e) -> p e t", e=NE)))
                st.link(v.tensor_tensor_scan(run[:].rearrange("p e t -> p (e t)"), ones[:, 0:NT * NE],
                                             cnt[:].rearrange("p e t -> p (e t)"), 0.0, ALU.mult, ALU.add))
                st.link(v.tensor_tensor(excl[:], run[:], cnt[:], ALU.subtract))
                st.link(v.tensor_tensor(n_e[:], run[:, :, NT - 1], excl[:, :, 0], ALU.subtract))
                st.link(v.tensor_tensor(cmp16[:], n_e[:].unsqueeze(2).broadcast_to([P, NE, NT]),
                                        iota_t[:].unsqueeze(1).broadcast_to([P, NE, NT]), ALU.is_gt))
                st.link(v.tensor_reduce(tiles_e[:], cmp16[:], AX.X, ALU.add))
                st.link(v.tensor_tensor_scan(end_e[:], ones[:, 0:NE], tiles_e[:], 0.0, ALU.mult, ALU.add))
                st.link(v.tensor_tensor(adj[:], end_e[:], tiles_e[:], ALU.subtract))
                st.link(v.scalar_tensor_tensor(out=adj[:], in0=adj[:], scalar=float(P), in1=excl[:, :, 0],
                                               op0=ALU.mult, op1=ALU.subtract))
                st.link(v.tensor_tensor(base[:], excl[:], adj[:].unsqueeze(2).broadcast_to([P, NE, NT]), ALU.add))
                st.link(v.tensor_tensor(slot_all[:], PS[3][:, 0:NT * NE].rearrange("p (t e) -> p t e", e=NE),
                                        base[:].rearrange("p e t -> p t e"), ALU.add))
                for k in range(KTOP):
                    st.done(v.tensor_tensor(slot_pick[:, k, :, :], pick[:, k, :, :], slot_all[:], ALU.mult))
                st.settle()
                st.link(v.tensor_reduce(slot[:], slot_pick[:].rearrange("p k t e -> p (k t) e"), AX.X, ALU.add))
                st.link(v.tensor_copy(slot_i[:], slot[:]))
                st.done(v.tensor_scalar(a_i[:], slot_i[:], 7, None, ALU.logical_shift_right))
                st.done(v.tensor_scalar(b_i[:], slot_i[:], P - 1, None, ALU.bitwise_and))
                st.settle()
                v.tensor_copy(b_f[:], b_i[:]).then_inc(s_bf, 1)
                st.link(v.tensor_copy(a_f[:], a_i[:]))
                dve.wait_ge(s_bf, layer + 1)
                st.done(v.tensor_tensor(val_g[:], group_val[:], a_f[:], ALU.subtract))
                st.done(v.tensor_scalar(val_p[:], b_f[:], -1.0, iota_p[:, 0:1], ALU.mult, ALU.add))
                st.link(v.tensor_tensor(onehot_a[:], iota_st[:].unsqueeze(1).broadcast_to([P, NG, ST]),
                                        a_f[:].unsqueeze(2).broadcast_to([P, NG, ST]), ALU.is_equal))
                st.done(v.tensor_tensor(rhs_ids[:, :, 0, :], onehot_a[:],
                                        val_g[:].unsqueeze(2).broadcast_to([P, NG, ST]), ALU.mult))
                st.settle()
                v.tensor_tensor(rhs_ids[:, :, 1, :], onehot_a[:],
                                val_p[:].unsqueeze(2).broadcast_to([P, NG, ST]), ALU.mult).then_inc(s_ids, 1)
                st.link(v.tensor_tensor(te_cmp[:], iota_st[:].unsqueeze(2).broadcast_to([P, ST, NE]),
                                        end_e[:].unsqueeze(1).broadcast_to([P, ST, NE]), ALU.is_ge))
                st.link(v.tensor_reduce(te_f[:], te_cmp[:], AX.X, ALU.add))
                v.tensor_scalar(te_i[:], te_f[:], float(NE - 1), None, ALU.min).then_inc(s_te, 1)
                dve.wait_ge(s_idp, layer + 1)
                st.link(v.scalar_tensor_tensor(out=ids_f[:], in0=PS[5][:, 0:ST], scalar=float(P), in1=slot_id[:],
                                               op0=ALU.mult, op1=ALU.add))
                st.link(v.scalar_tensor_tensor(out=rows_out[:], in0=PS[5][:, ST:2 * ST], scalar=float(KTOP * TOK),
                                               in1=ids_f[:], op0=ALU.add, op1=ALU.add))
                st.link(v.tensor_scalar(rows_in[:], rows_out[:], TOK - 1, None, ALU.bitwise_and))

            def experts(layer):
                B0 = layer * SLOT_TILES
                dve.wait_ge(s_te, layer + 1)

                def gather_index(pair, u):
                    j = pair * 2 + u
                    if not early(pair):
                        dve.wait_ge(s_gath[u], layer * 16 * (ST // 2) + pair * 16)
                    v.tensor_copy(gidx[u][:], rows_in[:, ds(j, 1)]).then_inc(s_gidx, 1)

                def copy_xt(pair, u):
                    j = pair * 2 + u
                    dve.wait_ge(s_xt, B0 + j + 1)
                    if not early(pair):
                        dve.wait_ge(s_upb, B0 + j - 1)
                    v.tensor_copy(XT[u][:], PS[u][:, 0:P]).then_inc(s_xtc, 1)

                def step(pair, u, last_one=False):
                    j = pair * 2 + u
                    e = dve.value_load(te_i[0:1, ds(j, 1)], min_val=0, max_val=NE - 1)
                    dve.wait_ge(s_upa, B0 + j + 1)
                    dve.wait_ge(s_w1, B0 + j + 1)
                    if not early(pair):
                        dve.wait_ge(s_y, B0 + j - 1)
                    for c in range(2):
                        last = v.tensor_scalar(H[u][:, c, :], PS[2 + u][:, c * P:(c + 1) * P],
                                               W1B[u][:, HID + c:HID + c + 1], 0.0, ALU.add, ALU.max)
                    last.then_inc(s_ra, 1)
                    if not last_one:
                        copy_xt(*after_tile(pair, u))
                        gather_index(pair + 1, u)
                    if not early(pair):
                        dve.wait_ge(s_sc[u], layer * 16 * (PAIRS + 2 - u) + pair * 16)
                    v.tensor_copy(sidx[u][:], rows_out[:, ds(j, 1)]).then_inc(s_sidx, 1)
                    dve.wait_ge(s_y, B0 + j + 1)
                    v.tensor_tensor(YS[u][:], PS[6 + u][:, 0:D], row(B2S, e), ALU.add).then_inc(s_yc, 1)

                gather_index(0, 0)
                gather_index(0, 1)
                copy_xt(0, 0)
                step(0, 0)
                step(0, 1)
                with dve.Fori(1, PAIRS + 1) as pair:
                    for u in range(2):
                        step(pair, u)
                step(PAIRS + 1, 0, True)
                for g in range(BATCH):
                    dve.wait_ge(s_yl[g], 32 * (layer + 1))
                    for t in range(g * NC, (g + 1) * NC):
                        st.done(v.scalar_tensor_tensor(out=X[:, t, :], in0=Y1[:, t, :], scalar=gate[:, 0, t:t + 1],
                                                       in1=X[:, t, :], op0=ALU.mult, op1=ALU.add))
                    st.settle()
                    for t in range(g * NC, (g + 1) * NC):
                        last = v.scalar_tensor_tensor(out=X[:, t, :], in0=Y2[:, t, :], scalar=gate[:, 1, t:t + 1],
                                                      in1=X[:, t, :], op0=ALU.mult, op1=ALU.add)
                    last.then_inc(s_comb, 1)
                dve.wait_ge(s_comb, BATCH * (layer + 1))

            def time_steps():
                dve.wait_ge(s_small, 2)
                st.link(v.tensor_tensor(dtr[:], PS[2][:, 0:NT * HEADS].rearrange("p (t h) -> p t h", h=HEADS),
                                        dtb[:].unsqueeze(1).broadcast_to([P, NT, HEADS]), ALU.add))
                v.scalar_tensor_tensor(out=sp[0][:], in0=dtr[:], scalar=-1.0, in1=dtr[:], op0=ALU.mult,
                                       op1=ALU.max).then_inc(s_sp, 1)
                dve.wait_ge(s_spe, 1)
                e, z, z2, p = sp[1][:], sp[2][:], sp[3][:], sp[4][:]
                st.link(v.tensor_scalar(z2, e, 2.0, None, ALU.add))
                st.link(v.reciprocal(z, z2))
                st.link(v.tensor_tensor(z, z, e, ALU.mult))
                st.link(v.tensor_tensor(z2, z, z, ALU.mult))
                st.link(v.tensor_scalar(p, z2, 1.0 / 17, None, ALU.mult))
                for k in (15, 13, 11, 9, 7, 5, 3):
                    st.link(v.scalar_tensor_tensor(out=p, in0=p, scalar=1.0 / k, in1=z2, op0=ALU.add, op1=ALU.mult))
                st.link(v.scalar_tensor_tensor(out=p, in0=p, scalar=1.0, in1=z, op0=ALU.add, op1=ALU.mult))
                st.link(v.tensor_scalar(z, dtr[:], 0.0, None, ALU.max))
                st.link(v.scalar_tensor_tensor(out=dt[:], in0=p, scalar=2.0, in1=z, op0=ALU.mult, op1=ALU.add))
                dve.wait_ge(s_w1s, 1)
                st.link(v.tensor_tensor(la[:], dt[:], expA[:].unsqueeze(1).broadcast_to([P, NT, HEADS]), ALU.mult))
                v.tensor_scalar(la[:], la[:], -1.0, LEAST_DECAY, ALU.mult, ALU.max).then_inc(s_la, 1)
                dve.wait_ge(s_dece, 1)
                st.link(v.tensor_tensor(dtd[:], dt[:], decay[:, 1, :, :], ALU.mult))

            def mixer():
                time_steps()

                def by_head(tensor, q):
                    return row(tensor, q).unsqueeze(2).broadcast_to([P, HEADS, HD])

                def heads(ap):
                    return ap.rearrange("p (h d) -> p h d", h=HEADS)

                def batch(b):
                    first = isinstance(b, int)

                    def taps(m, k):
                        dve.wait_ge(s_tap, b * TAPS + (m + 1))
                        for j in range(TAPS - 1):
                            back = TAPS - 1 - j
                            last = v.scalar_tensor_tensor(out=acc[m % 2][:, back:SEQ], in0=PS[m % 2][:, 0:SEQ - back],
                                                          scalar=cwh[:, k, j:j + 1], in1=acc[m % 2][:, back:SEQ],
                                                          op0=ALU.mult, op1=ALU.add)
                            if j < TAPS - 2:
                                st.link(last)
                        last.then_inc(s_cv, 1)

                    def activate(m, k):
                        dve.wait_ge(s_th, b * 6 + (m + 1))
                        if m == 0 and not first:
                            dve.wait_ge(s_yp, b * NC)
                            dve.wait_ge(s_seg, b * NC)
                        dve.wait_ge(s_cv, b * 6 + (m + 1))
                        v.scalar_tensor_tensor(out=conv[k][:], in0=th[m % 2][:], scalar=1.0, in1=acc[m % 2][:],
                                               op0=ALU.add, op1=ALU.mult).then_inc(s_act_ch, 1)

                    for m, k in enumerate(BLOCKS[0:TAPS]):
                        taps(m, k)
                        if m:
                            activate(m - 1, BLOCKS[m - 1])
                    activate(TAPS - 1, BLOCKS[TAPS - 1])
                    for m in (TAPS, TAPS + 1):
                        dve.wait_ge(s_th, b * 6 + (m + 1))
                        v.scalar_tensor_tensor(out=gz[:, m - TAPS, :], in0=th[m % 2][:], scalar=1.0, in1=PS[m % 2][:],
                                               op0=ALU.add, op1=ALU.mult).then_inc(s_cv, 1)

                    def d1(c):
                        q = b * NC + c
                        u = c % 2
                        dve.wait_ge(s_tr, q + 1)
                        if not (first and c < 2):
                            dve.wait_ge(s_yp, q - 1)
                        v.tensor_tensor(heads(xdt[u][:]), heads(PS[2][:, 0:INNER]), by_head(dt, q),
                                        ALU.mult).then_inc(s_xd, 1)
                        if c < NC - 1:
                            if c >= 2:
                                dve.wait_ge(s_u, b * (NC - 1) + (c - 1))
                            elif not first:
                                dve.wait_ge(s_u, b * (NC - 1))
                            v.tensor_tensor(heads(xend[u][:]), heads(PS[2][:, 0:INNER]), by_head(dtd, q),
                                            ALU.mult).then_inc(s_xe, 1)
                        v.tensor_tensor(gm[u][:], PS[2][:, INNER:INNER + P], upto[:], ALU.mult).then_inc(s_gmm, 1)
                        dve.wait_ge(s_gmm, q + 1)
                        dve.wait_ge(s_es, q + 1)
                        v.tensor_tensor(mix[u][:], eseg[u][:], gm[u][:].unsqueeze(1).broadcast_to([P, HEADS, P]),
                                        ALU.mult).then_inc(s_mix, 1)

                    def d2(c):
                        q = b * NC + c
                        u = c % 2
                        dve.wait_ge(s_yp, q + 1)
                        if c < NC - 1:
                            dve.wait_ge(s_u, b * (NC - 1) + (c + 1))
                            if c:
                                st.link(v.tensor_tensor(heads(S[:]), heads(S[:]),
                                                        decay[:, 2, ds(q, 1), :].rearrange("p a h -> p (a h)")
                                                        .unsqueeze(2).broadcast_to([P, HEADS, HD]), ALU.mult))
                                v.tensor_tensor(S[:], S[:], PS[7][:, 0:INNER], ALU.add).then_inc(s_S, 1)
                            else:
                                v.tensor_copy(S[:], PS[7][:, 0:INNER]).then_inc(s_S, 1)
                            dve.wait_ge(s_S, b * (NC - 1) + (c + 1))
                        if not (first and c < 2):
                            dve.wait_ge(s_yT, q - 1)
                        if c:
                            st.link(v.tensor_tensor(heads(yi[:]), heads(PS[6][:, INNER:2 * INNER]),
                                                    decay[:, 0, ds(q, 1), :].rearrange("p a h -> p (a h)")
                                                    .unsqueeze(2).broadcast_to([P, HEADS, HD]), ALU.mult))
                            v.tensor_tensor(yt[u][:], yi[:], PS[6][:, 0:INNER], ALU.add).then_inc(s_yt, 1)
                        else:
                            v.tensor_copy(yt[u][:], PS[6][:, 0:INNER]).then_inc(s_yt, 1)

                    def d3(c):
                        q = b * NC + c
                        dve.wait_ge(s_yT, q + 1)
                        if c == 0:
                            dve.wait_ge(s_cv, (b + 1) * 6)
                            if not first:
                                dve.wait_ge(s_o, b * NC)
                        v.tensor_tensor(y2T[:, c, :, :], PS[4][:, 0:INNER].rearrange("p (i t) -> p i t", i=IC),
                                        gz[:, :, c * P:(c + 1) * P], ALU.mult).then_inc(s_y2, 1)

                    d1(0)
                    for c in range(NC):
                        if c + 1 < NC:
                            d1(c + 1)
                        d2(c)
                        if c:
                            d3(c - 1)
                    d3(NC - 1)

                    dve.wait_ge(s_o, (b + 1) * NC)
                    st.link(v.tensor_scalar(rv[:, 0:NC], PS[1][:, 0:NC], 0.25 / INNER, EPS, ALU.mult, ALU.add))
                    rsqrt(rs[:, 0:NC], rv[:, 0:NC], rt[:, 0:NC])
                    st.link(v.tensor_scalar(rs[:, 0:NC], rs[:, 0:NC], 0.5, None, ALU.mult))
                    for c in range(NC):
                        last = v.scalar_tensor_tensor(out=res[:, c, :], in0=PS[0][:, c * P:(c + 1) * P],
                                                      scalar=rs[:, c:c + 1], in1=row(XN, b * NC + c),
                                                      op0=ALU.mult, op1=ALU.add)
                        if c < NC - 1:
                            st.done(last)
                    last.then_inc(s_res, 1)
                    st.settle()
                    dve.wait_ge(s_res, b + 1)
                    for c in range(NC):
                        st.done(v.bn_stats(stats[:, c, :], res[:, c, :]))
                    st.settle()
                    dve.sem_inc(s_stats, 1)
                    for c in range(NC):
                        st.done(v.bn_aggr(mv[:, c, :], stats[:, c, :]))
                    st.settle()
                    st.link(v.tensor_scalar(rv[:, 0:NC], mv[:, 0:NC, 1], EPS, None, ALU.add))
                    rsqrt(rs[:, 0:NC], rv[:, 0:NC], rt[:, 0:NC])
                    xb = X[:, ds(b * NC, NC), :]
                    for c in range(NC):
                        st.done(v.tensor_scalar(fin[:, c, :], res[:, c, :], mv[:, c, 0:1], rs[:, c:c + 1],
                                                ALU.subtract, ALU.mult))
                    st.link(v.tensor_tensor(xb, xb, lnb[:].unsqueeze(1).broadcast_to([P, NC, D]), ALU.add))
                    st.link(v.tensor_tensor(fin[:], fin[:], lnw[:].unsqueeze(1).broadcast_to([P, NC, D]), ALU.mult))
                    st.link(v.tensor_tensor(xb, xb, fin[:], ALU.add))

                before = st.n
                batch(0)
                steps = st.n - before
                with dve.Fori(1, BATCH) as b:
                    st.enter(b - 1, steps)
                    batch(b)
                    st.leave(BATCH - 1)

            norm(0)
            dve.wait_ge(s_w, WEIGHTS)
            dve.wait_ge(s_const, N_CONST)
            route(0)
            experts(0)
            parameters()
            norm(1)
            mixer()
            norm(2)
            route(1)
            experts(1)


_INS = ["L0_attn_x", "L0_attn_in_proj_w", "L0_attn_conv_w", "L0_attn_conv_b", "L0_attn_dt_bias", "L0_attn_A_log",
        "L0_attn_D", "L0_attn_norm_w", "L0_attn_out_proj_w", "L0_attn_ln_w", "L0_attn_ln_b", "L0_ffn_Wr", "L0_ffn_br",
        "L0_ffn_W1", "L0_ffn_b1", "L0_ffn_W2", "L0_ffn_b2"]


def kernel(**inputs):
    import numpy as _np
    import concourse.bacc as _bacc
    from concourse import mybir as _mybir
    from concourse.bass_utils import run_bass_kernel_spmd as _run

    nc = _bacc.Bacc("TRN2", target_bir_lowering=False, num_devices=1)
    arrays, args = {}, []
    for name in _INS:
        a = _np.ascontiguousarray(inputs[name])
        arrays[f"in_{name}"] = a
        args.append(nc.dram_tensor(f"in_{name}", a.shape, _mybir.dt.from_np(a.dtype), kind="ExternalInput").ap())
    out = nc.dram_tensor("out_x", (BATCH, SEQ, D), F32, kind="ExternalOutput").ap()
    macaron_block(nc, *args, out)
    r = _run(nc, [arrays], core_ids=[0])
    return r.results[0]["out_x"]
```

```python
import concourse.bass as bass
from concourse import mybir
from contextlib import ExitStack

F32 = mybir.dt.float32
BF16 = mybir.dt.bfloat16
I32 = mybir.dt.int32
U32 = mybir.dt.uint32
ALU = mybir.AluOpType
ACT = mybir.ActivationFunctionType
AX = mybir.AxisListType
ds = bass.ds

P = 128
BATCH, SEQ, D = 4, 512, 128
TOK = BATCH * SEQ
NT = TOK // P
NC = SEQ // P
NE, HID, KTOP = 8, 512, 2
HC = HID // P
NG = KTOP * NT
SLOT_TILES = NG + NE - 1
TRIO = 3
TURNS = SLOT_TILES // TRIO
assert SLOT_TILES % TRIO == 0
W1W = HID + HC
INNER, STATE, HEADS, HD, TAPS = 256, 128, 4, 64, 4
CONV = INNER + 2 * STATE
IC = INNER // P
VECS = NE * HC + CONV // P + IC
EPS = 1e-5
LEAST_DECAY = -100.0
RSQRT_SEED = float(0x5F3759DF)
Z0, DT0, X0 = 0, INNER, INNER + HEADS
WCOLS = 2 * INNER + 2 * STATE + HEADS


class Steps:

    def __init__(self, engine, sem):
        self.engine, self.sem, self.base, self.n, self.fixed = engine, sem, 0, 0, 0

    def done(self, instruction):
        instruction.then_inc(self.sem, 1)
        self.n += 1

    def settle(self):
        self.engine.wait_ge(self.sem, self.base + self.n)

    def link(self, instruction):
        self.done(instruction)
        self.settle()

    def enter(self, i, per):
        self.fixed = self.base + self.n
        self.base, self.n, self.per = self.fixed + i * per, 0, per

    def leave(self, count):
        assert self.n == self.per, (self.n, self.per)
        self.base, self.n = self.fixed + count * self.per, 0


BLOCKS = (2, 3, 0, 1, 4, 5)


def early(turn):
    return isinstance(turn, int) and turn == 0


def in_steps(engine, ahead):
    def step(turn, u):
        for k in sorted(ahead, reverse=True):
            t, w = turn + (u + k) // TRIO, (u + k) % TRIO
            if not (isinstance(t, int) and t >= TURNS):
                ahead[k](t, w)

    for j in range(max(ahead)):
        for k in sorted(ahead, reverse=True):
            if j < k:
                ahead[k](0, j)
    for u in range(TRIO):
        step(0, u)
    with engine.Fori(1, TURNS - 1) as turn:
        for u in range(TRIO):
            step(turn, u)
    for u in range(TRIO):
        step(TURNS - 1, u)


def row(tensor, t):
    return tensor[:, ds(t, 1), :].rearrange("p a c -> p (a c)")


def macaron_block(nc, x, in_proj_w, conv_w, conv_b, dt_bias, A_log, D_skip, norm_w, out_proj_w,
                  ln_w, ln_b, Wr, br, W1, b1, W2, b2, out):
    ctx = ExitStack()
    with ctx:
        def sb(name, shape, dt=F32):
            return ctx.enter_context(nc.sbuf_tensor(name, shape, dt))

        def sem(name):
            return ctx.enter_context(nc.semaphore(name))

        X = sb("X", [P, NT, D])
        XN = sb("XN", [P, NT, D])
        XNT = sb("XNT", [P, TOK])
        W1S = sb("W1S", [P, NE, W1W])
        W2S = sb("W2S", [P, NE, HC, D])
        B2S = sb("B2S", [P, NE, D])
        vec_rows = sb("vec_rows", [VECS, P])
        WrS = sb("WrS", [P, NE])
        BrS = sb("BrS", [P, NE])
        in_rows = sb("in_rows", [P, 6, D])
        in_rows_dt = sb("in_rows_dt", [HEADS, D])
        WT = sb("WT", [P, WCOLS])
        out_rows = sb("out_rows", [P, INNER])
        WoT = sb("WoT", [P, IC, D])
        cw = sb("cw", [P, TAPS, TAPS])
        cb = sb("cb", [P, TAPS])
        cwh = sb("cwh", [P, TAPS, TAPS])
        cbh = sb("cbh", [P, TAPS])
        dtb = sb("dtb", [P, HEADS])
        alog = sb("alog", [P, HEADS])
        expA = sb("expA", [P, HEADS])
        Dch = sb("Dch", [P, IC])
        nw = sb("nw", [P, IC])
        diagD = sb("diagD", [P, IC, P])
        lnw = sb("lnw", [P, D])
        lnb = sb("lnb", [P, D])
        ident = sb("ident", [P, P])
        ones = sb("ones", [P, P])
        upto = sb("upto", [P, P])
        after = sb("after", [P, P])
        before_bf = sb("before_bf", [P, P], BF16)
        ones_bf = sb("ones_bf", [P, P], BF16)
        iota_e = sb("iota_e", [P, NE])
        iota_t = sb("iota_t", [P, NT])
        iota_st = sb("iota_st", [P, SLOT_TILES])
        iota_p = sb("iota_p", [P, 1])
        iota_row = sb("iota_row", [P, P], BF16)
        slot_id = sb("slot_id", [P, SLOT_TILES])
        group_val = sb("group_val", [P, NG])
        stats = sb("stats", [P, NT, 6])
        mv = sb("mv", [P, NT, 2])
        rs = sb("rs", [P, NT])
        rt = sb("rt", [P, NT])
        rv = sb("rv", [P, NT])
        lg = sb("lg", [P, NT, NE])
        top = sb("top", [P, NT, 8])
        topi = sb("topi", [P, NT, 8], U32)
        topf = sb("topf", [P, NT, KTOP])
        gate = sb("gate", [P, KTOP, NT])
        gd = sb("gd", [P, NT])
        ge = sb("ge", [P, NT])
        gr = sb("gr", [P, NT])
        pick = sb("pick", [P, KTOP, NT, NE])
        picks_bf = sb("picks_bf", [P, NT * NE], BF16)
        cnt = sb("cnt", [P, NE, NT])
        run = sb("run", [P, NE, NT])
        excl = sb("excl", [P, NE, NT])
        n_e = sb("n_e", [P, NE])
        cmp16 = sb("cmp16", [P, NE, NT])
        tiles_e = sb("tiles_e", [P, NE])
        end_e = sb("end_e", [P, NE])
        adj = sb("adj", [P, NE])
        base = sb("base", [P, NE, NT])
        slot_all = sb("slot_all", [P, NT, NE])
        slot_pick = sb("slot_pick", [P, KTOP, NT, NE])
        slot = sb("slot", [P, NG])
        slot_i = sb("slot_i", [P, NG], I32)
        a_i = sb("a_i", [P, NG], I32)
        b_i = sb("b_i", [P, NG], I32)
        a_f = sb("a_f", [P, NG])
        b_f = sb("b_f", [P, NG])
        val_p = sb("val_p", [P, NG])
        val_g = sb("val_g", [P, NG])
        onehot_a = sb("onehot_a", [P, NG, SLOT_TILES], BF16)
        rhs_ids = sb("rhs_ids", [P, NG, 2, SLOT_TILES], BF16)
        onehot_b = sb("onehot_b", [P, NG, P], BF16)
        ids_f = sb("ids_f", [P, SLOT_TILES])
        rows_out = sb("rows_out", [P, SLOT_TILES], I32)
        rows_in = sb("rows_in", [P, SLOT_TILES], I32)
        te_cmp = sb("te_cmp", [P, SLOT_TILES, NE])
        te_f = sb("te_f", [P, SLOT_TILES])
        te_i = sb("te_i", [P, SLOT_TILES], I32)
        XG = [sb(f"XG{u}", [P, D]) for u in range(TRIO)]
        XT = [sb(f"XT{u}", [P, P]) for u in range(TRIO)]
        W1B = [sb(f"W1B{u}", [P, W1W]) for u in range(TRIO)]
        H = [sb(f"H{u}", [P, HC, P]) for u in range(TRIO)]
        YS = [sb(f"YS{u}", [P, D]) for u in range(TRIO)]
        Y1 = sb("Y1", [P, NT, D])
        Y2 = sb("Y2", [P, NT, D])
        dtr = sb("dtr", [P, NT, HEADS])
        sp = [sb(f"sp{k}", [P, NT, HEADS]) for k in range(5)]
        dt = sb("dt", [P, NT, HEADS])
        la = sb("la", [P, NT, HEADS])
        decay = sb("decay", [P, 3, NT, HEADS])
        dtd = sb("dtd", [P, NT, HEADS])
        acc = [sb(f"acc{k}", [P, SEQ]) for k in range(2)]
        th = [sb(f"th{k}", [P, SEQ]) for k in range(2)]
        conv = [sb(f"conv{k}", [P, SEQ]) for k in range(TAPS)]
        gz = sb("gz", [P, IC, SEQ])
        xdt = [sb(f"xdt{u}", [P, INNER]) for u in range(2)]
        xend = [sb(f"xend{u}", [P, INNER]) for u in range(2)]
        btok = [sb(f"btok{u}", [P, STATE]) for u in range(2)]
        gm = [sb(f"gm{u}", [P, P]) for u in range(2)]
        seg_rhs = [sb(f"seg_rhs{u}", [P, HEADS, P]) for u in range(2)]
        eseg = [sb(f"eseg{u}", [P, HEADS, P]) for u in range(2)]
        mix = [sb(f"mix{u}", [P, HEADS, P]) for u in range(2)]
        S = sb("S", [P, INNER])
        yi = sb("yi", [P, INNER])
        yt = [sb(f"yt{u}", [P, INNER]) for u in range(2)]
        y2T = sb("y2T", [P, NC, IC, P])
        sq = [sb(f"sq{u}", [P, IC, P]) for u in range(2)]
        res = sb("res", [P, NC, D])
        fin = sb("fin", [P, NC, D])

        PS = [ctx.enter_context(nc.psum_tensor(f"PS{i}", [P, 512], F32)) for i in range(8)]

        xn_dram = nc.dram_tensor("xn_rows", [TOK, D], F32, kind="Internal").ap()
        y_dram = nc.dram_tensor("y_rows", [KTOP * TOK + SLOT_TILES * P, D], F32, kind="Internal").ap()

        s_x = [sem(f"s_x{g}") for g in range(BATCH)]
        s_wr = sem("s_wr")
        s_par = sem("s_par")
        s_w = sem("s_w")
        s_const = sem("s_const")
        s_prep = sem("s_prep")
        s_w1s = sem("s_w1s")
        s_pool = sem("s_pool")
        s_stats = sem("s_stats")
        s_dve = sem("s_dve")
        s_act = sem("s_act")
        s_xn = sem("s_xn")
        s_xnd = sem("s_xnd")
        s_lnT = sem("s_lnT")
        s_xnt = sem("s_xnt")
        s_small = sem("s_small")
        s_gd = sem("s_gd")
        s_ge = sem("s_ge")
        s_picks = sem("s_picks")
        s_cnt = sem("s_cnt")
        s_bf = sem("s_bf")
        s_ob = sem("s_ob")
        s_ids = sem("s_ids")
        s_idp = sem("s_idp")
        s_te = sem("s_te")
        s_rows = sem("s_rows")
        s_gath = [sem(f"s_gath{u}") for u in range(TRIO)]
        s_sc = [sem(f"s_sc{u}") for u in range(TRIO)]
        s_xt = sem("s_xt")
        s_xtc = sem("s_xtc")
        s_w1 = sem("s_w1")
        s_upa = sem("s_upa")
        s_upb = sem("s_upb")
        s_ra = sem("s_ra")
        s_rb = sem("s_rb")
        s_y = sem("s_y")
        s_yc = sem("s_yc")
        s_yl = [sem(f"s_yl{g}") for g in range(BATCH)]
        s_comb = sem("s_comb")
        s_out = sem("s_out")
        s_sp = sem("s_sp")
        s_spe = sem("s_spe")
        s_la = sem("s_la")
        s_dec = sem("s_dec")
        s_dece = sem("s_dece")
        s_proj = sem("s_proj")
        s_tap = sem("s_tap")
        s_cv = sem("s_cv")
        s_th = sem("s_th")
        s_act_ch = sem("s_act_ch")
        s_segr = sem("s_segr")
        s_tr = sem("s_tr")
        s_trb = sem("s_trb")
        s_seg = sem("s_seg")
        s_bt = sem("s_bt")
        s_es = sem("s_es")
        s_xd = sem("s_xd")
        s_xe = sem("s_xe")
        s_gmm = sem("s_gmm")
        s_mix = sem("s_mix")
        s_yp = sem("s_yp")
        s_u = sem("s_u")
        s_S = sem("s_S")
        s_yt = sem("s_yt")
        s_yT = sem("s_yT")
        s_y2 = sem("s_y2")
        s_sq = sem("s_sq")
        s_o = sem("s_o")
        s_res = sem("s_res")
        block = ctx.enter_context(nc.Block())

        xf = x.rearrange("b s d -> (b s) d").rearrange("(t p) d -> p t d", p=P)
        of = out.rearrange("b s d -> (b s) d").rearrange("(t p) d -> p t d", p=P)
        N_CONST = 11
        N_PARAMS = 12 + 2 * IC
        WR, PARAMS, WEIGHTS = 16 * 2, 16 * N_PARAMS, 16 * 3

        @block.sync
        def _(sp_):
            for g in range(BATCH):
                sp_.dma_start(X[:, g * NC:(g + 1) * NC, :], xf[:, g * NC:(g + 1) * NC, :]).then_inc(s_x[g], 16)
            sp_.dma_start(WrS[:], Wr).then_inc(s_wr, 16)
            sp_.dma_start(BrS[:], br.partition_broadcast(P)).then_inc(s_wr, 16)
            params = [
                (vec_rows[0:NE * HC, :], b1.rearrange("e (c p) -> (e c) p", p=P)),
                (in_rows[:, 0:2, :], in_proj_w[0:INNER, :].rearrange("(c p) d -> p c d", p=P)),
                (in_rows[:, 2:6, :], in_proj_w[INNER:INNER + CONV, :].rearrange("(c p) d -> p c d", p=P)),
                (in_rows_dt[:], in_proj_w[INNER + CONV:INNER + CONV + HEADS, :]),
                (out_rows[:], out_proj_w),
                (cw[:], conv_w.rearrange("(c p) k -> p c k", p=P)),
                (vec_rows[NE * HC:NE * HC + TAPS, :], conv_b.rearrange("(c p) -> c p", p=P)),
                (vec_rows[NE * HC + TAPS:VECS, :], norm_w.rearrange("(c p) -> c p", p=P)),
                (dtb[:], dt_bias.partition_broadcast(P)), (alog[:], A_log.partition_broadcast(P)),
                (lnw[:], ln_w.partition_broadcast(P)), (lnb[:], ln_b.partition_broadcast(P)),
            ]
            params += [(Dch[k * HD:(k + 1) * HD, c:c + 1], D_skip[2 * c + k:2 * c + k + 1].partition_broadcast(HD))
                       for c in range(IC) for k in range(2)]
            assert len(params) == N_PARAMS
            for dst, src in params:
                sp_.dma_start(dst, src).then_inc(s_par, 16)
            for dst, src in (
                (W1S[:, :, 0:HID], W1.rearrange("e d h -> d e h")),
                (W2S[:].rearrange("p e c d -> p (e c) d"), W2.rearrange("e (c p) d -> p (e c) d", p=P)),
                (B2S[:], b2.partition_broadcast(P)),
            ):
                sp_.dma_start(dst, src).then_inc(s_w, 16)
            xn_v = xn_dram.rearrange("(t p) d -> p t d", p=P)
            y_v = y_dram[0:KTOP * TOK, :].rearrange("(k t p) d -> k p t d", p=P, k=KTOP)
            for layer in range(2):
                for g in range(BATCH):
                    sp_.wait_ge(s_xn, 2 * NT * layer + NC * (g + 1))
                    sp_.dma_start(xn_v[:, g * NC:(g + 1) * NC, :], XN[:, g * NC:(g + 1) * NC, :]).then_inc(s_xnd, 16)
                for u in range(TRIO):
                    sp_.wait_ge(s_sc[u], 16 * TURNS * (layer + 1))
                for g in range(BATCH):
                    for k, Y in enumerate((Y1, Y2)):
                        sp_.dma_start(Y[:, g * NC:(g + 1) * NC, :], y_v[k, :, g * NC:(g + 1) * NC, :]).then_inc(s_yl[g], 16)
            for g in range(BATCH):
                sp_.wait_ge(s_comb, BATCH + g + 1)
                sp_.dma_start(of[:, g * NC:(g + 1) * NC, :], X[:, g * NC:(g + 1) * NC, :]).then_inc(s_out, 16)
            sp_.wait_ge(s_out, 16 * BATCH)

        @block.gpsimd
        def _(pool):
            g = nc.gpsimd
            st = Steps(pool, s_pool)
            st.done(g.memset(ident[:], 0.0))
            st.done(g.memset(ones[:], 1.0))
            st.done(g.memset(upto[:], 1.0))
            st.done(g.memset(after[:], 1.0))
            st.done(g.memset(before_bf[:], 1.0))
            st.done(g.memset(ones_bf[:], 1.0))
            st.settle()
            g.affine_select(out=ident[:], in_=ident[:], compare_op=ALU.not_equal, fill=1.0, base=0,
                            pattern=[[-1, P]], channel_multiplier=1).then_inc(s_const, 1)
            g.affine_select(out=upto[:], in_=upto[:], compare_op=ALU.is_ge, fill=0.0, base=0,
                            pattern=[[1, P]], channel_multiplier=-1).then_inc(s_const, 1)
            g.affine_select(out=after[:], in_=after[:], compare_op=ALU.is_gt, fill=0.0, base=0,
                            pattern=[[-1, P]], channel_multiplier=1).then_inc(s_const, 1)
            g.affine_select(out=before_bf[:], in_=before_bf[:], compare_op=ALU.is_gt, fill=0.0, base=0,
                            pattern=[[1, P]], channel_multiplier=-1).then_inc(s_const, 1)
            small = dict(allow_small_or_imprecise_dtypes=True)
            g.iota(iota_e[:], pattern=[[1, NE]], base=0, channel_multiplier=0, **small).then_inc(s_const, 1)
            g.iota(iota_t[:], pattern=[[P, NT]], base=0, channel_multiplier=0, **small).then_inc(s_const, 1)
            g.iota(iota_st[:], pattern=[[1, SLOT_TILES]], base=0, channel_multiplier=0, **small).then_inc(s_const, 1)
            g.iota(iota_p[:], pattern=[[0, 1]], base=0, channel_multiplier=1, **small).then_inc(s_const, 1)
            g.iota(iota_row[:], pattern=[[1, P]], base=0, channel_multiplier=0, **small).then_inc(s_const, 1)
            g.iota(slot_id[:], pattern=[[P, SLOT_TILES]], base=0, channel_multiplier=1, **small).then_inc(s_const, 1)
            g.iota(group_val[:], pattern=[[1, NG]], base=-NG, channel_multiplier=0, **small).then_inc(s_const, 1)

            def experts(layer):
                pool.wait_ge(s_xnd, 16 * BATCH * (layer + 1))
                pool.wait_ge(s_rows, layer + 1)

                def gather(j):
                    u = j % TRIO
                    if j >= TRIO:
                        pool.wait_ge(s_xt, layer * SLOT_TILES + j - TRIO + 1)
                    g.indirect_dma_start(out=XG[u][:], out_offset=None, in_=xn_dram,
                                         in_offset=bass.IndirectOffsetOnAxis(ap=rows_in[:, j:j + 1], axis=0)
                                         ).then_inc(s_gath[u], 16)

                def scatter(j):
                    u = j % TRIO
                    pool.wait_ge(s_yc, layer * SLOT_TILES + j + 1)
                    g.indirect_dma_start(out=y_dram, in_=YS[u][:], in_offset=None,
                                         out_offset=bass.IndirectOffsetOnAxis(ap=rows_out[:, j:j + 1], axis=0)
                                         ).then_inc(s_sc[u], 16)

                ahead = TRIO + 2
                for j in range(ahead):
                    gather(j)
                for j in range(SLOT_TILES):
                    if j + ahead < SLOT_TILES:
                        gather(j + ahead)
                    scatter(j)

            experts(0)
            pool.wait_ge(s_la, 1)

            def batch(b):
                for c in range(NC):
                    if not (isinstance(b, int) and c < 2):
                        pool.wait_ge(s_seg, b * NC + (c - 1))
                    g.tensor_tensor(seg_rhs[c % 2][:], upto[:].unsqueeze(1).broadcast_to([P, HEADS, P]),
                                    row(la, b * NC + c).unsqueeze(2).broadcast_to([P, HEADS, P]),
                                    ALU.mult).then_inc(s_segr, 1)

            batch(0)
            with pool.Fori(1, BATCH) as b:
                batch(b)
            experts(1)

        @block.tensor
        def _(pe):
            mm = nc.tensor.matmul

            def norm_project(n, rhs, width):
                def small(g):
                    pe.wait_ge(s_xnt, BATCH * n + g + 1)
                    for t in range(g * NC, (g + 1) * NC):
                        last = mm(PS[2][:, t * width:(t + 1) * width], XNT[:, t * P:(t + 1) * P], rhs,
                                  start=True, stop=True)
                    return last

                for g in range(BATCH):
                    pe.wait_ge(s_xn, NT * n + (g + 1) * NC)
                    if g >= 2:
                        pe.wait_ge(s_xnt, BATCH * n + g - 1)
                    for c in range(NC):
                        last = nc.tensor.transpose(PS[g % 2][:, c * P:(c + 1) * P], XN[:, g * NC + c, :], ident[:])
                    last.then_inc(s_lnT, 1)
                    if g:
                        small(g - 1)
                small(BATCH - 1).then_inc(s_small, 1)

            def weights():
                pe.wait_ge(s_par, PARAMS)
                for c in range(4):
                    nc.tensor.transpose(PS[6][:, c * P:(c + 1) * P], in_rows[:, c, :], ident[:])
                for c in range(2):
                    nc.tensor.transpose(PS[7][:, c * P:(c + 1) * P], in_rows[:, 4 + c, :], ident[:])
                nc.tensor.transpose(PS[7][:, 256:256 + HEADS], in_rows_dt[:], ident[0:HEADS, 0:HEADS])
                nc.tensor.transpose(PS[7][:, 260:260 + VECS], vec_rows[:], ident[0:VECS, 0:VECS])
                for c in range(IC):
                    last = nc.tensor.transpose(PS[5][:, c * P:(c + 1) * P], out_rows[:, c * P:(c + 1) * P], ident[:])
                last.then_inc(s_prep, 1)

            def experts(layer):
                pe.wait_ge(s_picks, layer + 1)
                mm(PS[3][:, 0:NT * NE], before_bf[:], picks_bf[:], start=True, stop=True)
                mm(PS[4][:, 0:NT * NE], ones_bf[:], picks_bf[:], start=True, stop=True).then_inc(s_cnt, 1)
                pe.wait_ge(s_w1s, 1)
                pe.wait_ge(s_ids, layer + 1)
                for q in range(NG):
                    pe.wait_ge(s_ob, NG * layer + q + 1)
                    last = mm(PS[5][:, 0:2 * SLOT_TILES], onehot_b[:, q, :], rhs_ids[:, q, :, :].rearrange("p a b -> p (a b)"),
                              start=(q == 0), stop=(q == NG - 1))
                last.then_inc(s_idp, 1)
                pe.wait_ge(s_te, layer + 1)
                B0 = layer * SLOT_TILES

                pe.wait_ge(s_w, WEIGHTS)

                def turned(turn, u):
                    j = turn * TRIO + u
                    pe.wait_ge(s_gath[u], 16 * (layer * TURNS + turn + 1))
                    if not (early(turn) and u == 0):
                        pe.wait_ge(s_xtc, B0 + j)
                    nc.tensor.transpose(PS[0][:, 0:P], XG[u][:], ident[:]).then_inc(s_xt, 1)

                def up(turn, u):
                    j = turn * TRIO + u
                    pe.wait_ge(s_xtc, B0 + j + 1)
                    pe.wait_ge(s_w1, B0 + j + 1)
                    for half, ready in enumerate((s_upa, s_upb)):
                        for c in range(2):
                            h = 2 * half + c
                            last = mm(PS[2 + TRIO * half + u][:, c * P:(c + 1) * P], W1B[u][:, h * P:(h + 1) * P],
                                      XT[u][:], start=True, stop=True)
                        last.then_inc(ready, 1)

                def down(turn, u):
                    j = turn * TRIO + u
                    e = pe.value_load(te_i[0:1, ds(j, 1)], min_val=0, max_val=NE - 1)
                    pe.wait_ge(s_ra, B0 + j + 1)
                    pe.wait_ge(s_rb, B0 + j + 1)
                    if not (early(turn) and u == 0):
                        pe.wait_ge(s_yc, B0 + j)
                    for c in range(HC):
                        last = mm(PS[1][:, 0:D], H[u][:, c, :], W2S[:, ds(e, 1), c, :].rearrange("p a d -> p (a d)"),
                                  start=(c == 0), stop=(c == HC - 1))
                    last.then_inc(s_y, 1)

                in_steps(pe, {2: turned, 1: up, 0: down})

            def mixer():
                pe.wait_ge(s_la, 1)
                flat = la[:].rearrange("p t h -> p (t h)")
                for k, m in enumerate((upto, after, ones)):
                    last = mm(PS[3][:, k * NT * HEADS:(k + 1) * NT * HEADS], m[:], flat, start=True, stop=True)
                last.then_inc(s_dec, 1)
                pe.wait_ge(s_dece, 1)

                def batch(b):
                    first = isinstance(b, int)

                    def s1(c):
                        q = b * NC + c
                        tile = slice(c * P, (c + 1) * P)
                        if not (first and c == 0):
                            pe.wait_ge(s_gmm, q)
                        for i in range(IC):
                            nc.tensor.transpose(PS[2][:, i * P:(i + 1) * P], conv[i][:, tile], ident[:])
                        mm(PS[2][:, 2 * P:3 * P], conv[2][:, tile], conv[3][:, tile], start=True,
                           stop=True).then_inc(s_tr, 1)
                        if c < NC - 1:
                            if not (first and c == 0):
                                pe.wait_ge(s_bt, b * (NC - 1) + c)
                            nc.tensor.transpose(PS[3][:, 0:P], conv[2][:, tile], ident[:]).then_inc(s_trb, 1)
                        pe.wait_ge(s_segr, q + 1)
                        if not (first and c == 0):
                            pe.wait_ge(s_es, q)
                        mm(PS[5][:], after[:], seg_rhs[c % 2][:].rearrange("p h t -> p (h t)"), start=True,
                           stop=True).then_inc(s_seg, 1)

                    def s2(c):
                        q = b * NC + c
                        tile = slice(c * P, (c + 1) * P)
                        u = c % 2
                        if not (first and c == 0):
                            pe.wait_ge(s_yt, q)
                        for i in range(IC):
                            mm(PS[6][:, i * P:(i + 1) * P], conv[i][:, tile], diagD[:, i, :], start=(i == 0),
                               stop=False, skip_group_check=True)
                        pe.wait_ge(s_mix, q + 1)
                        pe.wait_ge(s_xd, q + 1)
                        for h in range(HEADS):
                            last = mm(PS[6][:, h * HD:(h + 1) * HD], mix[u][:, h, :], xdt[u][:, h * HD:(h + 1) * HD],
                                      start=False, stop=True, skip_group_check=True)
                        if c:
                            pe.wait_ge(s_S, b * (NC - 1) + c)
                            last = mm(PS[6][:, INNER:2 * INNER], conv[3][:, tile], S[:], start=True, stop=True,
                                      skip_group_check=True)
                        last.then_inc(s_yp, 1)
                        if c < NC - 1:
                            pe.wait_ge(s_bt, b * (NC - 1) + c + 1)
                            pe.wait_ge(s_xe, b * (NC - 1) + c + 1)
                            if not (first and c == 0):
                                pe.wait_ge(s_S, b * (NC - 1) + c)
                            mm(PS[7][:, 0:INNER], btok[u][:], xend[u][:], start=True, stop=True).then_inc(s_u, 1)

                    def s3(c):
                        q = b * NC + c
                        pe.wait_ge(s_yt, q + 1)
                        if not (first and c == 0):
                            pe.wait_ge(s_y2, q)
                        for i in range(IC):
                            last = nc.tensor.transpose(PS[4][:, i * P:(i + 1) * P], yt[c % 2][:, i * P:(i + 1) * P], ident[:])
                        last.then_inc(s_yT, 1)

                    def s4(c):
                        q = b * NC + c
                        if c == 0:
                            pe.wait_ge(s_cv, (b + 1) * 6)
                        pe.wait_ge(s_y2, q + 1)
                        for i in range(IC):
                            mm(PS[0][:, c * P:(c + 1) * P], y2T[:, c, i, :], WoT[:, i, :], start=(i == 0), stop=(i == IC - 1))
                        pe.wait_ge(s_sq, q + 1)
                        for i in range(IC):
                            last = mm(PS[1][:, c:c + 1], sq[c % 2][:, i, :], ones[:, 0:1], start=(i == 0), stop=(i == IC - 1))
                        last.then_inc(s_o, 1)

                    for m, k in enumerate(BLOCKS):
                        if m < 2:
                            if not first:
                                pe.wait_ge(s_res, b)
                        else:
                            pe.wait_ge(s_cv, b * 6 + (m - 1))
                        w0 = X0 + k * P if k < TAPS else Z0 + (k - TAPS) * P
                        mm(PS[m % 2][:], WT[:, w0:w0 + P], XNT[:, ds(b * SEQ, SEQ)], start=True,
                           stop=True).then_inc(s_proj, 1)
                    pe.wait_ge(s_act_ch, (b + 1) * TAPS)
                    s1(0)
                    for c in range(NC):
                        if c + 1 < NC:
                            s1(c + 1)
                        s2(c)
                        if c:
                            s3(c - 1)
                        if c > 1:
                            s4(c - 2)
                    s3(NC - 1)
                    s4(NC - 2)
                    s4(NC - 1)

                batch(0)
                with pe.Fori(1, BATCH) as b:
                    batch(b)

            pe.wait_ge(s_const, N_CONST)
            pe.wait_ge(s_wr, WR)
            norm_project(0, WrS[:], NE)
            weights()
            experts(0)
            norm_project(1, WT[:, DT0:DT0 + HEADS], HEADS)
            mixer()
            norm_project(2, WrS[:], NE)
            experts(1)

        @block.scalar
        def _(act):
            A = nc.scalar.activation
            st = Steps(act, s_act)

            def norm_project(n):
                for g in range(BATCH):
                    act.wait_ge(s_lnT, BATCH * n + g + 1)
                    A(XNT[:, g * SEQ:(g + 1) * SEQ], PS[g % 2][:], ACT.Copy).then_inc(s_xnt, 1)

            def weights():
                act.wait_ge(s_prep, 1)
                act.wait_ge(s_par, PARAMS)
                st.done(A(WT[:, Z0:Z0 + INNER], PS[6][:, 0:INNER], ACT.Copy))
                st.done(A(WT[:, X0:X0 + INNER], PS[6][:, INNER:2 * INNER], ACT.Copy))
                st.done(A(WT[:, X0 + INNER:X0 + CONV], PS[7][:, 0:2 * P], ACT.Copy))
                st.done(A(WT[:, DT0:DT0 + HEADS], PS[7][:, 256:256 + HEADS], ACT.Copy))
                st.done(A(W1S[:, :, HID:W1W], PS[7][:, 260:260 + NE * HC].rearrange("p (e c) -> p e c", e=NE), ACT.Copy))
                st.done(A(cb[:], PS[7][:, 260 + NE * HC:260 + NE * HC + TAPS], ACT.Copy))
                st.done(A(nw[:], PS[7][:, 260 + NE * HC + TAPS:260 + VECS], ACT.Copy))
                st.done(A(expA[:], alog[:], ACT.Exp))
                st.settle()
                st.done(A(WoT[:, 0, :], PS[5][:, 0:P], ACT.Copy, scale=nw[:, 0:1]))
                st.settle()
                A(WoT[:, 1, :], PS[5][:, P:2 * P], ACT.Copy, scale=nw[:, 1:2]).then_inc(s_w1s, 1)

            def experts(layer):
                act.wait_ge(s_gd, layer + 1)
                A(ge[:], gd[:], ACT.Exp).then_inc(s_ge, 1)
                act.wait_ge(s_te, layer + 1)
                act.wait_ge(s_w1s, 1)
                B0 = layer * SLOT_TILES

                act.wait_ge(s_w, WEIGHTS)

                def weights_of(turn, u):
                    j = turn * TRIO + u
                    e = act.value_load(te_i[0:1, ds(j, 1)], min_val=0, max_val=NE - 1)
                    if not early(turn):
                        act.wait_ge(s_upb, B0 + j - TRIO + 1)
                        act.wait_ge(s_ra, B0 + j - TRIO + 1)
                        act.wait_ge(s_rb, B0 + j - TRIO + 1)
                    A(W1B[u][:], W1S[:, ds(e, 1), :].rearrange("p a h -> p (a h)"), ACT.Copy).then_inc(s_w1, 1)

                def relu(turn, u):
                    j = turn * TRIO + u
                    act.wait_ge(s_upb, B0 + j + 1)
                    act.wait_ge(s_w1, B0 + j + 1)
                    if not early(turn):
                        act.wait_ge(s_y, B0 + j - TRIO + 1)
                    for c in range(2):
                        last = A(H[u][:, 2 + c, :], PS[2 + TRIO + u][:, c * P:(c + 1) * P], ACT.Relu,
                                 bias=W1B[u][:, HID + 2 + c:HID + 3 + c])
                    last.then_inc(s_rb, 1)

                in_steps(act, {2: weights_of, 1: relu})

            def mixer():
                act.wait_ge(s_sp, 1)
                A(sp[1][:], sp[0][:], ACT.Exp, scale=-1.0).then_inc(s_spe, 1)
                act.wait_ge(s_dec, 1)
                A(decay[:].rearrange("p k t h -> p (k t h)"), PS[3][:, 0:3 * NT * HEADS], ACT.Exp).then_inc(s_dece, 1)

                def batch(b):
                    first = isinstance(b, int)

                    def tanh(m):
                        if m < 2:
                            if not first:
                                act.wait_ge(s_cv, b * 6 + (m - 1))
                        else:
                            act.wait_ge(s_act_ch, b * TAPS + (m - 1))
                        if m < TAPS:
                            act.wait_ge(s_cv, b * 6 + (m + 1))
                            A(th[m % 2][:], acc[m % 2][:], ACT.Tanh).then_inc(s_th, 1)
                        else:
                            act.wait_ge(s_proj, b * 6 + (m + 1))
                            A(th[m % 2][:], PS[m % 2][:], ACT.Tanh, scale=0.5).then_inc(s_th, 1)

                    for m, k in enumerate(BLOCKS[0:TAPS]):
                        act.wait_ge(s_proj, b * 6 + (m + 1))
                        if not (first and m < 2):
                            act.wait_ge(s_act_ch, b * TAPS + (m - 1))
                        A(acc[m % 2][:], PS[m % 2][:], ACT.Identity, bias=cbh[:, k:k + 1],
                          scale=cwh[:, k, TAPS - 1:TAPS]).then_inc(s_tap, 1)
                        if m:
                            tanh(m - 1)
                    tanh(TAPS - 1)
                    tanh(TAPS)
                    tanh(TAPS + 1)

                    def chunk(c):
                        q = b * NC + c
                        u = c % 2
                        if c < NC - 1:
                            act.wait_ge(s_trb, b * (NC - 1) + (c + 1))
                            if c >= 2:
                                act.wait_ge(s_u, b * (NC - 1) + (c - 1))
                            elif not first:
                                act.wait_ge(s_u, b * (NC - 1))
                            A(btok[u][:], PS[3][:, 0:P], ACT.Copy).then_inc(s_bt, 1)
                        act.wait_ge(s_seg, q + 1)
                        if not (first and c < 2):
                            act.wait_ge(s_mix, q - 1)
                        A(eseg[u][:].rearrange("p h t -> p (h t)"), PS[5][:], ACT.Exp).then_inc(s_es, 1)

                    def squares(c):
                        q = b * NC + c
                        act.wait_ge(s_y2, q + 1)
                        if not (first and c < 2):
                            act.wait_ge(s_o, q - 1)
                        A(sq[c % 2][:], y2T[:, c, :, :], ACT.Square).then_inc(s_sq, 1)

                    chunk(0)
                    chunk(1)
                    for c in range(NC):
                        if c + 2 < NC:
                            chunk(c + 2)
                        squares(c)

                batch(0)
                with act.Fori(1, BATCH) as b:
                    batch(b)

            norm_project(0)
            weights()
            experts(0)
            norm_project(1)
            mixer()
            norm_project(2)
            experts(1)

        @block.vector
        def _(dve):
            v = nc.vector
            st = Steps(dve, s_dve)

            def rsqrt(r, val, tmp):
                st.link(v.tensor_scalar(r.bitcast(I32), val.bitcast(I32), -0.5, RSQRT_SEED, ALU.mult, ALU.add))
                for _ in range(3):
                    st.link(v.tensor_tensor(tmp, r, r, ALU.mult))
                    st.link(v.scalar_tensor_tensor(out=tmp, in0=tmp, scalar=-0.5, in1=val, op0=ALU.mult, op1=ALU.mult))
                    st.link(v.scalar_tensor_tensor(out=r, in0=tmp, scalar=1.5, in1=r, op0=ALU.add, op1=ALU.mult))

            def norm(n):
                for t in range(NT):
                    if n == 0 and t % NC == 0:
                        dve.wait_ge(s_x[t // NC], 16)
                    st.done(v.bn_stats(stats[:, t, :], X[:, t, :]))
                st.settle()
                for t in range(NT):
                    st.done(v.bn_aggr(mv[:, t, :], stats[:, t, :]))
                st.settle()
                st.link(v.tensor_scalar(rv[:], mv[:, :, 1], EPS, None, ALU.add))
                rsqrt(rs[:], rv[:], rt[:])
                if n == 1:
                    dve.wait_ge(s_xnd, 16 * BATCH)
                for t in range(NT):
                    v.tensor_scalar(XN[:, t, :], X[:, t, :], mv[:, t, 0:1], rs[:, t:t + 1],
                                    ALU.subtract, ALU.mult).then_inc(s_xn, 1)

            def parameters():
                dve.wait_ge(s_par, PARAMS)
                dve.wait_ge(s_w1s, 1)
                st.done(v.tensor_scalar(cwh[:].rearrange("p c k -> p (c k)"), cw[:].rearrange("p c k -> p (c k)"), 0.5, None, ALU.mult))
                st.done(v.tensor_scalar(cbh[:], cb[:], 0.5, None, ALU.mult))
                for c in range(IC):
                    st.done(v.tensor_scalar(diagD[:, c, :], ident[:], Dch[:, c:c + 1], None, ALU.mult))
                st.settle()

            def route(layer):
                dve.wait_ge(s_small, 2 * layer + 1)
                st.link(v.tensor_tensor(lg[:], PS[2][:, 0:NT * NE].rearrange("p (t e) -> p t e", e=NE),
                                        BrS[:].unsqueeze(1).broadcast_to([P, NT, NE]), ALU.add))
                for t in range(NT):
                    st.done(v.max(top[:, t, :], lg[:, t, :]))
                st.settle()
                for t in range(NT):
                    st.done(v.max_index(topi[:, t, :], top[:, t, :], lg[:, t, :]))
                v.tensor_tensor(gd[:], top[:, :, 1], top[:, :, 0], ALU.subtract).then_inc(s_gd, 1)
                st.settle()
                st.link(v.tensor_copy(topf[:], topi[:, :, 0:KTOP]))
                for k in range(KTOP):
                    st.done(v.tensor_tensor(pick[:, k, :, :], iota_e[:].unsqueeze(1).broadcast_to([P, NT, NE]),
                                            topf[:, :, k:k + 1].broadcast_to([P, NT, NE]), ALU.is_equal))
                st.settle()
                v.tensor_tensor(picks_bf[:].rearrange("p (t e) -> p t e", e=NE), pick[:, 0, :, :], pick[:, 1, :, :],
                                ALU.add).then_inc(s_picks, 1)
                dve.wait_ge(s_ge, layer + 1)
                st.link(v.tensor_scalar(gr[:], ge[:], 2.0, 2.0, ALU.mult, ALU.add))
                st.link(v.reciprocal(gate[:, 0, :], gr[:]))
                st.done(v.tensor_tensor(gate[:, 1, :], gate[:, 0, :], ge[:], ALU.mult))
                dve.wait_ge(s_cnt, layer + 1)
                st.link(v.tensor_copy(cnt[:], PS[4][:, 0:NT * NE].rearrange("p (t e) -> p e t", e=NE)))
                st.link(v.tensor_tensor_scan(run[:].rearrange("p e t -> p (e t)"), ones[:, 0:NT * NE],
                                             cnt[:].rearrange("p e t -> p (e t)"), 0.0, ALU.mult, ALU.add))
                st.link(v.tensor_tensor(excl[:], run[:], cnt[:], ALU.subtract))
                st.link(v.tensor_tensor(n_e[:], run[:, :, NT - 1], excl[:, :, 0], ALU.subtract))
                st.link(v.tensor_tensor(cmp16[:], n_e[:].unsqueeze(2).broadcast_to([P, NE, NT]),
                                        iota_t[:].unsqueeze(1).broadcast_to([P, NE, NT]), ALU.is_gt))
                st.link(v.tensor_reduce(tiles_e[:], cmp16[:], AX.X, ALU.add))
                st.link(v.tensor_tensor_scan(end_e[:], ones[:, 0:NE], tiles_e[:], 0.0, ALU.mult, ALU.add))
                st.link(v.tensor_tensor(adj[:], end_e[:], tiles_e[:], ALU.subtract))
                st.link(v.scalar_tensor_tensor(out=adj[:], in0=adj[:], scalar=float(P), in1=excl[:, :, 0],
                                               op0=ALU.mult, op1=ALU.subtract))
                st.link(v.tensor_tensor(base[:], excl[:], adj[:].unsqueeze(2).broadcast_to([P, NE, NT]), ALU.add))
                st.link(v.tensor_tensor(slot_all[:], PS[3][:, 0:NT * NE].rearrange("p (t e) -> p t e", e=NE),
                                        base[:].rearrange("p e t -> p t e"), ALU.add))
                for k in range(KTOP):
                    st.done(v.tensor_tensor(slot_pick[:, k, :, :], pick[:, k, :, :], slot_all[:], ALU.mult))
                st.settle()
                st.link(v.tensor_reduce(slot[:], slot_pick[:].rearrange("p k t e -> p (k t) e"), AX.X, ALU.add))
                st.link(v.tensor_copy(slot_i[:], slot[:]))
                st.done(v.tensor_scalar(a_i[:], slot_i[:], 7, None, ALU.logical_shift_right))
                st.done(v.tensor_scalar(b_i[:], slot_i[:], P - 1, None, ALU.bitwise_and))
                st.settle()
                v.tensor_copy(b_f[:], b_i[:]).then_inc(s_bf, 1)
                st.link(v.tensor_copy(a_f[:], a_i[:]))
                dve.wait_ge(s_bf, layer + 1)
                st.done(v.tensor_tensor(val_g[:], group_val[:], a_f[:], ALU.subtract))
                st.done(v.tensor_scalar(val_p[:], b_f[:], -1.0, iota_p[:, 0:1], ALU.mult, ALU.add))
                st.link(v.tensor_tensor(onehot_a[:], iota_st[:].unsqueeze(1).broadcast_to([P, NG, SLOT_TILES]),
                                        a_f[:].unsqueeze(2).broadcast_to([P, NG, SLOT_TILES]), ALU.is_equal))
                st.done(v.tensor_tensor(rhs_ids[:, :, 0, :], onehot_a[:],
                                        val_g[:].unsqueeze(2).broadcast_to([P, NG, SLOT_TILES]), ALU.mult))
                st.settle()
                v.tensor_tensor(rhs_ids[:, :, 1, :], onehot_a[:],
                                val_p[:].unsqueeze(2).broadcast_to([P, NG, SLOT_TILES]), ALU.mult).then_inc(s_ids, 1)
                st.link(v.tensor_tensor(te_cmp[:], iota_st[:].unsqueeze(2).broadcast_to([P, SLOT_TILES, NE]),
                                        end_e[:].unsqueeze(1).broadcast_to([P, SLOT_TILES, NE]), ALU.is_ge))
                st.link(v.tensor_reduce(te_f[:], te_cmp[:], AX.X, ALU.add))
                v.tensor_scalar(te_i[:], te_f[:], float(NE - 1), None, ALU.min).then_inc(s_te, 1)
                for q in range(NG):
                    v.tensor_scalar(onehot_b[:, q, :], iota_row[:], b_f[:, q:q + 1], None,
                                    ALU.is_equal).then_inc(s_ob, 1)
                dve.wait_ge(s_idp, layer + 1)
                st.link(v.scalar_tensor_tensor(out=ids_f[:], in0=PS[5][:, 0:SLOT_TILES], scalar=float(P), in1=slot_id[:],
                                               op0=ALU.mult, op1=ALU.add))
                st.link(v.scalar_tensor_tensor(out=rows_out[:], in0=PS[5][:, SLOT_TILES:2 * SLOT_TILES], scalar=float(KTOP * TOK),
                                               in1=ids_f[:], op0=ALU.add, op1=ALU.add))
                v.tensor_scalar(rows_in[:], rows_out[:], TOK - 1, None, ALU.bitwise_and).then_inc(s_rows, 1)

            def experts(layer):
                B0 = layer * SLOT_TILES
                dve.wait_ge(s_te, layer + 1)

                dve.wait_ge(s_w, WEIGHTS)

                def copy_xt(turn, u):
                    j = turn * TRIO + u
                    dve.wait_ge(s_xt, B0 + j + 1)
                    if not early(turn):
                        dve.wait_ge(s_upb, B0 + j - TRIO + 1)
                    v.tensor_copy(XT[u][:], PS[0][:, 0:P]).then_inc(s_xtc, 1)

                def relu(turn, u):
                    j = turn * TRIO + u
                    dve.wait_ge(s_upa, B0 + j + 1)
                    dve.wait_ge(s_w1, B0 + j + 1)
                    for c in range(2):
                        last = v.tensor_scalar(H[u][:, c, :], PS[2 + u][:, c * P:(c + 1) * P],
                                               W1B[u][:, HID + c:HID + c + 1], 0.0, ALU.add, ALU.max)
                    last.then_inc(s_ra, 1)

                def add_bias(turn, u):
                    j = turn * TRIO + u
                    e = dve.value_load(te_i[0:1, ds(j, 1)], min_val=0, max_val=NE - 1)
                    dve.wait_ge(s_y, B0 + j + 1)
                    if not early(turn):
                        dve.wait_ge(s_sc[u], 16 * (layer * TURNS + turn))
                    v.tensor_tensor(YS[u][:], PS[1][:, 0:D], row(B2S, e), ALU.add).then_inc(s_yc, 1)

                in_steps(dve, {2: copy_xt, 1: relu, 0: add_bias})
                for g in range(BATCH):
                    dve.wait_ge(s_yl[g], 32 * (layer + 1))
                    for t in range(g * NC, (g + 1) * NC):
                        st.done(v.scalar_tensor_tensor(out=X[:, t, :], in0=Y1[:, t, :], scalar=gate[:, 0, t:t + 1],
                                                       in1=X[:, t, :], op0=ALU.mult, op1=ALU.add))
                    st.settle()
                    for t in range(g * NC, (g + 1) * NC):
                        last = v.scalar_tensor_tensor(out=X[:, t, :], in0=Y2[:, t, :], scalar=gate[:, 1, t:t + 1],
                                                      in1=X[:, t, :], op0=ALU.mult, op1=ALU.add)
                    last.then_inc(s_comb, 1)
                dve.wait_ge(s_comb, BATCH * (layer + 1))

            def time_steps():
                dve.wait_ge(s_small, 2)
                st.link(v.tensor_tensor(dtr[:], PS[2][:, 0:NT * HEADS].rearrange("p (t h) -> p t h", h=HEADS),
                                        dtb[:].unsqueeze(1).broadcast_to([P, NT, HEADS]), ALU.add))
                v.scalar_tensor_tensor(out=sp[0][:], in0=dtr[:], scalar=-1.0, in1=dtr[:], op0=ALU.mult,
                                       op1=ALU.max).then_inc(s_sp, 1)
                dve.wait_ge(s_spe, 1)
                e, z, z2, p = sp[1][:], sp[2][:], sp[3][:], sp[4][:]
                st.link(v.tensor_scalar(z2, e, 2.0, None, ALU.add))
                st.link(v.reciprocal(z, z2))
                st.link(v.tensor_tensor(z, z, e, ALU.mult))
                st.link(v.tensor_tensor(z2, z, z, ALU.mult))
                st.link(v.tensor_scalar(p, z2, 1.0 / 17, None, ALU.mult))
                for k in (15, 13, 11, 9, 7, 5, 3):
                    st.link(v.scalar_tensor_tensor(out=p, in0=p, scalar=1.0 / k, in1=z2, op0=ALU.add, op1=ALU.mult))
                st.link(v.scalar_tensor_tensor(out=p, in0=p, scalar=1.0, in1=z, op0=ALU.add, op1=ALU.mult))
                st.link(v.tensor_scalar(z, dtr[:], 0.0, None, ALU.max))
                st.link(v.scalar_tensor_tensor(out=dt[:], in0=p, scalar=2.0, in1=z, op0=ALU.mult, op1=ALU.add))
                dve.wait_ge(s_w1s, 1)
                st.link(v.tensor_tensor(la[:], dt[:], expA[:].unsqueeze(1).broadcast_to([P, NT, HEADS]), ALU.mult))
                v.tensor_scalar(la[:], la[:], -1.0, LEAST_DECAY, ALU.mult, ALU.max).then_inc(s_la, 1)
                dve.wait_ge(s_dece, 1)
                st.link(v.tensor_tensor(dtd[:], dt[:], decay[:, 1, :, :], ALU.mult))

            def mixer():
                time_steps()

                def by_head(tensor, q):
                    return row(tensor, q).unsqueeze(2).broadcast_to([P, HEADS, HD])

                def heads(ap):
                    return ap.rearrange("p (h d) -> p h d", h=HEADS)

                def batch(b):
                    first = isinstance(b, int)

                    def taps(m, k):
                        dve.wait_ge(s_tap, b * TAPS + (m + 1))
                        for j in range(TAPS - 1):
                            back = TAPS - 1 - j
                            last = v.scalar_tensor_tensor(out=acc[m % 2][:, back:SEQ], in0=PS[m % 2][:, 0:SEQ - back],
                                                          scalar=cwh[:, k, j:j + 1], in1=acc[m % 2][:, back:SEQ],
                                                          op0=ALU.mult, op1=ALU.add)
                            if j < TAPS - 2:
                                st.link(last)
                        last.then_inc(s_cv, 1)

                    def activate(m, k):
                        dve.wait_ge(s_th, b * 6 + (m + 1))
                        if m == 0 and not first:
                            dve.wait_ge(s_yp, b * NC)
                            dve.wait_ge(s_seg, b * NC)
                        dve.wait_ge(s_cv, b * 6 + (m + 1))
                        v.scalar_tensor_tensor(out=conv[k][:], in0=th[m % 2][:], scalar=1.0, in1=acc[m % 2][:],
                                               op0=ALU.add, op1=ALU.mult).then_inc(s_act_ch, 1)

                    for m, k in enumerate(BLOCKS[0:TAPS]):
                        taps(m, k)
                        if m:
                            activate(m - 1, BLOCKS[m - 1])
                    activate(TAPS - 1, BLOCKS[TAPS - 1])
                    for m in (TAPS, TAPS + 1):
                        dve.wait_ge(s_th, b * 6 + (m + 1))
                        v.scalar_tensor_tensor(out=gz[:, m - TAPS, :], in0=th[m % 2][:], scalar=1.0, in1=PS[m % 2][:],
                                               op0=ALU.add, op1=ALU.mult).then_inc(s_cv, 1)

                    def d1(c):
                        q = b * NC + c
                        u = c % 2
                        dve.wait_ge(s_tr, q + 1)
                        if not (first and c < 2):
                            dve.wait_ge(s_yp, q - 1)
                        v.tensor_tensor(heads(xdt[u][:]), heads(PS[2][:, 0:INNER]), by_head(dt, q),
                                        ALU.mult).then_inc(s_xd, 1)
                        if c < NC - 1:
                            if c >= 2:
                                dve.wait_ge(s_u, b * (NC - 1) + (c - 1))
                            elif not first:
                                dve.wait_ge(s_u, b * (NC - 1))
                            v.tensor_tensor(heads(xend[u][:]), heads(PS[2][:, 0:INNER]), by_head(dtd, q),
                                            ALU.mult).then_inc(s_xe, 1)
                        v.tensor_tensor(gm[u][:], PS[2][:, INNER:INNER + P], upto[:], ALU.mult).then_inc(s_gmm, 1)
                        dve.wait_ge(s_gmm, q + 1)
                        dve.wait_ge(s_es, q + 1)
                        v.tensor_tensor(mix[u][:], eseg[u][:], gm[u][:].unsqueeze(1).broadcast_to([P, HEADS, P]),
                                        ALU.mult).then_inc(s_mix, 1)

                    def d2(c):
                        q = b * NC + c
                        u = c % 2
                        dve.wait_ge(s_yp, q + 1)
                        if c < NC - 1:
                            dve.wait_ge(s_u, b * (NC - 1) + (c + 1))
                            if c:
                                st.link(v.tensor_tensor(heads(S[:]), heads(S[:]),
                                                        decay[:, 2, ds(q, 1), :].rearrange("p a h -> p (a h)")
                                                        .unsqueeze(2).broadcast_to([P, HEADS, HD]), ALU.mult))
                                v.tensor_tensor(S[:], S[:], PS[7][:, 0:INNER], ALU.add).then_inc(s_S, 1)
                            else:
                                v.tensor_copy(S[:], PS[7][:, 0:INNER]).then_inc(s_S, 1)
                            dve.wait_ge(s_S, b * (NC - 1) + (c + 1))
                        if not (first and c < 2):
                            dve.wait_ge(s_yT, q - 1)
                        if c:
                            st.link(v.tensor_tensor(heads(yi[:]), heads(PS[6][:, INNER:2 * INNER]),
                                                    decay[:, 0, ds(q, 1), :].rearrange("p a h -> p (a h)")
                                                    .unsqueeze(2).broadcast_to([P, HEADS, HD]), ALU.mult))
                            v.tensor_tensor(yt[u][:], yi[:], PS[6][:, 0:INNER], ALU.add).then_inc(s_yt, 1)
                        else:
                            v.tensor_copy(yt[u][:], PS[6][:, 0:INNER]).then_inc(s_yt, 1)

                    def d3(c):
                        q = b * NC + c
                        dve.wait_ge(s_yT, q + 1)
                        if c == 0:
                            dve.wait_ge(s_cv, (b + 1) * 6)
                            if not first:
                                dve.wait_ge(s_o, b * NC)
                        v.tensor_tensor(y2T[:, c, :, :], PS[4][:, 0:INNER].rearrange("p (i t) -> p i t", i=IC),
                                        gz[:, :, c * P:(c + 1) * P], ALU.mult).then_inc(s_y2, 1)

                    d1(0)
                    for c in range(NC):
                        if c + 1 < NC:
                            d1(c + 1)
                        d2(c)
                        if c:
                            d3(c - 1)
                    d3(NC - 1)

                    dve.wait_ge(s_o, (b + 1) * NC)
                    st.link(v.tensor_scalar(rv[:, 0:NC], PS[1][:, 0:NC], 0.25 / INNER, EPS, ALU.mult, ALU.add))
                    rsqrt(rs[:, 0:NC], rv[:, 0:NC], rt[:, 0:NC])
                    st.link(v.tensor_scalar(rs[:, 0:NC], rs[:, 0:NC], 0.5, None, ALU.mult))
                    for c in range(NC):
                        last = v.scalar_tensor_tensor(out=res[:, c, :], in0=PS[0][:, c * P:(c + 1) * P],
                                                      scalar=rs[:, c:c + 1], in1=row(XN, b * NC + c),
                                                      op0=ALU.mult, op1=ALU.add)
                        if c < NC - 1:
                            st.done(last)
                    last.then_inc(s_res, 1)
                    st.settle()
                    dve.wait_ge(s_res, b + 1)
                    for c in range(NC):
                        st.done(v.bn_stats(stats[:, c, :], res[:, c, :]))
                    st.settle()
                    dve.sem_inc(s_stats, 1)
                    for c in range(NC):
                        st.done(v.bn_aggr(mv[:, c, :], stats[:, c, :]))
                    st.settle()
                    st.link(v.tensor_scalar(rv[:, 0:NC], mv[:, 0:NC, 1], EPS, None, ALU.add))
                    rsqrt(rs[:, 0:NC], rv[:, 0:NC], rt[:, 0:NC])
                    xb = X[:, ds(b * NC, NC), :]
                    for c in range(NC):
                        st.done(v.tensor_scalar(fin[:, c, :], res[:, c, :], mv[:, c, 0:1], rs[:, c:c + 1],
                                                ALU.subtract, ALU.mult))
                    st.link(v.tensor_tensor(xb, xb, lnb[:].unsqueeze(1).broadcast_to([P, NC, D]), ALU.add))
                    st.link(v.tensor_tensor(fin[:], fin[:], lnw[:].unsqueeze(1).broadcast_to([P, NC, D]), ALU.mult))
                    st.link(v.tensor_tensor(xb, xb, fin[:], ALU.add))

                before = st.n
                batch(0)
                steps = st.n - before
                with dve.Fori(1, BATCH) as b:
                    st.enter(b - 1, steps)
                    batch(b)
                    st.leave(BATCH - 1)

            norm(0)
            dve.wait_ge(s_wr, WR)
            dve.wait_ge(s_const, N_CONST)
            route(0)
            experts(0)
            parameters()
            norm(1)
            mixer()
            norm(2)
            route(1)
            experts(1)


_INS = ["L0_attn_x", "L0_attn_in_proj_w", "L0_attn_conv_w", "L0_attn_conv_b", "L0_attn_dt_bias", "L0_attn_A_log",
        "L0_attn_D", "L0_attn_norm_w", "L0_attn_out_proj_w", "L0_attn_ln_w", "L0_attn_ln_b", "L0_ffn_Wr", "L0_ffn_br",
        "L0_ffn_W1", "L0_ffn_b1", "L0_ffn_W2", "L0_ffn_b2"]


def kernel(**inputs):
    import numpy as _np
    import concourse.bacc as _bacc
    from concourse import mybir as _mybir
    from concourse.bass_utils import run_bass_kernel_spmd as _run

    nc = _bacc.Bacc("TRN2", target_bir_lowering=False, num_devices=1)
    arrays, args = {}, []
    for name in _INS:
        a = _np.ascontiguousarray(inputs[name])
        arrays[f"in_{name}"] = a
        args.append(nc.dram_tensor(f"in_{name}", a.shape, _mybir.dt.from_np(a.dtype), kind="ExternalInput").ap())
    out = nc.dram_tensor("out_x", (BATCH, SEQ, D), F32, kind="ExternalOutput").ap()
    macaron_block(nc, *args, out)
    r = _run(nc, [arrays], core_ids=[0])
    return r.results[0]["out_x"]
```

```python
import concourse.bass as bass
from concourse import mybir
from contextlib import ExitStack

F32 = mybir.dt.float32
BF16 = mybir.dt.bfloat16
I32 = mybir.dt.int32
U32 = mybir.dt.uint32
ALU = mybir.AluOpType
ACT = mybir.ActivationFunctionType
AX = mybir.AxisListType
ds = bass.ds

P = 128
BATCH, SEQ, D = 4, 512, 128
TOK = BATCH * SEQ
NT = TOK // P
NC = SEQ // P
NE, HID, KTOP = 8, 512, 2
HC = HID // P
NG = KTOP * NT
SLOT_TILES = NG + NE - 1
TRIO = 3
LAP = 2 * TRIO
TURNS = SLOT_TILES // LAP
assert LAP > SLOT_TILES - TURNS * LAP > 0
W1W = HID + HC
INNER, STATE, HEADS, HD, TAPS = 256, 128, 4, 64, 4
CONV = INNER + 2 * STATE
IC = INNER // P
VECS = NE * HC + CONV // P + IC
EPS = 1e-5
LEAST_DECAY = -100.0
RSQRT_SEED = float(0x5F3759DF)
Z0, DT0, X0 = 0, INNER, INNER + HEADS
WCOLS = 2 * INNER + 2 * STATE + HEADS


class Steps:

    def __init__(self, engine, sem):
        self.engine, self.sem, self.base, self.n, self.fixed = engine, sem, 0, 0, 0

    def done(self, instruction):
        instruction.then_inc(self.sem, 1)
        self.n += 1

    def settle(self):
        self.engine.wait_ge(self.sem, self.base + self.n)

    def link(self, instruction):
        self.done(instruction)
        self.settle()

    def enter(self, i, per):
        self.fixed = self.base + self.n
        self.base, self.n, self.per = self.fixed + i * per, 0, per

    def leave(self, count):
        assert self.n == self.per, (self.n, self.per)
        self.base, self.n = self.fixed + count * self.per, 0


BLOCKS = (2, 3, 0, 1, 4, 5)


def early(turn, u):
    return isinstance(turn, int) and turn * LAP + u < TRIO


def beyond(i, n):
    return not (isinstance(i, int) and i < n)


def in_steps(engine, ahead):
    def step(turn, u):
        for k in sorted(ahead, reverse=True):
            t, w = turn + (u + k) // LAP, (u + k) % LAP
            if not (isinstance(t, int) and t * LAP + w >= SLOT_TILES):
                ahead[k](t, w)

    for early_step in range(-max(ahead), 0):
        for k in sorted(ahead, reverse=True):
            if early_step + k >= 0:
                ahead[k](0, early_step + k)
    for u in range(LAP):
        step(0, u)
    with engine.Fori(1, TURNS) as turn:
        for u in range(LAP):
            step(turn, u)
    for u in range(SLOT_TILES - TURNS * LAP):
        step(TURNS, u)


def tiles_of(u):
    return len(range(u, SLOT_TILES, LAP))


def row(tensor, t):
    return tensor[:, ds(t, 1), :].rearrange("p a c -> p (a c)")


def macaron_block(nc, x, in_proj_w, conv_w, conv_b, dt_bias, A_log, D_skip, norm_w, out_proj_w,
                  ln_w, ln_b, Wr, br, W1, b1, W2, b2, out):
    ctx = ExitStack()
    with ctx:
        def sb(name, shape, dt=F32):
            return ctx.enter_context(nc.sbuf_tensor(name, shape, dt))

        def sem(name):
            return ctx.enter_context(nc.semaphore(name))

        X = sb("X", [P, NT, D])
        XN = sb("XN", [P, NT, D])
        XNT = sb("XNT", [P, TOK])
        W1S = sb("W1S", [P, NE, W1W])
        W2S = sb("W2S", [P, NE, HC, D])
        B2S = sb("B2S", [P, NE, D])
        vec_rows = sb("vec_rows", [VECS, P])
        WrS = sb("WrS", [P, NE])
        BrS = sb("BrS", [P, NE])
        in_rows = sb("in_rows", [P, 6, D])
        in_rows_dt = sb("in_rows_dt", [HEADS, D])
        WT = sb("WT", [P, WCOLS])
        out_rows = sb("out_rows", [P, INNER])
        WoT = sb("WoT", [P, IC, D])
        cw = sb("cw", [P, TAPS, TAPS])
        cb = sb("cb", [P, TAPS])
        dtb = sb("dtb", [P, HEADS])
        alog = sb("alog", [P, HEADS])
        expA = sb("expA", [P, HEADS])
        Dch = sb("Dch", [P, IC])
        nw = sb("nw", [P, IC])
        diagD = sb("diagD", [P, IC, P])
        lnw = sb("lnw", [P, D])
        lnb = sb("lnb", [P, D])
        ident = sb("ident", [P, P])
        ones = sb("ones", [P, P])
        upto = sb("upto", [P, P])
        after = sb("after", [P, P])
        before_bf = sb("before_bf", [P, P], BF16)
        ones_bf = sb("ones_bf", [P, P], BF16)
        iota_e = sb("iota_e", [P, NE])
        iota_t = sb("iota_t", [P, NT])
        iota_st = sb("iota_st", [P, SLOT_TILES])
        iota_p = sb("iota_p", [P, 1])
        iota_b = sb("iota_b", [P, P, NG], BF16)
        iota_a = sb("iota_a", [P, SLOT_TILES, NG], BF16)
        no_pair = sb("no_pair", [P, SLOT_TILES])
        group_row = sb("group_row", [P, NG], BF16)
        stats = sb("stats", [P, NT, 6])
        mv = sb("mv", [P, NT, 2])
        rs = sb("rs", [P, NT])
        rt = sb("rt", [P, NT])
        shift = sb("shift", [P, NT])
        rv = sb("rv", [P, NT])
        lg = sb("lg", [P, NT, NE])
        top = sb("top", [P, NT, 8])
        topi = sb("topi", [P, NT, 8], U32)
        topf = sb("topf", [P, NT, KTOP])
        gate = sb("gate", [P, KTOP, NT])
        gd = sb("gd", [P, NT])
        ge = sb("ge", [P, NT])
        gr = sb("gr", [P, NT])
        pick = sb("pick", [P, KTOP, NT, NE])
        picks_bf = sb("picks_bf", [P, NT * NE], BF16)
        cnt = sb("cnt", [P, NE, NT])
        run = sb("run", [P, NE, NT])
        excl = sb("excl", [P, NE, NT])
        n_e = sb("n_e", [P, NE])
        cmp16 = sb("cmp16", [P, NE, NT])
        tiles_e = sb("tiles_e", [P, NE])
        end_e = sb("end_e", [P, NE])
        adj = sb("adj", [P, NE])
        base = sb("base", [P, NE, NT])
        slot_all = sb("slot_all", [P, NT, NE])
        slot_pick = sb("slot_pick", [P, KTOP, NT, NE])
        slot = sb("slot", [P, NG])
        slot_i = sb("slot_i", [P, NG], I32)
        a_i = sb("a_i", [P, NG], I32)
        b_i = sb("b_i", [P, NG], I32)
        a_bf = sb("a_bf", [P, NG], BF16)
        b_bf = sb("b_bf", [P, NG], BF16)
        rhs_ids = sb("rhs_ids", [P, 3, SLOT_TILES, NG], BF16)
        onehot_b = sb("onehot_b", [P, P, NG], BF16)
        ids_f = sb("ids_f", [P, SLOT_TILES])
        rows_out = sb("rows_out", [P, SLOT_TILES], I32)
        rows_in = sb("rows_in", [P, SLOT_TILES], I32)
        te_cmp = sb("te_cmp", [P, SLOT_TILES, NE])
        te_f = sb("te_f", [P, SLOT_TILES])
        te_i = sb("te_i", [P, SLOT_TILES], I32)
        XG = [sb(f"XG{u}", [P, D]) for u in range(LAP)]
        XT = [sb(f"XT{u}", [P, P]) for u in range(TRIO)]
        W1B = [sb(f"W1B{u}", [P, W1W]) for u in range(TRIO)]
        H = [sb(f"H{u}", [P, HC, P]) for u in range(TRIO)]
        YS = [sb(f"YS{u}", [P, D]) for u in range(LAP)]
        Y12 = sb("Y12", [P, KTOP, NT, D])
        Y1, Y2 = Y12[:, 0, :, :], Y12[:, 1, :, :]
        dtr = sb("dtr", [P, NT, HEADS])
        sp = [sb(f"sp{k}", [P, NT, HEADS]) for k in range(5)]
        dt = sb("dt", [P, NT, HEADS])
        la = sb("la", [P, NT, HEADS])
        decay = sb("decay", [P, 3, NT, HEADS])
        dtd = sb("dtd", [P, NT, HEADS])
        acc = [sb(f"acc{k}", [P, SEQ]) for k in range(TAPS)]
        conv = [sb(f"conv{k}", [P, SEQ]) for k in range(TAPS)]
        gz = Y12
        xdt = [sb(f"xdt{u}", [P, INNER]) for u in range(2)]
        xend = [sb(f"xend{u}", [P, INNER]) for u in range(2)]
        btok = [sb(f"btok{u}", [P, STATE]) for u in range(2)]
        gm = [sb(f"gm{u}", [P, P]) for u in range(2)]
        seg_rhs = [sb(f"seg_rhs{u}", [P, HEADS, P]) for u in range(2)]
        eseg = [sb(f"eseg{u}", [P, HEADS, P]) for u in range(2)]
        mix = [sb(f"mix{u}", [P, HEADS, P]) for u in range(2)]
        spare = sb("spare", [P, 1])
        S = sb("S", [P, INNER])
        S_kept = sb("S_kept", [P, INNER])
        yi = sb("yi", [P, INNER])
        yt = [sb(f"yt{u}", [P, INNER]) for u in range(2)]
        y2T = sb("y2T", [P, NC, IC, P])
        sq = [sb(f"sq{u}", [P, IC, P]) for u in range(2)]
        O = sb("O", [P, NT, D + 1])
        res, fin = Y1, Y2

        PS = [ctx.enter_context(nc.psum_tensor(f"PS{i}", [P, 512], F32)) for i in range(8)]

        xn_dram = nc.dram_tensor("xn_rows", [TOK, D], F32, kind="Internal").ap()
        y_dram = nc.dram_tensor("y_rows", [KTOP * TOK + SLOT_TILES * P, D], F32, kind="Internal").ap()

        s_x = [sem(f"s_x{g}") for g in range(BATCH)]
        s_wr = sem("s_wr")
        s_par = sem("s_par")
        s_w = sem("s_w")
        s_const = sem("s_const")
        s_iota = sem("s_iota")
        s_prep = sem("s_prep")
        s_w1s = sem("s_w1s")
        s_pool = sem("s_pool")
        s_side = sem("s_side")
        s_dve = sem("s_dve")
        s_act = sem("s_act")
        s_ids_p = sem("s_ids_p")
        s_near = sem("s_near")
        s_weighed = sem("s_weighed")
        s_scaled = sem("s_scaled")
        s_added = sem("s_added")
        s_rs = sem("s_rs")
        s_xn = [sem("s_xn_dve"), sem("s_xn_act")]
        s_xnd = sem("s_xnd")
        s_lnT = sem("s_lnT")
        s_xnt = sem("s_xnt")
        s_small = sem("s_small")
        s_gd = sem("s_gd")
        s_ge = sem("s_ge")
        s_picks = sem("s_picks")
        s_cnt = sem("s_cnt")
        s_ob = sem("s_ob")
        s_ids = sem("s_ids")
        s_idp = sem("s_idp")
        s_te = sem("s_te")
        s_rows = sem("s_rows")
        s_gath = [sem(f"s_gath{u}") for u in range(LAP)]
        s_sc = [sem(f"s_sc{u}") for u in range(LAP)]
        s_xt = sem("s_xt")
        s_xtc = sem("s_xtc")
        s_w1 = sem("s_w1")
        s_upa = sem("s_upa")
        s_upb = sem("s_upb")
        s_ra = sem("s_ra")
        s_rb = sem("s_rb")
        s_y = sem("s_y")
        s_yc = sem("s_yc")
        s_yl = [sem(f"s_yl{g}") for g in range(BATCH)]
        s_gated = sem("s_gated")
        s_comb = sem("s_comb")
        s_comb_pool = sem("s_comb_pool")
        s_out = sem("s_out")
        s_sp = sem("s_sp")
        s_spe = sem("s_spe")
        s_la = sem("s_la")
        s_dec = sem("s_dec")
        s_dece = sem("s_dece")
        s_proj = sem("s_proj")
        s_tap = sem("s_tap")
        s_cv = sem("s_cv")
        s_silu = sem("s_silu")
        s_table = sem("s_table")
        s_segr = sem("s_segr")
        s_tr = sem("s_tr")
        s_trb = sem("s_trb")
        s_seg = sem("s_seg")
        s_bt = sem("s_bt")
        s_es = sem("s_es")
        s_xd = sem("s_xd")
        s_xe = sem("s_xe")
        s_gmm = sem("s_gmm")
        s_mix = sem("s_mix")
        s_yp = sem("s_yp")
        s_u = sem("s_u")
        s_S = sem("s_S")
        s_kept = sem("s_kept")
        s_yt = sem("s_yt")
        s_yT = sem("s_yT")
        s_y2 = sem("s_y2")
        s_sq = sem("s_sq")
        s_sqs = sem("s_sqs")
        s_o = sem("s_o")
        s_oc = sem("s_oc")
        s_lnb = sem("s_lnb")
        block = ctx.enter_context(nc.Block())

        xf = x.rearrange("b s d -> (b s) d").rearrange("(t p) d -> p t d", p=P)
        of = out.rearrange("b s d -> (b s) d").rearrange("(t p) d -> p t d", p=P)
        N_CONST = 10
        QUARTER = NG // 4
        EARLIER = NT - NC
        N_PARAMS = 12 + 2 * IC
        WR, PARAMS, WEIGHTS = 16 * 2, 16 * N_PARAMS, 16 * 3

        def wait_xn(engine, n, g):
            if g == 1:
                engine.wait_ge(s_xn[1], NC * (n + 1))
            else:
                engine.wait_ge(s_xn[0], NC * ((BATCH - 1) * n + max(g, 1)))

        @block.sync
        def _(sp_):
            for g in range(BATCH):
                sp_.dma_start(X[:, g * NC:(g + 1) * NC, :], xf[:, g * NC:(g + 1) * NC, :]).then_inc(s_x[g], 16)
            sp_.dma_start(WrS[:], Wr).then_inc(s_wr, 16)
            sp_.dma_start(BrS[:], br.partition_broadcast(P)).then_inc(s_wr, 16)
            params = [
                (vec_rows[0:NE * HC, :], b1.rearrange("e (c p) -> (e c) p", p=P)),
                (in_rows[:, 0:2, :], in_proj_w[0:INNER, :].rearrange("(c p) d -> p c d", p=P)),
                (in_rows[:, 2:6, :], in_proj_w[INNER:INNER + CONV, :].rearrange("(c p) d -> p c d", p=P)),
                (in_rows_dt[:], in_proj_w[INNER + CONV:INNER + CONV + HEADS, :]),
                (out_rows[:], out_proj_w),
                (cw[:], conv_w.rearrange("(c p) k -> p c k", p=P)),
                (vec_rows[NE * HC:NE * HC + TAPS, :], conv_b.rearrange("(c p) -> c p", p=P)),
                (vec_rows[NE * HC + TAPS:VECS, :], norm_w.rearrange("(c p) -> c p", p=P)),
                (dtb[:], dt_bias.partition_broadcast(P)), (alog[:], A_log.partition_broadcast(P)),
                (lnw[:], ln_w.partition_broadcast(P)), (lnb[:], ln_b.partition_broadcast(P)),
            ]
            params += [(Dch[k * HD:(k + 1) * HD, c:c + 1], D_skip[2 * c + k:2 * c + k + 1].partition_broadcast(HD))
                       for c in range(IC) for k in range(2)]
            assert len(params) == N_PARAMS
            for dst, src in params:
                sp_.dma_start(dst, src).then_inc(s_par, 16)
            for dst, src in (
                (W1S[:, :, 0:HID], W1.rearrange("e d h -> d e h")),
                (W2S[:].rearrange("p e c d -> p (e c) d"), W2.rearrange("e (c p) d -> p (e c) d", p=P)),
                (B2S[:], b2.partition_broadcast(P)),
            ):
                sp_.dma_start(dst, src).then_inc(s_w, 16)
            xn_v = xn_dram.rearrange("(t p) d -> p t d", p=P)
            y_v = y_dram[0:KTOP * TOK, :].rearrange("(k t p) d -> k p t d", p=P, k=KTOP)
            for layer in range(2):
                for g in range(BATCH):
                    wait_xn(sp_, 2 * layer, g)
                    sp_.dma_start(xn_v[:, g * NC:(g + 1) * NC, :], XN[:, g * NC:(g + 1) * NC, :]).then_inc(s_xnd, 16)
                for u in range(LAP):
                    sp_.wait_ge(s_sc[u], 16 * tiles_of(u) * (layer + 1))
                for g in (0, BATCH - 1, *range(1, BATCH - 1)):
                    for k, Y in enumerate((Y1, Y2)):
                        sp_.dma_start(Y[:, g * NC:(g + 1) * NC, :], y_v[k, :, g * NC:(g + 1) * NC, :]).then_inc(s_yl[g], 16)
            for g in range(BATCH):
                if g < BATCH - 1:
                    sp_.wait_ge(s_comb, 2 + g + 1)
                else:
                    sp_.wait_ge(s_comb_pool, 2)
                sp_.dma_start(of[:, g * NC:(g + 1) * NC, :], X[:, g * NC:(g + 1) * NC, :]).then_inc(s_out, 16)
            sp_.wait_ge(s_out, 16 * BATCH)

        def heads(ap):
            return ap.rearrange("p (h d) -> p h d", h=HEADS)

        def by_chunk(k, q):
            return (decay[:, k, ds(q, 1), :].rearrange("p a h -> p (a h)").unsqueeze(2)
                    .broadcast_to([P, HEADS, HD]))

        @block.gpsimd
        def _(pool):
            g = nc.gpsimd
            st = Steps(pool, s_pool)
            st.done(g.memset(ident[:], 0.0))
            st.done(g.memset(ones[:], 1.0))
            st.done(g.memset(upto[:], 1.0))
            st.done(g.memset(after[:], 1.0))
            st.done(g.memset(before_bf[:], 1.0))
            st.done(g.memset(ones_bf[:], 1.0))
            st.settle()
            g.affine_select(out=ident[:], in_=ident[:], compare_op=ALU.not_equal, fill=1.0, base=0,
                            pattern=[[-1, P]], channel_multiplier=1).then_inc(s_const, 1)
            g.affine_select(out=upto[:], in_=upto[:], compare_op=ALU.is_ge, fill=0.0, base=0,
                            pattern=[[1, P]], channel_multiplier=-1).then_inc(s_const, 1)
            g.affine_select(out=after[:], in_=after[:], compare_op=ALU.is_gt, fill=0.0, base=0,
                            pattern=[[-1, P]], channel_multiplier=1).then_inc(s_const, 1)
            g.affine_select(out=before_bf[:], in_=before_bf[:], compare_op=ALU.is_gt, fill=0.0, base=0,
                            pattern=[[1, P]], channel_multiplier=-1).then_inc(s_const, 1)
            small = dict(allow_small_or_imprecise_dtypes=True)
            g.iota(iota_e[:], pattern=[[1, NE]], base=0, channel_multiplier=0, **small).then_inc(s_const, 1)
            g.iota(iota_t[:], pattern=[[P, NT]], base=0, channel_multiplier=0, **small).then_inc(s_const, 1)
            g.iota(iota_st[:], pattern=[[1, SLOT_TILES]], base=0, channel_multiplier=0, **small).then_inc(s_const, 1)
            g.iota(iota_p[:], pattern=[[0, 1]], base=0, channel_multiplier=1, **small).then_inc(s_const, 1)
            g.iota(no_pair[:], pattern=[[-P, SLOT_TILES]], base=-KTOP * TOK, channel_multiplier=-1, **small).then_inc(s_const, 1)
            g.iota(group_row[:], pattern=[[P, NG]], base=0, channel_multiplier=0, **small).then_inc(s_const, 1)
            g.iota(iota_a[:], pattern=[[1, SLOT_TILES], [0, NG]], base=0, channel_multiplier=0, **small).then_inc(s_iota, 1)
            g.iota(iota_b[:], pattern=[[1, P], [0, NG]], base=0, channel_multiplier=0, **small).then_inc(s_iota, 1)

            def experts(layer):
                pool.wait_ge(s_xnd, 16 * BATCH * (layer + 1))
                pool.wait_ge(s_rows, layer + 1)

                def gather(j):
                    u = j % LAP
                    if j >= LAP:
                        pool.wait_ge(s_xt, layer * SLOT_TILES + j - LAP + 1)
                    g.indirect_dma_start(out=XG[u][:], out_offset=None, in_=xn_dram,
                                         in_offset=bass.IndirectOffsetOnAxis(ap=rows_in[:, j:j + 1], axis=0)
                                         ).then_inc(s_gath[u], 16)

                def scatter(j):
                    u = j % LAP
                    pool.wait_ge(s_yc, layer * SLOT_TILES + j + 1)
                    g.indirect_dma_start(out=y_dram, in_=YS[u][:], in_offset=None,
                                         out_offset=bass.IndirectOffsetOnAxis(ap=rows_out[:, j:j + 1], axis=0)
                                         ).then_inc(s_sc[u], 16)

                ahead = LAP + 2
                for j in range(ahead):
                    gather(j)
                for j in range(SLOT_TILES):
                    if j + ahead < SLOT_TILES:
                        gather(j + ahead)
                    scatter(j)

                xb = X[:, NT - NC:NT, :]
                pool.wait_ge(s_gated, 2 * layer + 1)
                st.link(g.tensor_tensor(xb, xb, Y1[:, NT - NC:NT, :], ALU.add))
                pool.wait_ge(s_gated, 2 * layer + 2)
                g.tensor_tensor(xb, xb, Y2[:, NT - NC:NT, :], ALU.add).then_inc(s_comb_pool, 1)

            def mixer():
                def segments(q, u):
                    if beyond(q, 2):
                        pool.wait_ge(s_seg, q - 1)
                    g.tensor_tensor(seg_rhs[u][:], upto[:].unsqueeze(1).broadcast_to([P, HEADS, P]),
                                    row(la, q).unsqueeze(2).broadcast_to([P, HEADS, P]), ALU.mult).then_inc(s_segr, 1)

                def mixing(q, u):
                    pool.wait_ge(s_gmm, q + 1)
                    pool.wait_ge(s_es, q + 1)
                    if beyond(q, 2):
                        pool.wait_ge(s_yp, q - 1)
                    g.tensor_tensor(mix[u][:], eseg[u][:], gm[u][:].unsqueeze(1).broadcast_to([P, HEADS, P]),
                                    ALU.mult).then_inc(s_mix, 1)

                def squares(q, u):
                    pool.wait_ge(s_sq, q + 1)
                    g.tensor_tensor(sq[u][:, 0, :], sq[u][:, 0, :], sq[u][:, 1, :], ALU.add).then_inc(s_sqs, 1)

                pool.wait_ge(s_par, PARAMS)
                for k in (1, BATCH - 1):
                    wait_xn(pool, 1, k)
                for k in range(BATCH):
                    xb = X[:, k * NC:(k + 1) * NC, :]
                    g.tensor_tensor(xb, xb, lnb[:].unsqueeze(1).broadcast_to([P, NC, D]), ALU.add).then_inc(s_lnb, 1)
                pool.wait_ge(s_la, 1)
                segments(0, 0)
                segments(1, 1)

                def batch(b, last_batch=False):
                    for c in range(NC):
                        q = b * NC + c
                        u = c % 2
                        if not (last_batch and c >= NC - 2):
                            segments(q + 2, u)
                        if beyond(q, 3):
                            squares(q - 3, 1 - u)
                        mixing(q, u)
                        if 0 < c < NC - 1:
                            pool.wait_ge(s_S, b * (NC - 1) + c)
                            g.tensor_tensor(heads(S_kept[:]), heads(S[:]), by_chunk(2, q), ALU.mult).then_inc(s_kept, 1)

                batch(0)
                with pool.Fori(1, BATCH - 1) as b:
                    batch(b)
                batch(BATCH - 1, True)
                for q in range(NT - 3, NT):
                    squares(q, q % 2)
            experts(0)
            mixer()
            pool.wait_ge(s_lnb, BATCH)
            for k in range(2):
                pool.wait_ge(s_scaled, k + 1)
                xb = X[:, k * NC:(k + 1) * NC, :]
                g.tensor_tensor(xb, xb, fin[:, k * NC:(k + 1) * NC, :], ALU.add).then_inc(s_added, 1)
            experts(1)

        @block.tensor
        def _(pe):
            mm = nc.tensor.matmul

            def keep_busy(n):
                for _ in range(n):
                    mm(PS[0][:, 0:P], ident[:], ones[:], start=True, stop=True)

            def norm_project(n, rhs, width, besides=None):
                def small(g):
                    bank = PS[1 if g == BATCH - 1 and not besides else 2]
                    pe.wait_ge(s_xnt, BATCH * n + g + 1)
                    for t in range(g * NC, (g + 1) * NC):
                        last = mm(bank[:, t * width:(t + 1) * width], XNT[:, t * P:(t + 1) * P], rhs,
                                  start=True, stop=True)
                    if g == BATCH - 1 or (g == BATCH - 2 and not besides):
                        last.then_inc(s_small, 1)

                if n:
                    pe.wait_ge(s_near, n)
                    keep_busy(26 if n == 1 else 16)
                for groups in ((0, 1), (2, 3)) if besides else ((0, 1), (2,), (3,)):
                    for k in groups:
                        wait_xn(pe, n, k)
                        for c in range(NC):
                            last = nc.tensor.transpose(PS[3 + k][:, c * P:(c + 1) * P], XN[:, k * NC + c, :], ident[:])
                        last.then_inc(s_lnT, 1)
                    if besides and 0 in groups:
                        besides(0)
                    for k in groups:
                        small(k)
                    if besides and 0 in groups:
                        besides(1)

            def weights():
                pe.wait_ge(s_par, PARAMS)
                for c in range(4):
                    nc.tensor.transpose(PS[6][:, c * P:(c + 1) * P], in_rows[:, c, :], ident[:])
                for c in range(2):
                    nc.tensor.transpose(PS[7][:, c * P:(c + 1) * P], in_rows[:, 4 + c, :], ident[:])
                nc.tensor.transpose(PS[7][:, 256:256 + HEADS], in_rows_dt[:], ident[0:HEADS, 0:HEADS])
                nc.tensor.transpose(PS[7][:, 260:260 + VECS], vec_rows[:], ident[0:VECS, 0:VECS])
                for c in range(IC):
                    last = nc.tensor.transpose(PS[5][:, c * P:(c + 1) * P], out_rows[:, c * P:(c + 1) * P], ident[:])
                last.then_inc(s_prep, 1)

            def experts(layer):
                pe.wait_ge(s_picks, layer + 1)
                mm(PS[3][:, 0:NT * NE], before_bf[:], picks_bf[:], start=True, stop=True)
                mm(PS[4][:, 0:NT * NE], ones_bf[:], picks_bf[:], start=True, stop=True).then_inc(s_cnt, 1)
                keep_busy(22)
                pe.wait_ge(s_w1s, 1)
                pe.wait_ge(s_ids, 2 * (layer + 1))
                pe.wait_ge(s_ids_p, layer + 1)
                for q in range(NG):
                    if q % QUARTER == 0:
                        pe.wait_ge(s_ob, 4 * layer + q // QUARTER + 1)
                    last = mm(PS[5][:, 0:3 * SLOT_TILES], onehot_b[:, :, q], rhs_ids[:, :, :, q],
                              start=(q == 0), stop=(q == NG - 1))
                last.then_inc(s_idp, 1)
                keep_busy(10)
                pe.wait_ge(s_te, layer + 1)
                B0 = layer * SLOT_TILES

                pe.wait_ge(s_w, WEIGHTS)

                def turned(turn, u):
                    j = turn * LAP + u
                    pe.wait_ge(s_gath[u], 16 * (layer * tiles_of(u) + turn + 1))
                    if not (early(turn, u) and u == 0):
                        pe.wait_ge(s_xtc, B0 + j)
                    nc.tensor.transpose(PS[0][:, 0:P], XG[u][:], ident[:]).then_inc(s_xt, 1)

                def up(turn, u):
                    j = turn * LAP + u
                    w = u % TRIO
                    pe.wait_ge(s_xtc, B0 + j + 1)
                    pe.wait_ge(s_w1, B0 + j + 1)
                    for half, ready in enumerate((s_upa, s_upb)):
                        for c in range(2):
                            h = 2 * half + c
                            last = mm(PS[2 + TRIO * half + w][:, c * P:(c + 1) * P], W1B[w][:, h * P:(h + 1) * P],
                                      XT[w][:], start=True, stop=True)
                        last.then_inc(ready, 1)

                def down(turn, u):
                    j = turn * LAP + u
                    w = u % TRIO
                    e = pe.value_load(te_i[0:1, ds(j, 1)], min_val=0, max_val=NE - 1)
                    pe.wait_ge(s_ra, B0 + j + 1)
                    pe.wait_ge(s_rb, B0 + j + 1)
                    if not (early(turn, u) and u == 0):
                        pe.wait_ge(s_yc, B0 + j)
                    for c in range(HC):
                        last = mm(PS[1][:, 0:D], H[w][:, c, :], W2S[:, ds(e, 1), c, :].rearrange("p a d -> p (a d)"),
                                  start=(c == 0), stop=(c == HC - 1))
                    last.then_inc(s_y, 1)

                in_steps(pe, {2: turned, 1: up, 0: down})

            def mixer():
                def project(n, m):
                    k = BLOCKS[m]
                    if m == 0 and not beyond(n, 1):
                        pe.wait_ge(s_xnt, BATCH + 1)
                    if m >= 2:
                        pe.wait_ge(s_cv, n * TAPS + (m - 1))
                    elif beyond(n, 1):
                        pe.wait_ge(s_silu, n * 6 - 1 + m)
                    w0 = X0 + k * P if k < TAPS else Z0 + (k - TAPS) * P
                    mm(PS[m % 2][:], WT[:, w0:w0 + P], XNT[:, ds(n * SEQ, SEQ)], start=True,
                       stop=True).then_inc(s_proj, 1)

                def segments(q, u):
                    pe.wait_ge(s_segr, q + 1)
                    if beyond(q, 1):
                        pe.wait_ge(s_es, q)
                    mm(PS[5][:], after[:], seg_rhs[u][:].rearrange("p h t -> p (h t)"), start=True,
                       stop=True).then_inc(s_seg, 1)

                def batch(b, last_batch=False):
                    first = isinstance(b, int) and b == 0

                    def s1(c):
                        q = b * NC + c
                        tile = slice(c * P, (c + 1) * P)
                        if c == 0:
                            pe.wait_ge(s_silu, b * 6 + TAPS)
                        if c >= 2:
                            pe.wait_ge(s_xe, b * (NC - 1) + (c - 1))
                        elif not first:
                            if c:
                                pe.wait_ge(s_xd, q - 1)
                            else:
                                pe.wait_ge(s_xe, b * (NC - 1))
                        bank = PS[2 + c % 2]
                        for i in range(IC):
                            nc.tensor.transpose(bank[:, i * P:(i + 1) * P], conv[i][:, tile], ident[:])
                        mm(bank[:, INNER:INNER + P], conv[2][:, tile], conv[3][:, tile], start=True,
                           stop=True).then_inc(s_tr, 1)
                        if c < NC - 1:
                            if not (first and c == 0):
                                pe.wait_ge(s_bt, b * (NC - 1) + c)
                            if not first and c == 0:
                                pe.wait_ge(s_oc, q - 2)
                            if not first and c == 2:
                                pe.wait_ge(s_oc, q - 3)
                            nc.tensor.transpose(PS[4][:, 2 * P:3 * P], conv[2][:, tile], ident[:]).then_inc(s_trb, 1)

                    def s2(c):
                        q = b * NC + c
                        tile = slice(c * P, (c + 1) * P)
                        u = c % 2
                        if not (first and c == 0):
                            pe.wait_ge(s_yt, q)
                        for i in range(IC):
                            mm(PS[6][:, i * P:(i + 1) * P], conv[i][:, tile], diagD[:, i, :], start=(i == 0),
                               stop=False, skip_group_check=True)
                        pe.wait_ge(s_mix, q + 1)
                        pe.wait_ge(s_xd, q + 1)
                        for h in range(HEADS):
                            last = mm(PS[6][:, h * HD:(h + 1) * HD], mix[u][:, h, :], xdt[u][:, h * HD:(h + 1) * HD],
                                      start=False, stop=True, skip_group_check=True)
                        if c:
                            pe.wait_ge(s_S, b * (NC - 1) + c)
                            last = mm(PS[6][:, INNER:2 * INNER], conv[3][:, tile], S[:], start=True, stop=True,
                                      skip_group_check=True)
                        last.then_inc(s_yp, 1)
                        if c < NC - 1:
                            pe.wait_ge(s_bt, b * (NC - 1) + c + 1)
                            pe.wait_ge(s_xe, b * (NC - 1) + c + 1)
                            if not (first and c == 0):
                                pe.wait_ge(s_S, b * (NC - 1) + c)
                            if c >= 2:
                                pe.wait_ge(s_y2, q - 1)
                            elif c == 0 and not first:
                                pe.wait_ge(s_y2, q)
                            mm(PS[7][:, INNER:2 * INNER], btok[u][:], xend[u][:], start=True, stop=True).then_inc(s_u, 1)

                    def s3(c):
                        q = b * NC + c
                        pe.wait_ge(s_yt, q + 1)
                        if not (first and c == 0):
                            pe.wait_ge(s_y2, q)
                        if c + 1 < NC - 1:
                            pe.wait_ge(s_S, b * (NC - 1) + (c + 2))
                        for i in range(IC):
                            last = nc.tensor.transpose(PS[7][:, i * P:(i + 1) * P], yt[c % 2][:, i * P:(i + 1) * P], ident[:])
                        last.then_inc(s_yT, 1)

                    if first:
                        pe.wait_ge(s_la, 1)
                        flat = la[:].rearrange("p t h -> p (t h)")
                        for k, m in enumerate((upto, after, ones)):
                            last = mm(PS[3][:, k * NT * HEADS:(k + 1) * NT * HEADS], m[:], flat, start=True, stop=True)
                        last.then_inc(s_dec, 1)
                    s1(0)
                    if first:
                        segments(0, 0)
                    if not last_batch:
                        project(b + 1, 0)
                    if first:
                        segments(1, 1)
                        pe.wait_ge(s_dece, 1)
                    for c in range(NC):
                        if c + 1 < NC:
                            s1(c + 1)
                        if c == NC - 1 and not last_batch:
                            segments(b * NC + c + 2, c % 2)
                        s2(c)
                        if not last_batch:
                            project(b + 1, c + 1)
                        if c < (NC - 2 if last_batch else NC - 1):
                            segments(b * NC + c + 2, c % 2)
                        if c:
                            s3(c - 1)
                        if not (first and c < 2):
                            pe.wait_ge(s_bt, b * (NC - 1) + min(c + 2, NC - 1))
                            project_out(b * NC + c - 2, (c - 2) % NC)
                    if not last_batch:
                        project(b + 1, TAPS + 1)
                    s3(NC - 1)

                def project_out(q, c):
                    pe.wait_ge(s_y2, q + 1)
                    if beyond(q, 1):
                        pe.wait_ge(s_oc, q)
                    for i in range(IC):
                        mm(PS[4][:, 0:D], y2T[:, c, i, :], WoT[:, i, :], start=(i == 0), stop=(i == IC - 1))
                    pe.wait_ge(s_sqs, q + 1)
                    mm(PS[4][:, D:D + 1], sq[c % 2][:, 0, :], ones[:, 0:1], start=True, stop=True).then_inc(s_o, 1)

                norm_project(1, WT[:, DT0:DT0 + HEADS], HEADS, lambda m: project(0, m))
                for m in range(2, TAPS + 2):
                    project(0, m)
                batch(0)
                with pe.Fori(1, BATCH - 1) as b:
                    batch(b)
                batch(BATCH - 1, True)
                project_out(NT - 2, NC - 2)
                project_out(NT - 1, NC - 1)

            pe.wait_ge(s_const, N_CONST)
            keep_busy(26)
            pe.wait_ge(s_wr, WR)
            norm_project(0, WrS[:], NE)
            weights()
            experts(0)
            mixer()
            norm_project(2, WrS[:], NE)
            experts(1)

        @block.scalar
        def _(act):
            A = nc.scalar.activation
            st = Steps(act, s_act)

            def norm(n, g):
                act.wait_ge(s_rs, n + 1)
                if n == 1:
                    act.wait_ge(s_xnd, 16 * BATCH)
                for t in range(g * NC, (g + 1) * NC):
                    A(XN[:, t, :], X[:, t, :], ACT.Identity, bias=shift[:, t:t + 1],
                      scale=rs[:, t:t + 1]).then_inc(s_xn[1], 1)

            def norm_project(n, besides=None):
                norm(n, 1)
                for g in range(BATCH):
                    act.wait_ge(s_lnT, BATCH * n + g + 1)
                    A(XNT[:, g * SEQ:(g + 1) * SEQ], PS[3 + g][:], ACT.Copy).then_inc(s_xnt, 1)
                    if g == 1 and besides:
                        besides(0)
                        besides(1)

            def weights():
                act.wait_ge(s_prep, 1)
                act.wait_ge(s_par, PARAMS)
                st.done(A(WT[:, Z0:Z0 + INNER], PS[6][:, 0:INNER], ACT.Copy))
                st.done(A(WT[:, X0:X0 + INNER], PS[6][:, INNER:2 * INNER], ACT.Copy))
                st.done(A(WT[:, X0 + INNER:X0 + CONV], PS[7][:, 0:2 * P], ACT.Copy))
                st.done(A(WT[:, DT0:DT0 + HEADS], PS[7][:, 256:256 + HEADS], ACT.Copy))
                st.done(A(W1S[:, :, HID:W1W], PS[7][:, 260:260 + NE * HC].rearrange("p (e c) -> p e c", e=NE), ACT.Copy))
                st.done(A(cb[:], PS[7][:, 260 + NE * HC:260 + NE * HC + TAPS], ACT.Copy))
                st.done(A(nw[:], PS[7][:, 260 + NE * HC + TAPS:260 + VECS], ACT.Copy))
                st.done(A(expA[:], alog[:], ACT.Exp))
                st.settle()
                st.done(A(WoT[:, 0, :], PS[5][:, 0:P], ACT.Copy, scale=nw[:, 0:1]))
                st.settle()
                A(WoT[:, 1, :], PS[5][:, P:2 * P], ACT.Copy, scale=nw[:, 1:2]).then_inc(s_w1s, 1)

            def experts(layer):
                act.wait_ge(s_gd, layer + 1)
                A(ge[:], gd[:], ACT.Exp).then_inc(s_ge, 1)
                act.wait_ge(s_ids, 2 * layer + 1)
                A(rhs_ids[:, 2, :, :], rhs_ids[:, 0, :, :], ACT.Copy, scale=iota_p[:, 0:1]).then_inc(s_ids_p, 1)
                act.wait_ge(s_te, layer + 1)
                act.wait_ge(s_w1s, 1)
                B0 = layer * SLOT_TILES

                act.wait_ge(s_w, WEIGHTS)

                def weights_of(turn, u):
                    j = turn * LAP + u
                    w = u % TRIO
                    e = act.value_load(te_i[0:1, ds(j, 1)], min_val=0, max_val=NE - 1)
                    if not early(turn, u):
                        act.wait_ge(s_upb, B0 + j - TRIO + 1)
                        act.wait_ge(s_ra, B0 + j - TRIO + 1)
                        act.wait_ge(s_rb, B0 + j - TRIO + 1)
                    A(W1B[w][:], W1S[:, ds(e, 1), :].rearrange("p a h -> p (a h)"), ACT.Copy).then_inc(s_w1, 1)

                def relu(turn, u):
                    j = turn * LAP + u
                    w = u % TRIO
                    act.wait_ge(s_upb, B0 + j + 1)
                    act.wait_ge(s_w1, B0 + j + 1)
                    if not early(turn, u):
                        act.wait_ge(s_y, B0 + j - TRIO + 1)
                    for c in range(2):
                        last = A(H[w][:, 2 + c, :], PS[2 + TRIO + w][:, c * P:(c + 1) * P], ACT.Relu,
                                 bias=W1B[w][:, HID + 2 + c:HID + 3 + c])
                    last.then_inc(s_rb, 1)

                in_steps(act, {2: weights_of, 1: relu})

                act.wait_ge(s_yl[BATCH - 1], 32 * (layer + 1))
                for k, Y in enumerate((Y1, Y2)):
                    for t in range(NT - NC, NT):
                        last = A(Y[:, t, :], Y[:, t, :], ACT.Copy, scale=gate[:, k, t:t + 1])
                        if t < NT - 1:
                            st.done(last)
                    last.then_inc(s_gated, 1)

            def mixer():
                def tap(n, m):
                    k = BLOCKS[m]
                    act.wait_ge(s_proj, n * 6 + (m + 1))
                    if beyond(n, 1):
                        act.wait_ge(s_silu, n * 6 - 6 + (m + 1))
                    A(acc[m][:], PS[m % 2][:], ACT.Identity, bias=cb[:, k:k + 1],
                      scale=cw[:, k, TAPS - 1:TAPS]).then_inc(s_tap, 1)

                def silu(n, m):
                    if m < TAPS:
                        act.wait_ge(s_cv, n * TAPS + (m + 1))
                        if beyond(n, 1):
                            act.wait_ge(s_yp, n * NC)
                        A(conv[BLOCKS[m]][:], acc[m][:], ACT.Silu).then_inc(s_silu, 1)
                    else:
                        act.wait_ge(s_proj, n * 6 + (m + 1))
                        A(gz[:, m - TAPS, ds(n * NC, NC), :].rearrange("p c t -> p (c t)"), PS[m % 2][:], ACT.Silu).then_inc(s_silu, 1)

                def decays(q, u):
                    act.wait_ge(s_seg, q + 1)
                    if beyond(q, 2):
                        act.wait_ge(s_mix, q - 1)
                    A(eseg[u][:].rearrange("p h t -> p (h t)"), PS[5][:], ACT.Exp).then_inc(s_es, 1)

                def copy_out(q):
                    act.wait_ge(s_o, q + 1)
                    A(row(O, q), PS[4][:, 0:D + 1], ACT.Copy).then_inc(s_oc, 1)

                def load_table(function):
                    A(spare[:], ones[:, 0:1], function).then_inc(s_table, 1)

                def batch(b, last_batch=False):
                    first = isinstance(b, int) and b == 0

                    def copy_b(c):
                        act.wait_ge(s_trb, b * (NC - 1) + (c + 1))
                        if c >= 2:
                            act.wait_ge(s_u, b * (NC - 1) + (c - 1))
                        elif not first:
                            act.wait_ge(s_u, b * (NC - 1))
                        A(btok[c % 2][:], PS[4][:, 2 * P:3 * P], ACT.Copy).then_inc(s_bt, 1)

                    def squares(c):
                        q = b * NC + c
                        act.wait_ge(s_y2, q + 1)
                        if not (first and c < 2):
                            act.wait_ge(s_o, q - 1)
                        A(sq[c % 2][:], y2T[:, c, :, :], ACT.Square).then_inc(s_sq, 1)

                    copy_b(0)
                    if first:
                        act.wait_ge(s_dec, 1)
                        A(decay[:].rearrange("p k t h -> p (k t h)"), PS[3][:, 0:3 * NT * HEADS],
                          ACT.Exp).then_inc(s_dece, 1)
                        decays(0, 0)
                        decays(1, 1)
                    for c in range(NC):
                        if c + 1 < NC - 1:
                            copy_b(c + 1)
                        if not last_batch:
                            tap(b + 1, c)
                            if c == 0 and not first:
                                load_table(ACT.Exp)
                        if not (last_batch and c >= NC - 2):
                            decays(b * NC + c + 2, c % 2)
                        if c == NC - 1:
                            if not last_batch:
                                load_table(ACT.Silu)
                                for m in range(TAPS):
                                    silu(b + 1, m)
                        if c and c < NC - 1:
                            squares(c - 1)
                        if not (first and c < 2):
                            copy_out(b * NC + c - 2)
                    if not last_batch:
                        silu(b + 1, TAPS)
                    squares(NC - 2)
                    if not last_batch:
                        silu(b + 1, TAPS + 1)
                    squares(NC - 1)

                norm_project(1, lambda m: tap(0, m))
                act.wait_ge(s_sp, 1)
                A(sp[1][:], sp[0][:], ACT.Exp, scale=-1.0).then_inc(s_spe, 1)
                for m in range(2, TAPS):
                    tap(0, m)
                for m in range(TAPS + 2):
                    silu(0, m)
                load_table(ACT.Exp)
                batch(0)
                with act.Fori(1, BATCH - 1) as b:
                    batch(b)
                batch(BATCH - 1, True)
                copy_out(NT - 2)
                copy_out(NT - 1)

            norm_project(0)
            weights()
            experts(0)
            mixer()
            act.wait_ge(s_weighed, 1)
            for t in range(2 * NC):
                last = A(fin[:, t, :], fin[:, t, :], ACT.Copy, scale=rs[:, t:t + 1])
                if t % NC == NC - 1:
                    last.then_inc(s_scaled, 1)
                else:
                    st.done(last)
            norm_project(2)
            experts(1)

        @block.vector
        def _(dve):
            v = nc.vector
            st = Steps(dve, s_dve)
            side = Steps(dve, s_side)

            def rsqrt(r, val, tmp, besides=None):
                k = 0

                def link(instruction):
                    nonlocal k
                    st.done(instruction)
                    if besides:
                        besides(k)
                        k += 1
                    st.settle()

                link(v.tensor_scalar(r.bitcast(I32), val.bitcast(I32), -0.5, RSQRT_SEED, ALU.mult, ALU.add))
                for _ in range(3):
                    link(v.tensor_tensor(tmp, r, r, ALU.mult))
                    link(v.scalar_tensor_tensor(out=tmp, in0=tmp, scalar=-0.5, in1=val, op0=ALU.mult, op1=ALU.mult))
                    link(v.scalar_tensor_tensor(out=r, in0=tmp, scalar=1.5, in1=r, op0=ALU.add, op1=ALU.mult))

            def in_turn(action, tiles):
                return lambda k: action(tiles[k]) if k < len(tiles) else None

            def statistics(src, t):
                side.done(v.bn_stats(stats[:, t, :], src[:, t, :]))

            def scales(lo, hi, besides=None):
                side.settle()
                for t in range(lo, hi):
                    st.done(v.bn_aggr(mv[:, t, :], stats[:, t, :]))
                st.settle()
                st.link(v.tensor_scalar(rv[:, lo:hi], mv[:, lo:hi, 1], EPS, None, ALU.add))
                rsqrt(rs[:, lo:hi], rv[:, lo:hi], rt[:, lo:hi], besides)

            def norm(n, head, prepare):
                def apply(t):
                    v.tensor_scalar(XN[:, t, :], X[:, t, :], mv[:, t, 0:1], rs[:, t:t + 1],
                                    ALU.subtract, ALU.mult).then_inc(s_xn[0], 1)

                v.scalar_tensor_tensor(out=shift[:, NC:2 * NC], in0=mv[:, NC:2 * NC, 0], scalar=-1.0,
                                       in1=rs[:, NC:2 * NC], op0=ALU.mult, op1=ALU.mult).then_inc(s_rs, 1)
                if n == 1:
                    dve.wait_ge(s_xnd, 16 * BATCH)
                for t in range(NC):
                    apply(t)
                prepare()
                scales(head, NT, in_turn(apply, range(2 * NC, head)))
                for t in range(head, NT):
                    apply(t)

            def parameters():
                dve.wait_ge(s_par, PARAMS)
                dve.wait_ge(s_w1s, 1)
                for c in range(IC):
                    st.done(v.tensor_scalar(diagD[:, c, :], ident[:], Dch[:, c:c + 1], None, ALU.mult))
                st.settle()

            def route(layer):
                for part, (lo, hi) in enumerate(((0, EARLIER), (EARLIER, NT))):
                    dve.wait_ge(s_small, 3 * layer + part + 1)
                    st.link(v.tensor_tensor(lg[:, lo:hi, :],
                                            PS[2 - part][:, lo * NE:hi * NE].rearrange("p (t e) -> p t e", e=NE),
                                            BrS[:].unsqueeze(1).broadcast_to([P, hi - lo, NE]), ALU.add))
                    for t in range(lo, hi):
                        st.done(v.max(top[:, t, :], lg[:, t, :]))
                    st.settle()
                    for t in range(lo, hi):
                        st.done(v.max_index(topi[:, t, :], top[:, t, :], lg[:, t, :]))
                v.tensor_tensor(gd[:], top[:, :, 1], top[:, :, 0], ALU.subtract).then_inc(s_gd, 1)
                st.settle()
                st.link(v.tensor_copy(topf[:], topi[:, :, 0:KTOP]))
                for k in range(KTOP):
                    st.done(v.tensor_tensor(pick[:, k, :, :], iota_e[:].unsqueeze(1).broadcast_to([P, NT, NE]),
                                            topf[:, :, k:k + 1].broadcast_to([P, NT, NE]), ALU.is_equal))
                st.settle()
                v.tensor_tensor(picks_bf[:].rearrange("p (t e) -> p t e", e=NE), pick[:, 0, :, :], pick[:, 1, :, :],
                                ALU.add).then_inc(s_picks, 1)
                dve.wait_ge(s_cnt, layer + 1)
                st.link(v.tensor_copy(cnt[:], PS[4][:, 0:NT * NE].rearrange("p (t e) -> p e t", e=NE)))
                st.link(v.tensor_tensor_scan(run[:].rearrange("p e t -> p (e t)"), ones[:, 0:NT * NE],
                                             cnt[:].rearrange("p e t -> p (e t)"), 0.0, ALU.mult, ALU.add))
                st.link(v.tensor_tensor(excl[:], run[:], cnt[:], ALU.subtract))
                st.link(v.tensor_tensor(n_e[:], run[:, :, NT - 1], excl[:, :, 0], ALU.subtract))
                st.link(v.tensor_tensor(cmp16[:], n_e[:].unsqueeze(2).broadcast_to([P, NE, NT]),
                                        iota_t[:].unsqueeze(1).broadcast_to([P, NE, NT]), ALU.is_gt))
                st.link(v.tensor_reduce(tiles_e[:], cmp16[:], AX.X, ALU.add))
                st.link(v.tensor_tensor_scan(end_e[:], ones[:, 0:NE], tiles_e[:], 0.0, ALU.mult, ALU.add))
                st.link(v.tensor_tensor(adj[:], end_e[:], tiles_e[:], ALU.subtract))
                st.link(v.scalar_tensor_tensor(out=adj[:], in0=adj[:], scalar=float(P), in1=excl[:, :, 0],
                                               op0=ALU.mult, op1=ALU.subtract))
                st.link(v.tensor_tensor(base[:], excl[:], adj[:].unsqueeze(2).broadcast_to([P, NE, NT]), ALU.add))
                st.link(v.tensor_tensor(slot_all[:], PS[3][:, 0:NT * NE].rearrange("p (t e) -> p t e", e=NE),
                                        base[:].rearrange("p e t -> p t e"), ALU.add))
                for k in range(KTOP):
                    st.done(v.tensor_tensor(slot_pick[:, k, :, :], pick[:, k, :, :], slot_all[:], ALU.mult))
                st.settle()
                st.link(v.tensor_reduce(slot[:], slot_pick[:].rearrange("p k t e -> p (k t) e"), AX.X, ALU.add))
                st.link(v.tensor_copy(slot_i[:], slot[:]))
                st.done(v.tensor_scalar(a_i[:], slot_i[:], 7, None, ALU.logical_shift_right))
                st.done(v.tensor_scalar(b_i[:], slot_i[:], P - 1, None, ALU.bitwise_and))
                st.settle()
                st.done(v.tensor_copy(a_bf[:], a_i[:]))
                st.link(v.tensor_copy(b_bf[:], b_i[:]))
                dve.wait_ge(s_iota, 2)
                v.tensor_tensor(rhs_ids[:, 0, :, :], iota_a[:], a_bf[:].unsqueeze(1).broadcast_to([P, SLOT_TILES, NG]),
                                ALU.is_equal).then_inc(s_ids, 1)
                dve.wait_ge(s_ids, 2 * layer + 1)
                v.tensor_tensor(rhs_ids[:, 1, :, :], rhs_ids[:, 0, :, :],
                                group_row[:].unsqueeze(1).broadcast_to([P, SLOT_TILES, NG]), ALU.mult).then_inc(s_ids, 1)
                for k in range(4):
                    part = slice(k * QUARTER, (k + 1) * QUARTER)
                    v.tensor_tensor(onehot_b[:, :, part], iota_b[:, :, part],
                                    b_bf[:, part].unsqueeze(1).broadcast_to([P, P, QUARTER]),
                                    ALU.is_equal).then_inc(s_ob, 1)
                dve.wait_ge(s_idp, layer + 1)
                ids = PS[5][:, 0:3 * SLOT_TILES].rearrange("p (k s) -> p k s", k=3)
                st.link(v.scalar_tensor_tensor(out=ids_f[:], in0=ids[:, 0, :], scalar=1.0, in1=no_pair[:],
                                               op0=ALU.subtract, op1=ALU.mult))
                st.link(v.tensor_tensor(ids_f[:], ids_f[:], ids[:, 1, :], ALU.add))
                st.link(v.tensor_tensor(rows_out[:], ids_f[:], ids[:, 2, :], ALU.add))
                v.tensor_scalar(rows_in[:], rows_out[:], TOK - 1, None, ALU.bitwise_and).then_inc(s_rows, 1)
                st.link(v.tensor_tensor(te_cmp[:], iota_st[:].unsqueeze(2).broadcast_to([P, SLOT_TILES, NE]),
                                        end_e[:].unsqueeze(1).broadcast_to([P, SLOT_TILES, NE]), ALU.is_ge))
                st.link(v.tensor_reduce(te_f[:], te_cmp[:], AX.X, ALU.add))
                v.tensor_scalar(te_i[:], te_f[:], float(NE - 1), None, ALU.min).then_inc(s_te, 1)
                dve.wait_ge(s_ge, layer + 1)
                st.link(v.tensor_scalar(gr[:], ge[:], 2.0, 2.0, ALU.mult, ALU.add))
                st.link(v.reciprocal(gate[:, 0, :], gr[:]))
                st.link(v.tensor_tensor(gate[:, 1, :], gate[:, 0, :], ge[:], ALU.mult))

            def experts(layer):
                B0 = layer * SLOT_TILES
                dve.wait_ge(s_te, layer + 1)

                dve.wait_ge(s_w, WEIGHTS)

                def copy_xt(turn, u):
                    j = turn * LAP + u
                    w = u % TRIO
                    dve.wait_ge(s_xt, B0 + j + 1)
                    if not early(turn, u):
                        dve.wait_ge(s_upb, B0 + j - TRIO + 1)
                    v.tensor_copy(XT[w][:], PS[0][:, 0:P]).then_inc(s_xtc, 1)

                def relu(turn, u):
                    j = turn * LAP + u
                    w = u % TRIO
                    dve.wait_ge(s_upa, B0 + j + 1)
                    dve.wait_ge(s_w1, B0 + j + 1)
                    for c in range(2):
                        last = v.tensor_scalar(H[w][:, c, :], PS[2 + w][:, c * P:(c + 1) * P],
                                               W1B[w][:, HID + c:HID + c + 1], 0.0, ALU.add, ALU.max)
                    last.then_inc(s_ra, 1)

                def add_bias(turn, u):
                    j = turn * LAP + u
                    e = dve.value_load(te_i[0:1, ds(j, 1)], min_val=0, max_val=NE - 1)
                    dve.wait_ge(s_y, B0 + j + 1)
                    if beyond(turn, 1):
                        dve.wait_ge(s_sc[u], 16 * (layer * tiles_of(u) + turn))
                    v.tensor_tensor(YS[u][:], PS[1][:, 0:D], row(B2S, e), ALU.add).then_inc(s_yc, 1)

                in_steps(dve, {2: copy_xt, 1: relu, 0: add_bias})
            def combine(layer, g):
                first_choice(layer, g)
                side.settle()
                for t in range(g * NC, (g + 1) * NC):
                    last = add_choice(1, Y2, t)
                last.then_inc(s_comb, 1)

            def add_choice(k, Y, t):
                return v.scalar_tensor_tensor(out=X[:, t, :], in0=Y[:, t, :], scalar=gate[:, k, t:t + 1],
                                              in1=X[:, t, :], op0=ALU.mult, op1=ALU.add)

            def first_choice(layer, g):
                dve.wait_ge(s_yl[g], 32 * (layer + 1))
                for t in range(g * NC, (g + 1) * NC):
                    side.done(add_choice(0, Y1, t))

            def time_steps(besides):
                def link(instruction):
                    st.done(instruction)
                    besides()
                    st.settle()

                dve.wait_ge(s_small, 3)
                st.link(v.tensor_tensor(dtr[:], PS[2][:, 0:NT * HEADS].rearrange("p (t h) -> p t h", h=HEADS),
                                        dtb[:].unsqueeze(1).broadcast_to([P, NT, HEADS]), ALU.add))
                v.scalar_tensor_tensor(out=sp[0][:], in0=dtr[:], scalar=-1.0, in1=dtr[:], op0=ALU.mult,
                                       op1=ALU.max).then_inc(s_sp, 1)
                dve.wait_ge(s_spe, 1)
                e, z, z2, p = sp[1][:], sp[2][:], sp[3][:], sp[4][:]
                st.link(v.tensor_scalar(z2, e, 2.0, None, ALU.add))
                st.link(v.reciprocal(z, z2))
                st.link(v.tensor_tensor(z, z, e, ALU.mult))
                st.link(v.tensor_tensor(z2, z, z, ALU.mult))
                st.link(v.tensor_scalar(p, z2, 1.0 / 17, None, ALU.mult))
                for k in (15, 13, 11, 9, 7, 5, 3):
                    link(v.scalar_tensor_tensor(out=p, in0=p, scalar=1.0 / k, in1=z2, op0=ALU.add, op1=ALU.mult))
                st.link(v.scalar_tensor_tensor(out=p, in0=p, scalar=1.0, in1=z, op0=ALU.add, op1=ALU.mult))
                st.link(v.tensor_scalar(z, dtr[:], 0.0, None, ALU.max))
                st.link(v.scalar_tensor_tensor(out=dt[:], in0=p, scalar=2.0, in1=z, op0=ALU.mult, op1=ALU.add))
                dve.wait_ge(s_w1s, 1)
                st.link(v.tensor_tensor(la[:], dt[:], expA[:].unsqueeze(1).broadcast_to([P, NT, HEADS]), ALU.mult))
                v.tensor_scalar(la[:], la[:], -1.0, LEAST_DECAY, ALU.mult, ALU.max).then_inc(s_la, 1)
                dve.wait_ge(s_dece, 1)
                st.link(v.tensor_tensor(dtd[:], dt[:], decay[:, 1, :, :], ALU.mult))

            def mean_square(lo, hi):
                dve.wait_ge(s_oc, hi)
                st.link(v.tensor_scalar(rv[:, lo:hi], O[:, lo:hi, D], 1.0 / INNER, EPS, ALU.mult, ALU.add))

            def rms(lo, hi, besides=None):
                mean_square(lo, hi)
                rsqrt(rs[:, lo:hi], rv[:, lo:hi], rt[:, lo:hi], besides)

            def residual(lo, hi):
                for t in range(lo, hi):
                    side.done(v.scalar_tensor_tensor(out=res[:, t, :], in0=O[:, t, 0:D], scalar=rs[:, t:t + 1],
                                                     in1=XN[:, t, :], op0=ALU.mult, op1=ALU.add))

            def weigh(t):
                side.done(v.scalar_tensor_tensor(out=fin[:, t, :], in0=res[:, t, :], scalar=mv[:, t, 0:1], in1=lnw[:],
                                                 op0=ALU.subtract, op1=ALU.mult))

            def add_normed(t):
                side.done(v.scalar_tensor_tensor(out=X[:, t, :], in0=fin[:, t, :], scalar=rs[:, t:t + 1], in1=X[:, t, :],
                                                 op0=ALU.mult, op1=ALU.add))

            def finish_earlier(c):
                if c == 0:
                    rms(0, EARLIER - NC)
                elif c == 1:
                    residual(0, EARLIER - NC)
                elif c == 2:
                    side.settle()
                    rms(EARLIER - NC, EARLIER, in_turn(lambda t: statistics(res, t), range(EARLIER - NC)))
                    residual(EARLIER - NC, EARLIER)
                else:
                    side.settle()
                    for t in range(EARLIER - NC, EARLIER):
                        statistics(res, t)

            def finish():
                side.settle()
                for t in range(EARLIER):
                    st.done(v.bn_aggr(mv[:, t, :], stats[:, t, :]))
                st.settle()
                st.done(v.tensor_scalar(rv[:, 0:EARLIER], mv[:, 0:EARLIER, 1], EPS, None, ALU.add))
                for t in range(4):
                    weigh(t)
                mean_square(EARLIER, NT)
                rsqrt(rs[:], rv[:], rt[:], in_turn(weigh, range(4, EARLIER)))
                side.settle()
                dve.sem_inc(s_weighed, 1)
                residual(EARLIER, NT)
                dve.wait_ge(s_lnb, BATCH)
                for t in range(2 * NC, EARLIER):
                    add_normed(t)
                side.settle()
                for t in range(2 * NC, NT):
                    statistics(res if t >= EARLIER else X, t)
                for g in range(2):
                    dve.wait_ge(s_added, g + 1)
                    for t in range(g * NC, (g + 1) * NC):
                        statistics(X, t)
                side.settle()
                dve.sem_inc(s_near, 1)
                for t in range(NT):
                    st.done(v.bn_aggr(mv[:, t, :], stats[:, t, :]))
                st.settle()
                st.link(v.tensor_scalar(rv[:], mv[:, :, 1], EPS, None, ALU.add))
                rsqrt(rs[:], rv[:], rt[:], in_turn(weigh, range(EARLIER, NT)))

            def finish_last():
                side.settle()
                for t in range(EARLIER, NT):
                    add_normed(t)
                side.settle()
                for t in range(EARLIER, NT):
                    statistics(X, t)

            def mixer():
                def by_head(tensor, q):
                    return row(tensor, q).unsqueeze(2).broadcast_to([P, HEADS, HD])

                def tap(n, m, j):
                    back = TAPS - 1 - j
                    if j == 0:
                        dve.wait_ge(s_tap, n * TAPS + (m + 1))
                    else:
                        side.settle()
                    last = v.scalar_tensor_tensor(out=acc[m][:, back:SEQ], in0=PS[m % 2][:, 0:SEQ - back],
                                                  scalar=cw[:, BLOCKS[m], j:j + 1], in1=acc[m][:, back:SEQ],
                                                  op0=ALU.mult, op1=ALU.add)
                    if j < TAPS - 2:
                        side.done(last)
                    else:
                        last.then_inc(s_cv, 1)

                def taps(n, m):
                    for j in range(TAPS - 1):
                        tap(n, m, j)

                def batch(b, last_batch=False):
                    first = isinstance(b, int) and b == 0

                    def d1(c):
                        q = b * NC + c
                        u = c % 2
                        dve.wait_ge(s_tr, q + 1)
                        if not (first and c < 2):
                            dve.wait_ge(s_mix, q - 1)
                        v.tensor_tensor(gm[u][:], PS[2 + u][:, INNER:INNER + P], upto[:], ALU.mult).then_inc(s_gmm, 1)
                        if not (first and c < 2):
                            dve.wait_ge(s_yp, q - 1)
                        v.tensor_tensor(heads(xdt[u][:]), heads(PS[2 + u][:, 0:INNER]), by_head(dt, q),
                                        ALU.mult).then_inc(s_xd, 1)
                        if c < NC - 1:
                            if c >= 2:
                                dve.wait_ge(s_u, b * (NC - 1) + (c - 1))
                            elif not first:
                                dve.wait_ge(s_u, b * (NC - 1))
                            v.tensor_tensor(heads(xend[u][:]), heads(PS[2 + u][:, 0:INNER]), by_head(dtd, q),
                                            ALU.mult).then_inc(s_xe, 1)

                    def d2(c, between):
                        q = b * NC + c
                        u = c % 2
                        between(0)
                        dve.wait_ge(s_yp, q + 1)
                        if c:
                            st.done(v.tensor_tensor(heads(yi[:]), heads(PS[6][:, INNER:2 * INNER]), by_chunk(0, q),
                                                    ALU.mult))
                        between(1)
                        if c < NC - 1:
                            dve.wait_ge(s_u, b * (NC - 1) + (c + 1))
                            if c:
                                dve.wait_ge(s_kept, b * (NC - 2) + c)
                                v.tensor_tensor(S[:], S_kept[:], PS[7][:, INNER:2 * INNER], ALU.add).then_inc(s_S, 1)
                            else:
                                v.tensor_copy(S[:], PS[7][:, INNER:2 * INNER]).then_inc(s_S, 1)
                        if not (first and c < 2):
                            dve.wait_ge(s_yT, q - 1)
                        if c:
                            st.settle()
                            v.tensor_tensor(yt[u][:], yi[:], PS[6][:, 0:INNER], ALU.add).then_inc(s_yt, 1)
                        else:
                            v.tensor_copy(yt[u][:], PS[6][:, 0:INNER]).then_inc(s_yt, 1)
                        between(2)

                    def d3(c):
                        q = b * NC + c
                        dve.wait_ge(s_yT, q + 1)
                        if c == 0:
                            dve.wait_ge(s_silu, (b + 1) * 6)
                        if not first:
                            dve.wait_ge(s_o, q - NC + 1)
                        v.tensor_tensor(y2T[:, c, :, :], PS[7][:, 0:INNER].rearrange("p (i t) -> p i t", i=IC),
                                        gz[:, :, ds(q, 1), :].rearrange("p i a t -> p i (a t)"), ALU.mult).then_inc(s_y2, 1)

                    d1(0)
                    for c in range(NC):
                        if c + 1 < NC:
                            d1(c + 1)
                        if c == NC - 1 and not last_batch:
                            taps(b + 1, c)
                        d2(c, (lambda k: None) if last_batch or c == NC - 1 else (lambda k: tap(b + 1, c, k)))
                        if c and c < NC - 1:
                            d3(c - 1)
                        if last_batch:
                            finish_earlier(c)
                    d3(NC - 2)
                    d3(NC - 1)

                for m in range(2):
                    taps(0, m)
                rest = [(m, j) for m in (2, 3) for j in range(TAPS - 1)]
                time_steps(lambda: tap(0, *rest.pop(0)) if rest else None)
                assert not rest
                before, before_side = st.n, side.n
                batch(0)
                steps, side_steps = st.n - before, side.n - before_side
                with dve.Fori(1, BATCH - 1) as b:
                    st.enter(b - 1, steps)
                    side.enter(b - 1, side_steps)
                    batch(b)
                    st.leave(BATCH - 2)
                    side.leave(BATCH - 2)
                batch(BATCH - 1, True)

            def on_arrival(t):
                if t % NC == 0:
                    dve.wait_ge(s_x[t // NC], 16)
                statistics(X, t)

            def first_choice_of_2(k):
                if k == 0:
                    dve.wait_ge(s_yl[2], 32)
                if k < NC:
                    side.done(add_choice(0, Y1, 2 * NC + k))

            def second_half_of_x():
                side.settle()
                for t in range(2 * NC, 3 * NC):
                    st.done(add_choice(1, Y2, t))
                st.settle()
                dve.wait_ge(s_comb_pool, 1)
                for t in range(2 * NC, NT):
                    statistics(X, t)

            for t in range(EARLIER):
                on_arrival(t)
            scales(0, EARLIER, in_turn(on_arrival, range(EARLIER, NT)))
            norm(0, EARLIER, lambda: None)
            dve.wait_ge(s_wr, WR)
            dve.wait_ge(s_const, N_CONST)
            route(0)
            experts(0)
            parameters()
            combine(0, 0)
            combine(0, 1)
            dve.wait_ge(s_comb, 2)
            dve.sem_inc(s_near, 1)
            for t in range(2 * NC):
                statistics(X, t)
            scales(0, 2 * NC, first_choice_of_2)
            norm(1, 2 * NC, second_half_of_x)
            mixer()
            finish()
            norm(2, EARLIER, finish_last)
            route(1)
            experts(1)
            for g in range(BATCH - 1):
                combine(1, g)


_INS = ["L0_attn_x", "L0_attn_in_proj_w", "L0_attn_conv_w", "L0_attn_conv_b", "L0_attn_dt_bias", "L0_attn_A_log",
        "L0_attn_D", "L0_attn_norm_w", "L0_attn_out_proj_w", "L0_attn_ln_w", "L0_attn_ln_b", "L0_ffn_Wr", "L0_ffn_br",
        "L0_ffn_W1", "L0_ffn_b1", "L0_ffn_W2", "L0_ffn_b2"]


def kernel(**inputs):
    import numpy as _np
    import concourse.bacc as _bacc
    from concourse import mybir as _mybir
    from concourse.bass_utils import run_bass_kernel_spmd as _run

    nc = _bacc.Bacc("TRN2", target_bir_lowering=False, num_devices=1)
    arrays, args = {}, []
    for name in _INS:
        a = _np.ascontiguousarray(inputs[name])
        arrays[f"in_{name}"] = a
        args.append(nc.dram_tensor(f"in_{name}", a.shape, _mybir.dt.from_np(a.dtype), kind="ExternalInput").ap())
    out = nc.dram_tensor("out_x", (BATCH, SEQ, D), F32, kind="ExternalOutput").ap()
    macaron_block(nc, *args, out)
    r = _run(nc, [arrays], core_ids=[0])
    return r.results[0]["out_x"]
```
